# Optimizing a Trainium2 kernel written in Bass

```python
import numpy as np
import jax
import jax.numpy as jnp

def _softmax(x, axis=-1):
    return jax.nn.softmax(x, axis=axis)

def _gelu(x):
    return jax.nn.gelu(x, approximate=True)

def _silu(x):
    return jax.nn.silu(x)

def _sigmoid(x):
    return jax.nn.sigmoid(x)

def _layernorm(x, axis=-1, eps=1e-05):
    m = jnp.mean(x, axis=axis, keepdims=True)
    v = jnp.var(x, axis=axis, keepdims=True)
    return (x - m) / jnp.sqrt(v + eps)

def _scatter_add(tgt, idx, src, axis=0):
    return tgt.at[idx].add(src)

def _segment_sum(src, seg, n):
    return jax.ops.segment_sum(src, seg, n)
kernel_name = 'mk_sandwich_d1_jaxref_r4_6f7050'

def setup_inputs(seed: int=0):
    np.random.seed(seed)
    _w = jnp.asarray

    def _L0_attn_setup():
        import math
        import jax, jax.numpy as jnp
        import numpy as np
        D_MODEL = 256
        N_HEAD = 16
        HEAD_DIM = D_MODEL // N_HEAD
        T = 1.0
        EPS = 1e-05

        def _layernorm(t, gamma, beta):
            m = t.mean(axis=-1, keepdims=True)
            var = ((t - m) ** 2).mean(axis=-1, keepdims=True)
            return (t - m) * jax.lax.rsqrt(var + EPS) * gamma + beta
        key = jax.random.key(seed)
        k1, k2, k3 = jax.random.split(key, 3)
        B, S = (4, 512)
        scale = 1.0 / math.sqrt(D_MODEL)
        return {'x': jax.random.normal(k1, (B, S, D_MODEL), dtype=jnp.float32), 'w_qkv': jax.random.normal(k2, (D_MODEL, 3 * D_MODEL), dtype=jnp.float32) * scale, 'w_proj': jax.random.normal(k3, (D_MODEL, D_MODEL), dtype=jnp.float32) * scale, 'q_gamma': jnp.ones((HEAD_DIM,), dtype=jnp.float32), 'q_beta': jnp.zeros((HEAD_DIM,), dtype=jnp.float32), 'k_gamma': jnp.ones((HEAD_DIM,), dtype=jnp.float32), 'k_beta': jnp.zeros((HEAD_DIM,), dtype=jnp.float32)}
    _L0_attn_in = _L0_attn_setup()

    def _L0_ffn_setup():
        import jax, jax.numpy as jnp
        import numpy as np
        D, H, E, K, S = (256, 512, 8, 2, 1)
        B, L = (4, 512)
        key = jax.random.key(seed)
        ks = jax.random.split(key, 9)
        std = 0.02
        return {'x': jax.random.normal(ks[0], (B, L, D), dtype=jnp.float32), 'router_w': jax.random.normal(ks[1], (E, D), dtype=jnp.float32) * std, 'experts_bias': jnp.zeros((E,), dtype=jnp.float32), 'w1': jax.random.normal(ks[2], (E, D, H), dtype=jnp.float32) * std, 'w3': jax.random.normal(ks[3], (E, D, H), dtype=jnp.float32) * std, 'w2': jax.random.normal(ks[4], (E, H, D), dtype=jnp.float32) * std, 'sw1': jax.random.normal(ks[5], (S, D, H), dtype=jnp.float32) * std, 'sw3': jax.random.normal(ks[6], (S, D, H), dtype=jnp.float32) * std, 'sw2': jax.random.normal(ks[7], (S, H, D), dtype=jnp.float32) * std}
    _L0_ffn_in = _L0_ffn_setup()
    _d = {'L0_attn_x': _L0_attn_in['x'], 'L0_attn_w_qkv': _L0_attn_in['w_qkv'], 'L0_attn_w_proj': _L0_attn_in['w_proj'], 'L0_attn_q_gamma': _L0_attn_in['q_gamma'], 'L0_attn_q_beta': _L0_attn_in['q_beta'], 'L0_attn_k_gamma': _L0_attn_in['k_gamma'], 'L0_attn_k_beta': _L0_attn_in['k_beta'], 'L0_ffn_router_w': _L0_ffn_in['router_w'], 'L0_ffn_experts_bias': _L0_ffn_in['experts_bias'], 'L0_ffn_w1': _L0_ffn_in['w1'], 'L0_ffn_w3': _L0_ffn_in['w3'], 'L0_ffn_w2': _L0_ffn_in['w2'], 'L0_ffn_sw1': _L0_ffn_in['sw1'], 'L0_ffn_sw3': _L0_ffn_in['sw3'], 'L0_ffn_sw2': _L0_ffn_in['sw2']}
    _x0 = _d['L0_attn_x']
    _d['L0_attn_x'] = jax.random.normal(jax.random.fold_in(jax.random.key(seed), 1), (2, 2048, 256), dtype=_x0.dtype)
    del _x0
    return _d

def reference(L0_attn_x, L0_attn_w_qkv, L0_attn_w_proj, L0_attn_q_gamma, L0_attn_q_beta, L0_attn_k_gamma, L0_attn_k_beta, L0_ffn_router_w, L0_ffn_experts_bias, L0_ffn_w1, L0_ffn_w3, L0_ffn_w2, L0_ffn_sw1, L0_ffn_sw3, L0_ffn_sw2):

    def _L0_attn_ref(x, w_qkv, w_proj, q_gamma, q_beta, k_gamma, k_beta):
        import math
        import jax, jax.numpy as jnp
        import numpy as np
        D_MODEL = 256
        N_HEAD = 16
        HEAD_DIM = D_MODEL // N_HEAD
        T = 1.0
        EPS = 1e-05

        def _layernorm(t, gamma, beta):
            m = t.mean(axis=-1, keepdims=True)
            var = ((t - m) ** 2).mean(axis=-1, keepdims=True)
            return (t - m) * jax.lax.rsqrt(var + EPS) * gamma + beta
        B, S, C = x.shape
        H, Dh = (N_HEAD, HEAD_DIM)
        qkv = (x @ w_qkv).reshape(B, S, 3, H, Dh)
        qkv = jnp.transpose(qkv, (2, 0, 3, 1, 4))
        q, k, v = (qkv[0], qkv[1], qkv[2])
        q = _layernorm(q, q_gamma, q_beta)
        k = _layernorm(k, k_gamma, k_beta)
        logits = jnp.einsum('bhsd,bhtd->bhst', q, k) / (math.sqrt(Dh) * T)
        att = jax.nn.softmax(logits, axis=-1)
        out = jnp.einsum('bhst,bhtd->bhsd', att, v)
        out = jnp.transpose(out, (0, 2, 1, 3)).reshape(B, S, C)
        return out @ w_proj

    def _L0_ffn_ref(x, router_w, experts_bias, w1, w3, w2, sw1, sw3, sw2):
        import jax, jax.numpy as jnp
        import numpy as np
        D, H, E, K, S = (256, 512, 8, 2, 1)
        B, L = (4, 512)
        b, l, d = x.shape
        xf = x.reshape(-1, d)
        sg = jnp.einsum('td,sdh->tsh', xf, sw1)
        su = jnp.einsum('td,sdh->tsh', xf, sw3)
        shared_out = jnp.einsum('tsh,shd->td', jax.nn.silu(sg) * su, sw2)
        logits = xf @ router_w.T + experts_bias
        rw, sel = jax.lax.top_k(logits, K)
        rw = jax.nn.softmax(rw.astype(jnp.float32), axis=-1).astype(x.dtype)
        cw = (jax.nn.one_hot(sel, E, dtype=x.dtype) * rw[..., None]).sum(axis=1)
        g = jnp.einsum('td,edh->teh', xf, w1)
        u = jnp.einsum('td,edh->teh', xf, w3)
        eo = jax.nn.silu(g) * u
        moe_out = jnp.einsum('te,teh,ehd->td', cw, eo, w2)
        return (moe_out + shared_out).reshape(b, l, d)
    x = L0_attn_x
    x = x + _layernorm(_L0_attn_ref(_layernorm(x, axis=-1), L0_attn_w_qkv, L0_attn_w_proj, L0_attn_q_gamma, L0_attn_q_beta, L0_attn_k_gamma, L0_attn_k_beta), axis=-1)
    x = x + _layernorm(_L0_ffn_ref(_layernorm(x, axis=-1), L0_ffn_router_w, L0_ffn_experts_bias, L0_ffn_w1, L0_ffn_w3, L0_ffn_w2, L0_ffn_sw1, L0_ffn_sw3, L0_ffn_sw2), axis=-1)
    return x

_drawn_inputs = setup_inputs


def setup_inputs(seed=0):
    import zlib

    import numpy as np

    out = dict(_drawn_inputs(seed))
    spreads = {'L0_attn_q_gamma': (1.0, 0.2),
     'L0_attn_q_beta': (0.0, 0.1),
     'L0_attn_k_gamma': (1.0, 0.2),
     'L0_attn_k_beta': (0.0, 0.1),
     'L0_ffn_experts_bias': (0.0, 0.1)}
    factors = {}
    for name, (base, spread) in spreads.items():
        noise = np.random.default_rng([zlib.crc32(name.encode()), seed]).standard_normal(out[name].shape)
        drawn = base * np.exp(spread * noise) if base else spread * noise
        out[name] = jnp.asarray(drawn.astype(out[name].dtype))
    for name, factor in factors.items():
        out[name] = (out[name] * factor).astype(out[name].dtype)
    return out
```

```python
from contextlib import ExitStack

import concourse.bass as bass
from concourse import mybir

F32 = mybir.dt.float32
BF16 = mybir.dt.bfloat16
F16 = mybir.dt.float16
I32 = mybir.dt.int32
U32 = mybir.dt.uint32
ALU = mybir.AluOpType
ACT = mybir.ActivationFunctionType
AX = mybir.AxisListType
RMAX = bass.bass_isa.ReduceOp.max

P = 128
B, S, D = 2, 2048, 256
H, DH = 16, 16
E, HID = 8, 512
EPS = 1e-5
T = B * S
TILES = T // P
KD = D // P
G = 4
GT = G * P
GROUPS = TILES // G
GPB = GROUPS // B
QR = 3 * DH
KR = 2 * DH
PAIR = 6 * DH
SROWS = 3
CROWS = PAIR + SROWS
VW = 64
VU = DH + 1
KSCALE = 2.0 ** 12
TOP = 15 * 0.6931471805599453
SAFE = 11.0


def wait(eng, sem, value):
    if isinstance(value, int) and value <= 0:
        return
    eng.wait_ge(sem, value)


def pipelined(eng, rounds, steps, stages, peel=1):
    def step(r, s):
        for lag, stage in stages:
            if s >= lag:
                stage(r, s - lag)
            elif not isinstance(r, int) or r > 0:
                stage(r - 1, s - lag + steps)
    for r in range(peel):
        for s in range(steps):
            step(r, s)
    with eng.Fori(peel, rounds) as r:
        for s in range(steps):
            step(r, s)
    for s in range(max(lag for lag, _ in stages)):
        for lag, stage in stages:
            if s < lag:
                stage(rounds - 1, s - lag + steps)


class Link:

    def __init__(self, eng, sem, per_step=0):
        self.eng, self.sem, self.per_step, self.base, self.n = eng, sem, per_step, 0, 0

    def start(self, step):
        assert self.n in (0, self.per_step), self.n
        self.base, self.n = step * self.per_step, 0

    def __call__(self, ins):
        self.n += 1
        ins.then_inc(self.sem, 1)
        self.eng.wait_ge(self.sem, self.base + self.n)


def settle(v, tick):
    v.memset(tick[:], 0.0)


def rstd_newton(link, v, var, root, out, tmp, ready_sem, ready_value):
    v.wait_ge(ready_sem, ready_value)
    link(v.reciprocal(out, root))
    link(v.tensor_tensor(tmp, out, out, ALU.mult))
    link(v.tensor_tensor(tmp, tmp, var, ALU.mult))
    link(v.tensor_scalar(tmp, tmp, -0.5, 1.5, ALU.mult, ALU.add))
    link(v.tensor_tensor(out, out, tmp, ALU.mult))


def setup(nc, dr, sb):
    with ExitStack() as ctx:
        def sem(name):
            return ctx.enter_context(nc.semaphore(name))
        gb = ctx.enter_context(nc.sbuf_tensor("gb", [P, 4, DH], F32))
        wmean = ctx.enter_context(nc.sbuf_tensor("wmean", [P, KD, 2 * H], F32))
        t0 = ctx.enter_context(nc.sbuf_tensor("t0", [P, 2, DH], F32))
        a = ctx.enter_context(nc.sbuf_tensor("a", [P, 4], F32))
        x_loaded = sem("x_loaded")
        w_loaded = sem("w_loaded")
        gb_loaded = sem("gb_loaded")
        zeroed = sem("zeroed")
        ident_made = sem("ident_made")
        setup_link = sem("setup_link")
        block = ctx.enter_context(nc.Block())

        @block.sync
        def _(sp):
            sp.dma_start(sb["wqkv"][:], dr["w_qkv"].rearrange("(k p) n -> p k n", p=P)).then_inc(w_loaded, 16)
            for i, name in enumerate(("q_gamma", "q_beta", "k_gamma", "k_beta")):
                sp.dma_start(gb[:, i, :], dr[name].partition_broadcast(P)).then_inc(gb_loaded, 16)
            for b in range(B):
                sp.dma_start(sb["x"][:, b * (TILES // B):(b + 1) * (TILES // B), :],
                             dr["x"][b].rearrange("(t p) d -> p t d", p=P)).then_inc(x_loaded, 16)
            sp.dma_start(sb["wproj"][:], dr["w_proj"].rearrange("(k p) n -> p k n", p=P)).then_inc(w_loaded, 16)
            sp.dma_start(sb["rw"][:], dr["router_w"]).then_inc(w_loaded, 16)
            sp.dma_start(sb["rbias"][:], dr["experts_bias"].partition_broadcast(P)).then_inc(w_loaded, 16)
            sp.wait_ge(x_loaded, 16 * B)
            sp.wait_ge(w_loaded, 16 * 4)

        @block.gpsimd
        def _(pool):
            pool.memset(sb["ident"][:], 0.0).then_inc(zeroed, 1)
            pool.memset(sb["sel"][:], 0.0).then_inc(zeroed, 1)
            pool.iota(sb["iota8"][:], pattern=[[1, E]], base=0, channel_multiplier=0,
                      allow_small_or_imprecise_dtypes=True).then_inc(ident_made, 1)
            pool.wait_ge(zeroed, 2)
            pool.affine_select(out=sb["ident"][:], in_=sb["ident"][:], compare_op=ALU.not_equal, fill=1.0,
                               base=0, pattern=[[-1, P]], channel_multiplier=1).then_inc(ident_made, 1)
            n = 2
            for j in range(2):
                cols = sb["sel"][:, VU * j:VU * j + DH]
                for i in range(3):
                    pool.wait_ge(ident_made, n)
                    pool.affine_select(out=cols, in_=cols, compare_op=ALU.not_equal, fill=1.0,
                                       base=-(VW * j + DH * i), pattern=[[-1, DH]],
                                       channel_multiplier=1).then_inc(ident_made, 1)
                    n += 1
                one = sb["sel"][:, VU * j + DH:VU * j + VU]
                pool.affine_select(out=one, in_=one, compare_op=ALU.not_equal, fill=1.0,
                                   base=-(VW * j + 3 * DH), pattern=[[-1, 1]],
                                   channel_multiplier=1).then_inc(ident_made, 1)
                n += 1

        @block.vector
        def _(v):
            link = Link(v, setup_link)
            v.wait_ge(ident_made, 2)
            v.tensor_copy(sb["ident_b"][:], sb["ident"][:])
            v.tensor_copy(sb["ident_h"][:], sb["ident"][:])
            v.wait_ge(w_loaded, 64)
            w = sb["wqkv"][:, :, 0:2 * D].rearrange("p k (h d) -> p k h d", d=DH)
            link(v.tensor_reduce(wmean[:], w, AX.X, ALU.add))
            link(v.tensor_scalar(wmean[:], wmean[:], 1.0 / DH, None, ALU.mult))
            for k in range(KD):
                link(v.tensor_tensor(w[:, k], w[:, k], wmean[:, k].unsqueeze(2).to_broadcast([P, 2 * H, DH]),
                                     ALU.subtract))
            v.wait_ge(gb_loaded, 64)
            link(v.scalar_tensor_tensor(t0[:], gb[:, 2:4, :], -1.0, gb[:, 2:4, :], ALU.mult, ALU.max))
            link(v.scalar_tensor_tensor(t0[:, 0], t0[:, 0], 4.0, t0[:, 1], ALU.mult, ALU.add))
            link(v.tensor_reduce(a[:, 0:1], t0[:, 0], AX.X, ALU.max))
            link(v.tensor_scalar(a[:, 0:1], a[:, 0:1], 1e-30, None, ALU.max))
            link(v.tensor_scalar(a[:, 1:2].bitcast(I32), a[:, 0:1].bitcast(I32), 0x7F800000, None,
                                 ALU.bitwise_and))
            link(v.reciprocal(a[:, 2:3], a[:, 1:2]))
            link(v.tensor_scalar(a[:, 2:3], a[:, 2:3], KSCALE, None, ALU.mult))
            link(v.tensor_scalar(a[:, 3:4], a[:, 1:2], 1.0 / (KSCALE * DH ** 0.5), None, ALU.mult))
            for i in range(4):
                out = sb["gain" if i % 2 == 0 else "bias"][:, (i // 2) * D:(i // 2 + 1) * D]
                scale = a[:, 3:4] if i < 2 else a[:, 2:3]
                link(v.tensor_scalar(out.rearrange("p (h d) -> p h d", d=DH),
                                     gb[:, i, :].unsqueeze(1).to_broadcast([P, H, DH]), scale, None, ALU.mult))


def project_qkv(nc, dr, sb):
    with ExitStack() as ctx:
        def sem(name):
            return ctx.enter_context(nc.semaphore(name))

        def sbuf(name, shape, dt):
            return ctx.enter_context(nc.sbuf_tensor(name, shape, dt))

        bn = sbuf("bn", [P, G, 6], F32)
        mv = sbuf("mv", [P, G, 2], F32)
        ve = sbuf("ve", [P, 2, G], F32)
        root = sbuf("root", [P, 2, G], F32)
        rs = sbuf("rs", [P, G], F32)
        tm = sbuf("tm", [P, G], F32)
        xn = sbuf("xn", [P, 2, G, D], F32)
        xnT = sbuf("xnT", [P, 2, KD, GT], F32)
        C = sbuf("C", [P, 2, G, 2 * D], F32)
        sq = sbuf("sq", [P, 2, G, 2 * D], F32)
        V32 = sbuf("V32", [P, 2, G, D], F32)
        NH = G * 2 * H
        hv = sbuf("hv", [P, 2, NH], F32)
        hroot = sbuf("hroot", [P, 2, NH], F32)
        hr = sbuf("hr", [P, NH], F32)
        ht = sbuf("ht", [P, NH], F32)
        hn = sbuf("hn", [P, NH], F32)
        rest = sbuf("rest", [P, G, D], F32)
        vrest = sbuf("vrest", [P, G, D], F32)
        TQ = sbuf("TQ", [P, G, H * QR], BF16)
        TK = sbuf("TK", [P, G, H * KR], F16)
        VT = sbuf("VT", [P, H, G, VW], BF16)
        NQ, NK = H * QR // P, H * KR // P
        qkT = sbuf("qkT", [P, NQ + NK, GT], BF16)
        norms = sbuf("norms", [P, GROUPS, 2], F32)
        ksum = sbuf("ksum", [P, GROUPS, NK], F32)
        stat = sbuf("stat", [P, 4], F32)
        allst = sbuf("allst", [P, 4], F32)
        fin = sbuf("fin", [P, 8], F32)
        shift = sbuf("shift", [B * H, SROWS, S], BF16)
        QP = [ctx.enter_context(nc.psum_tensor(f"QP{i}", [P, 1024], F32)) for i in range(2)]
        XP = [ctx.enter_context(nc.psum_tensor(f"XP{i}", [P, 2, KD, P], F32)) for i in range(2)]
        TP = [ctx.enter_context(nc.psum_tensor(f"TP{i}", [P, GT], BF16)) for i in range(2)]

        var_ready = sem("var_ready")
        root_ready = sem("root_ready")
        xn_ready = sem("xn_ready")
        xT_psum = sem("xT_psum")
        xT_ready = sem("xT_ready")
        qkv_psum = sem("qkv_psum")
        qkv_out = sem("qkv_out")
        head_var = sem("head_var")
        head_root = sem("head_root")
        heads_ready = sem("heads_ready")
        squares = sem("squares")
        sq_used = sem("sq_used")
        v1_ready = sem("v1_ready")
        vrest_ready = sem("vrest_ready")
        v2_ready = sem("v2_ready")
        v_ready = sem("v_ready")
        qk_ready = sem("qk_ready")
        part_psum = sem("part_psum")
        part_out = sem("part_out")
        stored = sem("stored")
        v_stored = sem("v_stored")
        vt_init = sem("vt_init")
        norms_ready = sem("norms_ready")
        reduced = sem("reduced")
        roots2 = sem("roots2")
        shift_ready = sem("shift_ready")
        shift_stored = sem("shift_stored")
        dve_link = sem("dve_link")
        rs_ready = sem("rs_ready")
        ROUNDS, STEPS = GROUPS // 2, 2
        NT = NQ + NK

        qt = dr["QT"].rearrange("r (g n) -> r g n", n=GT)
        kt = dr["KT"].rearrange("r (g n) -> r g n", n=GT)
        vd = dr["VD"]
        block = ctx.enter_context(nc.Block())

        @block.tensor
        def _(pe):
            def turn_x(r, s):
                g = r * STEPS + s
                pe.wait_ge(xn_ready, g + 1)
                for h in range(2):
                    wait(pe, xT_ready, 2 * g + h - 1)
                    for t in range(2):
                        for k in range(KD):
                            ins = pe.transpose(XP[h][:, t, k, :], xn[:, s, 2 * h + t, k * P:(k + 1) * P],
                                               sb["ident"][:])
                    ins.then_inc(xT_psum, 1)

            def qkv(r, s):
                g = r * STEPS + s
                pe.wait_ge(xT_ready, 2 * g + 2)
                for j in range(G):
                    wait(pe, qkv_out, G * g + j - 1)
                    for c0, c1 in ((0, 512), (512, 768)):
                        for k in range(KD):
                            ins = pe.matmul(QP[j % 2][:, c0:c1], xnT[:, s, k, j * P:(j + 1) * P],
                                            sb["wqkv"][:, k, c0:c1], start=(k == 0), stop=(k == KD - 1))
                    ins.then_inc(qkv_psum, 1)

            def turn_parts(r, s):
                g = r * STEPS + s
                pe.wait_ge(qk_ready, g + 1)
                for m in range(NT):
                    wait(pe, part_out, NT * g + max(m - 1, 0))
                    for j in range(G):
                        if m < NQ:
                            ins = pe.transpose(TP[m % 2][:, j * P:(j + 1) * P], TQ[:, j, m * P:(m + 1) * P],
                                               sb["ident_b"][:])
                        else:
                            ins = pe.transpose(TP[m % 2][:, j * P:(j + 1) * P].bitcast(F16),
                                               TK[:, j, (m - NQ) * P:(m - NQ + 1) * P], sb["ident_h"][:])
                    ins.then_inc(part_psum, 1)

            pipelined(pe, ROUNDS, STEPS, [(0, turn_x), (1, qkv), (2, turn_parts)], peel=2)

        @block.scalar
        def _(act):
            def norm_x(r, s):
                g = r * STEPS + s
                act.wait_ge(var_ready, g + 1)
                nc.scalar.activation(root[:, s], ve[:, s], ACT.Sqrt).then_inc(root_ready, 1)
                for h in range(2):
                    act.wait_ge(xT_psum, 2 * g + h + 1)
                    wait(act, qkv_psum, G * (g - 1))
                    nc.scalar.activation(
                        xnT[:, s, :, 2 * h * P:2 * (h + 1) * P].rearrange("p k (t n) -> p t k n", n=P),
                        XP[h][:], ACT.Copy).then_inc(xT_ready, 1)

            def take_qkv(r, s):
                g = r * STEPS + s
                wait(act, qk_ready, g - 1)
                wait(act, v_ready, g - 1)
                for j in range(G):
                    act.wait_ge(qkv_psum, G * g + j + 1)
                    nc.scalar.activation(C[:, s, j], QP[j % 2][:, 0:512], ACT.Copy)
                    nc.scalar.activation(sq[:, s, j], QP[j % 2][:, 0:512], ACT.Square)
                    nc.scalar.activation(V32[:, s, j], QP[j % 2][:, 512:768], ACT.Copy).then_inc(qkv_out, 1)

            def head_root_of(r, s):
                g = r * STEPS + s
                act.wait_ge(head_var, g + 1)
                nc.scalar.activation(hroot[:, s], hv[:, s], ACT.Sqrt).then_inc(head_root, 1)

            def split(r, s):
                g = r * STEPS + s
                vt = VT[:].rearrange("p h g w -> p g h w")
                v4 = V32[:, s].rearrange("p g (h d) -> p g h d", d=DH)
                act.wait_ge(qkv_out, G * g + G)
                act.wait_ge(vt_init, 2)
                wait(act, v_stored, 16 * g)
                for j in range(G):
                    ins = nc.scalar.activation(vt[:, j, :, 0:DH], v4[:, j], ACT.Copy)
                ins.then_inc(v1_ready, 1)
                act.wait_ge(vrest_ready, g + 1)
                r4 = vrest[:].rearrange("p g (h d) -> p g h d", d=DH)
                for j in range(G):
                    ins = nc.scalar.activation(vt[:, j, :, DH:2 * DH], r4[:, j], ACT.Copy)
                ins.then_inc(v2_ready, 1)
                act.wait_ge(heads_ready, g + 1)
                nc.scalar.activation(sq[:, s], C[:, s], ACT.Square).then_inc(squares, 1)

            def take_parts(r, s):
                g = r * STEPS + s
                wait(act, stored, 32 * g)
                for m in range(NT):
                    act.wait_ge(part_psum, NT * g + m + 1)
                    if m < NQ:
                        ins = nc.scalar.activation(qkT[:, m], TP[m % 2][:], ACT.Copy)
                    else:
                        ins = nc.scalar.activation(qkT[:, m].bitcast(F16), TP[m % 2][:].bitcast(F16), ACT.Copy,
                                                   accum_out=ksum[:, g, m - NQ:m - NQ + 1])
                    ins.then_inc(part_out, 1)

            pipelined(act, ROUNDS, STEPS, [(0, norm_x), (2, head_root_of), (1, take_qkv), (2, split),
                                           (2, take_parts)], peel=2)
            act.wait_ge(reduced, 1)
            nc.scalar.activation(fin[:, 0:2], allst[:, 0:2], ACT.Sqrt).then_inc(roots2, 1)

        @block.vector
        def _(v):
            link = Link(v, dve_link, 0)
            v.memset(VT[:], 0.0).then_inc(vt_init, 1)
            v.wait_ge(vt_init, 1)
            v.memset(VT[:, :, :, 3 * DH:3 * DH + 1], 1.0).then_inc(vt_init, 1)

            xlink = Link(v, sem("x_link"), 2 + 4)
            hlink = Link(v, sem("h_link"), 16)

            def norm_x(r, s):
                g = r * STEPS + s
                xlink.start(g)
                settle(v, sb["tick"])
                x4 = sb["x"][:].rearrange("p (g t) d -> p g t d", t=G)
                for t in range(G):
                    ins = v.bn_stats(bn[:, t, :], x4[:, g, t, :])
                xlink(ins)
                settle(v, sb["tick"])
                for t in range(G):
                    ins = v.bn_aggr(mv[:, t, :], bn[:, t, :])
                xlink(ins)
                v.tensor_scalar(ve[:, s], mv[:, :, 1], EPS, None, ALU.add).then_inc(var_ready, 1)
                v.wait_ge(var_ready, g + 1)
                v.wait_ge(root_ready, g + 1)
                xlink(v.reciprocal(rs[:], root[:, s]))
                xlink(v.tensor_tensor(tm[:], rs[:], rs[:], ALU.mult))
                xlink(v.tensor_tensor(tm[:], tm[:], ve[:, s], ALU.mult))
                xlink(v.tensor_scalar(tm[:], tm[:], -0.5, 1.5, ALU.mult, ALU.add))
                v.tensor_tensor(rs[:], rs[:], tm[:], ALU.mult).then_inc(rs_ready, 1)
                v.wait_ge(rs_ready, g + 1)
                wait(v, xT_psum, 2 * (g - 1))
                for t in range(G):
                    ins = v.tensor_scalar(xn[:, s, t, :], x4[:, g, t, :], mv[:, t, 0:1], rs[:, t:t + 1],
                                          ALU.subtract, ALU.mult)
                ins.then_inc(xn_ready, 1)

            def heads(r, s):
                g = r * STEPS + s
                hlink.start(g)
                v.wait_ge(qkv_out, G * g + G)
                c3 = C[:, s].rearrange("p g (h d) -> p (g h) d", d=DH)
                s3 = sq[:, s].rearrange("p g (h d) -> p (g h) d", d=DH)
                hlink(v.tensor_reduce(hv[:, s], s3, AX.X, ALU.add))
                v.tensor_scalar(hv[:, s], hv[:, s], 1.0 / DH, EPS, ALU.mult, ALU.add).then_inc(head_var, 1)
                vt = VT[:].rearrange("p h g w -> p g h w")
                v4 = V32[:, s].rearrange("p g (h d) -> p g h d", d=DH)
                r4 = vrest[:].rearrange("p g (h d) -> p g h d", d=DH)
                v.wait_ge(v1_ready, g + 1)
                for j in range(G):
                    ins = v.tensor_tensor(r4[:, j], v4[:, j], vt[:, j, :, 0:DH], ALU.subtract)
                ins.then_inc(vrest_ready, 1)
                v.wait_ge(head_var, g + 1)
                v.wait_ge(head_root, g + 1)
                hlink(v.reciprocal(hr[:], hroot[:, s]))
                hlink(v.tensor_tensor(ht[:], hr[:], hr[:], ALU.mult))
                hlink(v.tensor_tensor(ht[:], ht[:], hv[:, s], ALU.mult))
                hlink(v.tensor_scalar(ht[:], ht[:], -0.5, 1.5, ALU.mult, ALU.add))
                hlink(v.tensor_tensor(hr[:], hr[:], ht[:], ALU.mult))
                hlink(v.tensor_tensor(c3, c3, hr[:].unsqueeze(2).to_broadcast([P, NH, DH]), ALU.mult))
                gain = sb["gain"][:].unsqueeze(1).to_broadcast([P, G, 2 * D])
                bias = sb["bias"][:].unsqueeze(1).to_broadcast([P, G, 2 * D])
                hlink(v.tensor_tensor(C[:, s], C[:, s], gain, ALU.mult))
                v.tensor_tensor(C[:, s], C[:, s], bias, ALU.add).then_inc(heads_ready, 1)
                v.wait_ge(v2_ready, g + 1)
                for j in range(G):
                    ins = v.tensor_tensor(vt[:, j, :, 2 * DH:3 * DH], r4[:, j], vt[:, j, :, DH:2 * DH],
                                          ALU.subtract)
                ins.then_inc(v_ready, 1)
                v.wait_ge(heads_ready, g + 1)
                wait(v, part_psum, NT * g)
                q = C[:, s, :, 0:D].rearrange("p g (h d) -> p g h d", d=DH)
                k = C[:, s, :, D:2 * D].rearrange("p g (h d) -> p g h d", d=DH)
                tq = TQ[:].rearrange("p g (h i d) -> p g h i d", i=3, d=DH)
                tk = TK[:].rearrange("p g (h i d) -> p g h i d", i=2, d=DH)
                rr = rest[:].rearrange("p g (h d) -> p g h d", d=DH)

                def each(fn):
                    for j in range(G):
                        ins = fn(j)
                    return ins
                hlink(each(lambda j: v.tensor_copy(tq[:, j, :, 0], q[:, j])))
                hlink(each(lambda j: v.tensor_tensor(rr[:, j], q[:, j], tq[:, j, :, 0], ALU.subtract)))
                hlink(each(lambda j: v.tensor_copy(tq[:, j, :, 1], rr[:, j])))
                hlink(each(lambda j: v.tensor_tensor(tq[:, j, :, 2], rr[:, j], tq[:, j, :, 1], ALU.subtract)))
                hlink(each(lambda j: v.tensor_copy(tk[:, j, :, 0], k[:, j])))
                v.wait_ge(squares, g + 1)
                hlink(v.tensor_reduce(hn[:], s3, AX.X, ALU.add))
                hnv = hn[:].rearrange("p (g i h) -> p i g h", g=G, i=2)
                hlink(v.tensor_reduce(norms[:, g, 0:1], hnv[:, 0], AX.XY, ALU.max))
                hlink(v.tensor_reduce(norms[:, g, 1:2], hnv[:, 1], AX.XY, ALU.max))
                each(lambda j: v.tensor_tensor(tk[:, j, :, 1], k[:, j], tk[:, j, :, 0],
                                               ALU.subtract)).then_inc(qk_ready, 1)

            pipelined(v, ROUNDS, STEPS, [(0, norm_x), (2, heads)], peel=2)

            v.wait_ge(part_out, NT * GROUPS)
            v.memset(stat[:], 0.0).then_inc(norms_ready, 1)
            v.wait_ge(norms_ready, 1)
            link(v.tensor_reduce(stat[:, 0:2], norms[:].rearrange("p g i -> p i g"), AX.X, ALU.max))
            kb = ksum[:].rearrange("p (b g) m -> p b m g", b=B)
            link(v.tensor_reduce(ht[:, 0:B * NK].rearrange("p (b m) -> p b m", b=B), kb, AX.X, ALU.add))
            v.tensor_reduce(stat[:, 2:3], ht[:, 0:B * NK], AX.X, ALU.max,
                            apply_absolute_value=True).then_inc(norms_ready, 1)
            v.wait_ge(roots2, 1)
            link(v.tensor_tensor(fin[:, 2:3], fin[:, 0:1], fin[:, 1:2], ALU.mult))
            link(v.tensor_scalar(fin[:, 3:4], allst[:, 2:3], 4.01 / S, None, ALU.mult))
            link(v.tensor_tensor(fin[:, 3:4], fin[:, 3:4], fin[:, 0:1], ALU.mult))
            link(v.tensor_tensor(fin[:, 4:5], fin[:, 2:3], fin[:, 3:4], ALU.add))
            link(v.tensor_scalar(sb["guard"][:], fin[:, 4:5], 1.001, None, ALU.mult))
            link(v.tensor_scalar(fin[:, 5:6], fin[:, 2:3], -1.001, TOP, ALU.mult, ALU.add))
            link(v.memset(shift[:], 0.0))
            v.tensor_scalar(shift[:, 0, :], shift[:, 0, :], fin[0:B * H, 5:6], None,
                            ALU.add).then_inc(shift_ready, 1)

        @block.gpsimd
        def _(pool):
            pool.wait_ge(norms_ready, 2)
            pool.partition_all_reduce(allst[:], stat[:], P, RMAX).then_inc(reduced, 1)

        @block.sync
        def _(sp):
            def store(r, s):
                g = r * STEPS + s
                sp.wait_ge(v_ready, g + 1)
                sp.dma_start(vd[:, :, g, :], VT[:].rearrange("p h g w -> p h (g w)")).then_inc(v_stored, 16)
                sp.wait_ge(part_out, NT * g + NT)
                sp.dma_start(qt[:, g, :].rearrange("(m p) n -> p m n", p=P),
                             qkT[:, 0:NQ]).then_inc(stored, 16)
                sp.dma_start(kt[:, g, :].rearrange("(m p) n -> p m n", p=P),
                             qkT[:, NQ:NT].bitcast(F16)).then_inc(stored, 16)
            pipelined(sp, ROUNDS, STEPS, [(0, store)])
            sp.wait_ge(shift_ready, 1)
            sp.dma_start(dr["SH"].rearrange("i b n -> b i n"), shift[:]).then_inc(shift_stored, 16)
            sp.wait_ge(shift_stored, 16)
            sp.wait_ge(v_stored, 16 * GROUPS)
            sp.wait_ge(stored, 32 * GROUPS)


def true_maxima(nc, dr, sb):
    BH = B * H
    QTILES = S // P
    with ExitStack() as ctx:
        def sem(name):
            return ctx.enter_context(nc.semaphore(name))

        def sbuf(name, shape, dt):
            return ctx.enter_context(nc.sbuf_tensor(name, shape, dt))
        Q = sbuf("mQ", [PAIR, S], BF16)
        K = sbuf("mK", [PAIR, S], F16)
        top = sbuf("top", [P, BH, QTILES], F32)
        part = sbuf("part", [P, SROWS, BH * QTILES], BF16)
        turned = sbuf("mturned", [P, P], BF16)
        scores = ctx.enter_context(nc.psum_tensor("mscores", [P, S], F32))
        TM = ctx.enter_context(nc.psum_tensor("TM", [P, P], BF16))
        m_loaded = sem("m_loaded")
        m_scores = sem("m_scores")
        m_max = sem("m_max")
        m_link = sem("m_link")
        m_parts = sem("m_parts")
        m_turned = sem("m_turned")
        m_copied = sem("m_copied")
        m_stored = sem("m_stored")
        block = ctx.enter_context(nc.Block())

        @block.sync
        def _(sp):
            def load(bh):
                wait(sp, m_scores, bh * QTILES)
                load_head(sp, dr, bh, Q, K, m_loaded)
            load(0)
            with sp.Fori(1, BH) as bh:
                load(bh)
            for i in range(SROWS):
                for c in range(BH * QTILES // P):
                    sp.wait_ge(m_copied, i * (BH * QTILES // P) + c + 1)
                    rows = dr["SH"][i].rearrange("b (q n) -> (b q) n", n=P)
                    sp.dma_start(rows[c * P:(c + 1) * P, :], turned[:]).then_inc(m_stored, 16)
                    sp.wait_ge(m_stored, 16 * (i * (BH * QTILES // P) + c + 1))

        @block.tensor
        def _(pe):
            def head(bh):
                pe.wait_ge(m_loaded, LOADS * 16 * (bh + 1))
                for q in range(QTILES):
                    wait(pe, m_max, bh * QTILES + q)
                    for c in range(S // 512):
                        ins = pe.matmul(scores[:, c * 512:(c + 1) * 512], Q[:, q * P:(q + 1) * P],
                                        K[:, c * 512:(c + 1) * 512], start=True, stop=True)
                    ins.then_inc(m_scores, 1)
            head(0)
            with pe.Fori(1, BH) as bh:
                head(bh)
            pe.wait_ge(m_parts, 1)
            n = 0
            for i in range(SROWS):
                for c in range(BH * QTILES // P):
                    wait(pe, m_copied, n)
                    pe.transpose(TM[:], part[:, i, c * P:(c + 1) * P], sb["ident_b"][:]).then_inc(m_turned, 1)
                    n += 1

        @block.scalar
        def _(act):
            act.nop()

        @block.gpsimd
        def _(pool):
            pool.nop()

        @block.vector
        def _(v):
            with v.Fori(0, BH) as bh:
                for q in range(QTILES):
                    v.wait_ge(m_scores, bh * QTILES + q + 1)
                    v.tensor_reduce(top[:, bh, q:q + 1], scores[:], AX.X, ALU.max).then_inc(m_max, 1)
            v.wait_ge(m_max, BH * QTILES)
            link = Link(v, m_link)
            t = top[:].rearrange("p b q -> p (b q)")
            link(v.tensor_scalar(t, t, -1.0, TOP, ALU.mult, ALU.add))
            link(v.tensor_copy(part[:, 0], t))
            link(v.tensor_tensor(t, t, part[:, 0], ALU.subtract))
            link(v.tensor_copy(part[:, 1], t))
            v.tensor_tensor(part[:, 2], t, part[:, 1], ALU.subtract).then_inc(m_parts, 1)
            n = 0
            for i in range(SROWS):
                for c in range(BH * QTILES // P):
                    v.wait_ge(m_turned, n + 1)
                    wait(v, m_stored, 16 * n)
                    v.tensor_copy(turned[:], TM[:]).then_inc(m_copied, 1)
                    n += 1


LOADS = 8


def load_head(sp, dr, bh, Q, K, loaded):
    b, h = bh // H, bh % H
    qv = dr["QT"].rearrange("(h r) (b n) -> h b r n", r=QR, n=S)
    kv = dr["KT"].rearrange("(h r) (b n) -> h b r n", r=KR, n=S)
    for i in range(2):
        sp.dma_start(Q[i * QR:(i + 1) * QR, :], qv[h, b]).then_inc(loaded, 16)
    for i in range(2):
        for j in range(3):
            sp.dma_start(K[i * QR + j * DH:i * QR + (j + 1) * DH, :],
                         kv[h, b, i * DH:(i + 1) * DH]).then_inc(loaded, 16)


NP = 4
NB = 4
NL = 2
KT = S // P
STEPS = 2 * 2 * KT
LAG = 3
QC = 512
HI_ACT = [s for s in range(STEPS) if s % 2 == 1]
HI_DVE = [s for s in range(STEPS) if s not in HI_ACT]


def attention(nc, dr, sb):
    with ExitStack() as ctx:
        def sem(name):
            return ctx.enter_context(nc.semaphore(name))

        def sbuf(name, shape, dt):
            return ctx.enter_context(nc.sbuf_tensor(name, shape, dt))
        Q = [sbuf(f"Q{i}", [CROWS, S], BF16) for i in range(2)]
        K = [sbuf(f"K{i}", [CROWS, S], F16) for i in range(2)]
        V = [sbuf(f"V{i}", [P, KT, VW], BF16) for i in range(2)]
        pr = [sbuf(f"pr{i}", [P, 2 * QC], F32) for i in range(NP)]
        hi = [sbuf(f"hi{i}", [P, 2 * QC], F16) for i in range(NB)]
        lo = [sbuf(f"lo{i}", [P, 2 * QC], F16) for i in range(NB)]
        acc_sb = [sbuf(f"acc_sb{i}", [P, QC], F32) for i in range(2)]
        sc = [ctx.enter_context(nc.psum_tensor(f"sc{i}", [P, 2 * QC], F32)) for i in range(NL)]
        acc = [ctx.enter_context(nc.psum_tensor(f"acc{i}", [P, QC], F32)) for i in range(2)]
        turned = ctx.enter_context(nc.psum_tensor("turned", [P, QC // P, 2 * VU], F32))
        loaded = [sem(f"loaded{i}") for i in range(2)]
        ones = sem("ones")
        scores_ready = sem("scores_ready")
        exp_done = sem("exp_done")
        hi_act = sem("hi_act")
        hi_dve = sem("hi_dve")
        lo_done = sem("lo_done")
        pv_done = sem("pv_done")
        acc_out = sem("acc_out")
        turned_ready = sem("turned_ready")
        out_done = sem("out_done")
        ROUNDS = B * H // 2
        GS = KT
        GR = STEPS // GS
        block = ctx.enter_context(nc.Block())

        def hi_ready(eng, r, s):
            mine = HI_ACT if s in HI_ACT else HI_DVE
            eng.wait_ge(hi_act if s in HI_ACT else hi_dve, r * len(mine) + mine.index(s) + 1)

        @block.sync
        def _(sp):
            def load(r, s):
                wait(sp, pv_done, r * STEPS + (s - 1) * (STEPS // 2))
                bh = 2 * r + s
                load_head(sp, dr, bh, Q[s], K[s], loaded[s])
                sp.dma_start(Q[s][PAIR:CROWS, :], dr["SH"][:, bh, :]).then_inc(loaded[s], 16)
                b, h = bh // H, bh % H
                sp.dma_start(V[s][:].rearrange("p k w -> p (k w)"),
                             dr["VD"].rearrange("p h (b g) w -> p b h (g w)", b=B)[:, b, h]).then_inc(loaded[s], 16)
            pipelined(sp, ROUNDS, 2, [(0, load)])

        @block.tensor
        def _(pe):
            pe.wait_ge(ones, 2)

            def scores(r, s):
                n = r * STEPS + s
                head, k, c = s // (STEPS // 2), s % KT, s // KT % 2
                if s % (STEPS // 2) == 0:
                    pe.wait_ge(loaded[head], 16 * (LOADS + 2) * (r + 1))
                wait(pe, exp_done, n - NL + 1)
                for j in range(2):
                    ins = pe.matmul(sc[s % NL][:, j * QC:(j + 1) * QC], K[head][:, k * P:(k + 1) * P],
                                    Q[head][:, (2 * c + j) * QC:(2 * c + j + 1) * QC], start=True, stop=True)
                ins.then_inc(scores_ready, 1)

            def values(r, s):
                n = r * STEPS + s
                head, k = s // (STEPS // 2), s % KT
                if k == 0:
                    wait(pe, acc_out, r * GR + s // GS - 1)
                hi_ready(pe, r, s)
                for part, ready in ((hi, False), (lo, True)):
                    if ready:
                        pe.wait_ge(lo_done, n + 1)
                    for j in range(2):
                        ins = pe.matmul(acc[s // GS % 2][j * VW:(j + 1) * VW, :], V[head][:, k, :],
                                        part[s % NB][:, j * QC:(j + 1) * QC],
                                        start=(k == 0 and not ready), stop=(k == KT - 1 and ready))
                ins.then_inc(pv_done, 1)

            def turn(r, s):
                if s % GS != GS - 1:
                    return
                g = r * GR + s // GS
                pe.wait_ge(acc_out, g + 1)
                wait(pe, out_done, g)
                for q in range(QC // P):
                    ins = pe.matmul(turned[:, q, :], acc_sb[s // GS % 2][:, q * P:(q + 1) * P], sb["sel"][:],
                                    start=True, stop=True)
                ins.then_inc(turned_ready, 1)

            pipelined(pe, ROUNDS, STEPS, [(0, scores), (LAG, values), (LAG + 3, turn)])

        @block.scalar
        def _(act):
            def exponentials(r, s):
                n = r * STEPS + s
                act.wait_ge(scores_ready, n + 1)
                wait(act, lo_done, n - NP + 1)
                nc.scalar.activation(pr[s % NP][:], sc[s % NL][:], ACT.Exp).then_inc(exp_done, 1)

            def high(r, s):
                if s not in HI_ACT:
                    return
                n = r * STEPS + s
                act.wait_ge(exp_done, n + 1)
                wait(act, pv_done, n - NB + 1)
                nc.scalar.activation(hi[s % NB][:], pr[s % NP][:], ACT.Copy).then_inc(hi_act, 1)

            def take(r, s):
                if s % GS != GS - 1:
                    return
                g = r * GR + s // GS
                act.wait_ge(pv_done, r * STEPS + s + 1)
                wait(act, turned_ready, g - 1)
                nc.scalar.activation(acc_sb[s // GS % 2][:], acc[s // GS % 2][:], ACT.Copy).then_inc(acc_out, 1)

            pipelined(act, ROUNDS, STEPS, [(0, exponentials), (0, high), (LAG + 1, take)])

        @block.vector
        def _(v):
            for i in range(2):
                v.memset(K[i][PAIR:CROWS, :], 1.0).then_inc(ones, 1)
            out = sb["O"][:].rearrange("p (r g) j q d -> p r g j q d", r=ROUNDS)

            def low(r, s):
                n = r * STEPS + s
                v.wait_ge(exp_done, n + 1)
                wait(v, pv_done, n - NB + 1)
                if s in HI_DVE:
                    v.tensor_copy(hi[s % NB][:], pr[s % NP][:]).then_inc(hi_dve, 1)
                hi_ready(v, r, s)
                v.tensor_tensor(lo[s % NB][:], pr[s % NP][:], hi[s % NB][:],
                                ALU.subtract).then_inc(lo_done, 1)

            def keep(r, s):
                if s % GS != GS - 1:
                    return
                g = r * GR + s // GS
                v.wait_ge(turned_ready, g + 1)
                v.tensor_copy(out[:, r, s // GS].rearrange("p j q d -> p q j d"),
                              turned[:].rearrange("p q (j d) -> p q j d", j=2)).then_inc(out_done, 1)

            pipelined(v, ROUNDS, STEPS, [(0, low), (LAG + 4, keep)])


def project_and_route(nc, dr, sb):
    with ExitStack() as ctx:
        def sem(name):
            return ctx.enter_context(nc.semaphore(name))

        def sbuf(name, shape, dt):
            return ctx.enter_context(nc.sbuf_tensor(name, shape, dt))
        den = sbuf("den", [P, G, H], F32)
        att = sbuf("att", [P, 2, G, D], F32)
        attT = sbuf("attT", [P, 2, KD, GT], F32)
        y = sbuf("y", [P, G, D], F32)
        bn = sbuf("bn3", [P, G, 6], F32)
        mv = sbuf("mv3", [P, G, 2], F32)
        ve = sbuf("ve3", [P, 2, 2, G], F32)
        root = sbuf("root3", [P, 2, 2, G], F32)
        rs = sbuf("rs3", [P, G], F32)
        tm = sbuf("tm3", [P, G], F32)
        xn = sbuf("xn3", [P, 2, G, D], F32)
        z = sbuf("z", [P, TILES, E], F32)
        best = sbuf("best", [P, TILES, 8], F32)
        bidx = sbuf("bidx", [P, TILES, 8], U32)
        bidf = sbuf("bidf", [P, TILES, 2], F32)
        wt = sbuf("wt", [P, TILES, 2], F32)
        gap = sbuf("gap", [P, TILES], F32)
        hot = sbuf("hot", [P, TILES, E], F32)
        TPa = [ctx.enter_context(nc.psum_tensor(f"TPa{i}", [P, 2, KD, P], F32)) for i in range(2)]
        Y = ctx.enter_context(nc.psum_tensor("Y", [P, G, D], F32))
        TX = [ctx.enter_context(nc.psum_tensor(f"TX{i}", [P, 2, KD, P], F32)) for i in range(2)]
        Z = ctx.enter_context(nc.psum_tensor("Z", [P, G, E], F32))
        att_ready = sem("att_ready")
        aT_psum = sem("aT_psum")
        aT_ready = sem("aT_ready")
        y_psum = sem("y_psum")
        y_out = sem("y_out")
        var3 = sem("var3")
        root3 = sem("root3s")
        xn3 = sem("xn3s")
        xT3_psum = sem("xT3_psum")
        xT3 = sem("xT3")
        z_psum = sem("z_psum")
        z_out = sem("z_out")
        rs_done = sem("rs_done")
        x1_done = sem("x1_done")
        l3 = sem("l3")
        l3b = sem("l3b")
        l3c = sem("l3c")
        gap_ready = sem("gap_ready")
        gap_exp = sem("gap_exp")
        rw_turned = sem("rw_turned")
        rw_ready = sem("rw_ready")
        ROUNDS, STEPS3 = GROUPS // 2, 2
        block = ctx.enter_context(nc.Block())

        @block.tensor
        def _(pe):
            def turn_att(r, s):
                g = r * STEPS3 + s
                pe.wait_ge(att_ready, g + 1)
                for h in range(2):
                    wait(pe, aT_ready, 2 * g + h - 1)
                    for t in range(2):
                        for k in range(KD):
                            ins = pe.transpose(TPa[h][:, t, k, :], att[:, s, 2 * h + t, k * P:(k + 1) * P],
                                               sb["ident"][:])
                    ins.then_inc(aT_psum, 1)

            def project(r, s):
                g = r * STEPS3 + s
                pe.wait_ge(aT_ready, 2 * g + 2)
                wait(pe, y_out, g)
                for j in range(G):
                    for k in range(KD):
                        ins = pe.matmul(Y[:, j, :], attT[:, s, k, j * P:(j + 1) * P], sb["wproj"][:, k, :],
                                        start=(k == 0), stop=(k == KD - 1))
                ins.then_inc(y_psum, 1)

            def turn_xn(r, s):
                g = r * STEPS3 + s
                pe.wait_ge(xn3, g + 1)
                for h in range(2):
                    wait(pe, xT3, 2 * g + h - 1)
                    for t in range(2):
                        for k in range(KD):
                            ins = pe.transpose(TX[h][:, t, k, :], xn[:, s, 2 * h + t, k * P:(k + 1) * P],
                                               sb["ident"][:])
                    ins.then_inc(xT3_psum, 1)

            def route(r, s):
                g = r * STEPS3 + s
                pe.wait_ge(xT3, 2 * g + 2)
                wait(pe, z_out, g)
                for j in range(G):
                    for k in range(KD):
                        ins = pe.matmul(Z[:, j, :], attT[:, s, k, j * P:(j + 1) * P], sb["rwT"][:, k, :],
                                        start=(k == 0), stop=(k == KD - 1))
                ins.then_inc(z_psum, 1)

            for k in range(KD):
                ins = pe.transpose(Z[:, k, :], sb["rw"][:, k * P:(k + 1) * P], sb["ident"][0:E, 0:E])
            ins.then_inc(rw_turned, 1)
            pe.wait_ge(rw_ready, 1)
            pipelined(pe, ROUNDS, STEPS3, [(0, turn_att), (0, project), (1, turn_xn), (1, route)], peel=2)

        @block.scalar
        def _(act):
            def evac(r, s):
                g = r * STEPS3 + s
                wait(act, z_psum, g - 1)
                for h in range(2):
                    act.wait_ge(aT_psum, 2 * g + h + 1)
                    nc.scalar.activation(
                        attT[:, s, :, 2 * h * P:2 * (h + 1) * P].rearrange("p k (t n) -> p t k n", n=P),
                        TPa[h][:], ACT.Copy).then_inc(aT_ready, 1)

            def roots(i):
                def stage(r, s):
                    g = r * STEPS3 + s
                    act.wait_ge(var3, 2 * g + i + 1)
                    nc.scalar.activation(root[:, s, i], ve[:, s, i], ACT.Sqrt).then_inc(root3, 1)
                return stage

            def evac_xn(r, s):
                g = r * STEPS3 + s
                act.wait_ge(y_psum, g + 1)
                for h in range(2):
                    act.wait_ge(xT3_psum, 2 * g + h + 1)
                    tok = 2 * h * P
                    nc.scalar.activation(
                        attT[:, s, :, tok:tok + 2 * P].rearrange("p k (t n) -> p t k n", n=P),
                        TX[h][:], ACT.Copy)
                    x2 = sb["xT"][:].rearrange("p k (g h t n) -> p g h t k n", h=2, t=2, n=P)
                    nc.scalar.activation(x2[:, g, h], TX[h][:], ACT.Copy).then_inc(xT3, 1)

            pipelined(act, ROUNDS, STEPS3, [(0, evac), (1, roots(0)), (1, roots(1)), (1, evac_xn)], peel=2)
            act.wait_ge(gap_ready, 1)
            nc.scalar.activation(gap[:], gap[:], ACT.Exp).then_inc(gap_exp, 1)

        @block.vector
        def _(v):
            v.wait_ge(rw_turned, 1)
            v.tensor_copy(sb["rwT"][:], Z[:, 0:KD, :]).then_inc(rw_ready, 1)
            dl = Link(v, l3, 1)
            nl = Link(v, l3b, 14)
            x4 = sb["x"][:].rearrange("p (g t) d -> p g t d", t=G)
            o4 = sb["O"][:].rearrange("p (b h c) j q d -> p b c j q h d", b=B, h=H)

            def divide(r, s):
                g = r * STEPS3 + s
                dl.start(g)
                b = r // 2
                o = o4[:, b, r % 2, s]
                wait(v, att_ready, g)
                dl(v.reciprocal(den[:], o[:, :, :, DH]))
                wait(v, aT_psum, 2 * (g - 1))
                a4 = att[:, s].rearrange("p q (h d) -> p q h d", d=DH)
                for q in range(G):
                    ins = v.tensor_tensor(a4[:, q], o[:, q, :, 0:DH], den[:, q].unsqueeze(2).to_broadcast([P, H, DH]),
                                          ALU.mult)
                ins.then_inc(att_ready, 1)

            def norm_stats(src, g, s, i):
                settle(v, sb["tick"])
                for t in range(G):
                    ins = v.bn_stats(bn[:, t, :], src(t))
                nl(ins)
                settle(v, sb["tick"])
                for t in range(G):
                    ins = v.bn_aggr(mv[:, t, :], bn[:, t, :])
                nl(ins)
                v.tensor_scalar(ve[:, s, i], mv[:, :, 1], EPS, None, ALU.add).then_inc(var3, 1)
                v.wait_ge(var3, 2 * g + i + 1)
                rstd_newton(nl, v, ve[:, s, i], root[:, s, i], rs[:], tm[:], root3, 2 * g + i + 1)

            def residual(r, s):
                g = r * STEPS3 + s
                nl.start(g)
                v.wait_ge(y_psum, g + 1)
                norm_stats(lambda t: Y[:, t, :], g, s, 0)
                for t in range(G):
                    ins = v.tensor_scalar(y[:, t, :], Y[:, t, :], mv[:, t, 0:1], rs[:, t:t + 1],
                                          ALU.subtract, ALU.mult)
                ins.then_inc(y_out, 1)
                v.wait_ge(y_out, g + 1)
                v.tensor_tensor(x4[:, g], x4[:, g], y[:], ALU.add).then_inc(x1_done, 1)
                v.wait_ge(x1_done, g + 1)
                norm_stats(lambda t: x4[:, g, t, :], g, s, 1)
                wait(v, xT3_psum, 2 * (g - 1))
                for t in range(G):
                    ins = v.tensor_scalar(xn[:, s, t, :], x4[:, g, t, :], mv[:, t, 0:1], rs[:, t:t + 1],
                                          ALU.subtract, ALU.mult)
                ins.then_inc(xn3, 1)

            def keep_z(r, s):
                g = r * STEPS3 + s
                v.wait_ge(z_psum, g + 1)
                z4 = z[:].rearrange("p (g t) e -> p g t e", t=G)
                v.tensor_tensor(z4[:, g], Z[:], sb["rbias"][:].unsqueeze(1).to_broadcast([P, G, E]),
                                ALU.add).then_inc(z_out, 1)

            pipelined(v, ROUNDS, STEPS3, [(0, divide), (1, residual), (2, keep_z)], peel=2)

            link = Link(v, l3c)
            v.wait_ge(z_out, GROUPS)
            for t in range(TILES):
                ins = v.max(best[:, t, :], z[:, t, :])
            link(ins)
            for t in range(TILES):
                ins = v.max_index(bidx[:, t, :], best[:, t, :], z[:, t, :])
            link(ins)
            v.tensor_tensor(gap[:], best[:, :, 1], best[:, :, 0], ALU.subtract).then_inc(gap_ready, 1)
            link(v.tensor_copy(bidf[:], bidx[:, :, 0:2]))
            v.wait_ge(gap_exp, 1)
            link(v.tensor_scalar(wt[:, :, 0], gap[:], 1.0, None, ALU.add))
            link(v.reciprocal(wt[:, :, 0], wt[:, :, 0]))
            link(v.tensor_tensor(wt[:, :, 1], wt[:, :, 0], gap[:], ALU.mult))
            iota = sb["iota8"][:].unsqueeze(1).to_broadcast([P, TILES, E])

            def spread(a):
                return a.unsqueeze(2).to_broadcast([P, TILES, E])
            link(v.tensor_tensor(hot[:], iota, spread(bidf[:, :, 0]), ALU.is_equal))
            link(v.tensor_tensor(sb["cw"][:], hot[:], spread(wt[:, :, 0]), ALU.mult))
            link(v.tensor_tensor(hot[:], iota, spread(bidf[:, :, 1]), ALU.is_equal))
            link(v.tensor_tensor(hot[:], hot[:], spread(wt[:, :, 1]), ALU.mult))
            link(v.tensor_tensor(sb["cw"][:], sb["cw"][:], hot[:], ALU.add))


def experts(nc, dr, sb):
    with ExitStack() as ctx:
        def sem(name):
            return ctx.enter_context(nc.semaphore(name))

        def sbuf(name, shape, dt):
            return ctx.enter_context(nc.sbuf_tensor(name, shape, dt))
        KH = HID // P
        W1 = [sbuf(f"W1_{i}", [P, KD, HID], F32) for i in range(2)]
        W3 = [sbuf(f"W3_{i}", [P, KD, HID], F32) for i in range(2)]
        W2 = [sbuf(f"W2_{i}", [P, KH, D], F32) for i in range(2)]
        moe = sbuf("moe", [P, TILES, D], F32)
        sg = [sbuf(f"sg{i}", [P, GT], F32) for i in range(2)]
        hT = [sbuf(f"hT{i}", [P, KH, GT], F32) for i in range(2)]
        bn = sbuf("bn4", [P, TILES, 6], F32)
        mv = sbuf("mv4", [P, TILES, 2], F32)
        ve = sbuf("ve4", [P, TILES], F32)
        root = sbuf("root4", [P, TILES], F32)
        rs = sbuf("rs4", [P, TILES], F32)
        tm = sbuf("tm4", [P, TILES], F32)
        GP = [ctx.enter_context(nc.psum_tensor(f"GP{i}", [P, GT], F32)) for i in range(2)]
        UP = [ctx.enter_context(nc.psum_tensor(f"UP{i}", [P, GT], F32)) for i in range(2)]
        YP = [ctx.enter_context(nc.psum_tensor(f"YP{i}", [P, G, D], F32)) for i in range(2)]
        w_in = [sem(f"w_in{i}") for i in range(2)]
        g_psum = sem("g_psum")
        u_psum = sem("u_psum")
        silu_done = sem("silu_done")
        h_done = sem("h_done")
        y4_psum = sem("y4_psum")
        y4_out = sem("y4_out")
        var4 = sem("var4")
        root4 = sem("root4s")
        l4 = sem("l4")
        out_ready = sem("out_ready")
        out_stored = sem("out_stored")
        block = ctx.enter_context(nc.Block())
        NE = E + 1
        ROUNDS = GROUPS // 2

        @block.sync
        def _(sp):
            for e in range(NE):
                wait(sp, y4_psum, GROUPS * (e - 1))
                names = ("w1", "w3", "w2") if e else ("sw1", "sw3", "sw2")
                for name, dst in zip(names, (W1, W3, W2)):
                    sp.dma_start(dst[e % 2][:], dr[name][max(e - 1, 0)].rearrange(
                        "(k p) n -> p k n", p=P)).then_inc(w_in[e % 2], 16)
            for b in range(B):
                for c in range(4):
                    sp.wait_ge(out_ready, b * 4 + c + 1)
                    t0 = b * (TILES // B) + c * G
                    sp.dma_start(dr["out"][b, c * GT:(c + 1) * GT, :].rearrange("(t p) d -> p t d", p=P),
                                 sb["x"][:, t0:t0 + G, :]).then_inc(out_stored, 16)
            sp.wait_ge(out_stored, 16 * GROUPS)

        @block.tensor
        def _(pe):
            for e in range(NE):
                xT = sb["xT"][:].rearrange("p k (g n) -> p g k n", n=GT)
                pe.wait_ge(w_in[e % 2], 48 * (e // 2 + 1))

                def up(r, s, e=e):
                    g = e * GROUPS + r * 2 + s
                    for m in range(KH):
                        i = KH * g + m
                        wait(pe, silu_done, i - 1)
                        for k in range(KD):
                            ins = pe.matmul(GP[m % 2][:], W1[e % 2][:, k, m * P:(m + 1) * P],
                                            xT[:, r * 2 + s, k, :], start=(k == 0), stop=(k == KD - 1))
                        ins.then_inc(g_psum, 1)
                        wait(pe, h_done, i - 1)
                        for k in range(KD):
                            ins = pe.matmul(UP[m % 2][:], W3[e % 2][:, k, m * P:(m + 1) * P],
                                            xT[:, r * 2 + s, k, :], start=(k == 0), stop=(k == KD - 1))
                        ins.then_inc(u_psum, 1)

                def down(r, s, e=e):
                    g = e * GROUPS + r * 2 + s
                    pe.wait_ge(h_done, KH * (g + 1))
                    wait(pe, y4_out, g - 1)
                    for j in range(G):
                        for m in range(KH):
                            ins = pe.matmul(YP[s][:, j, :], hT[s][:, m, j * P:(j + 1) * P], W2[e % 2][:, m, :],
                                            start=(m == 0), stop=(m == KH - 1))
                    ins.then_inc(y4_psum, 1)
                pipelined(pe, ROUNDS, 2, [(0, up), (1, down)], peel=2)

        @block.scalar
        def _(act):
            for e in range(NE):
                def silu(r, s, e=e):
                    g = e * GROUPS + r * 2 + s
                    for m in range(KH):
                        i = KH * g + m
                        act.wait_ge(g_psum, i + 1)
                        wait(act, h_done, i - 1)
                        nc.scalar.activation(sg[m % 2][:], GP[m % 2][:], ACT.Silu).then_inc(silu_done, 1)
                pipelined(act, ROUNDS, 2, [(0, silu)], peel=2)
            act.wait_ge(var4, 1)
            nc.scalar.activation(root[:], ve[:], ACT.Sqrt).then_inc(root4, 1)

        @block.vector
        def _(v):
            m4 = moe[:].rearrange("p (g t) d -> p g t d", t=G)
            c4 = sb["cw"][:].rearrange("p (g t) e -> p g t e", t=G)
            for e in range(NE):
                def gate(r, s, e=e):
                    g = e * GROUPS + r * 2 + s
                    for m in range(KH):
                        i = KH * g + m
                        v.wait_ge(silu_done, i + 1)
                        v.wait_ge(u_psum, i + 1)
                        wait(v, y4_psum, g - 1)
                        v.tensor_tensor(hT[s][:, m, :], sg[m % 2][:], UP[m % 2][:], ALU.mult).then_inc(h_done, 1)

                def add(r, s, e=e):
                    g = e * GROUPS + r * 2 + s
                    v.wait_ge(y4_psum, g + 1)
                    if e > 0:
                        v.wait_ge(y4_out, g - GROUPS + 1)
                    for j in range(G):
                        if e == 0:
                            ins = v.tensor_copy(m4[:, r * 2 + s, j, :], YP[s][:, j, :])
                        else:
                            ins = v.scalar_tensor_tensor(m4[:, r * 2 + s, j, :], YP[s][:, j, :],
                                                         c4[:, r * 2 + s, j, e - 1:e],
                                                         m4[:, r * 2 + s, j, :], ALU.mult, ALU.add)
                    ins.then_inc(y4_out, 1)
                pipelined(v, ROUNDS, 2, [(0, gate), (1, add)], peel=2)
            link = Link(v, l4)
            v.wait_ge(y4_out, NE * GROUPS)
            for t in range(TILES):
                ins = v.bn_stats(bn[:, t, :], moe[:, t, :])
            link(ins)
            for t in range(TILES):
                ins = v.bn_aggr(mv[:, t, :], bn[:, t, :])
            link(ins)
            v.tensor_scalar(ve[:], mv[:, :, 1], EPS, None, ALU.add).then_inc(var4, 1)
            v.wait_ge(var4, 1)
            rstd_newton(link, v, ve[:], root[:], rs[:], tm[:], root4, 1)
            for g in range(GROUPS):
                for j in range(G):
                    t = g * G + j
                    ins = v.tensor_scalar(moe[:, t, :], moe[:, t, :], mv[:, t, 0:1], rs[:, t:t + 1],
                                          ALU.subtract, ALU.mult)
                link(ins)
                v.tensor_tensor(sb["x"][:, g * G:(g + 1) * G, :], sb["x"][:, g * G:(g + 1) * G, :],
                                moe[:, g * G:(g + 1) * G, :], ALU.add).then_inc(out_ready, 1)


def build(nc, dr):
    with ExitStack() as ctx:
        def sbuf(name, shape, dt):
            return ctx.enter_context(nc.sbuf_tensor(name, shape, dt))
        dr["QT"] = nc.dram_tensor("QT", (H * QR, T), BF16, kind="Internal").ap()
        dr["KT"] = nc.dram_tensor("KT", (H * KR, T), F16, kind="Internal").ap()
        dr["VD"] = nc.dram_tensor("VD", (P, H, GROUPS, G * VW), BF16, kind="Internal").ap()
        dr["SH"] = nc.dram_tensor("SH", (SROWS, B * H, S), BF16, kind="Internal").ap()
        sb = {
            "x": sbuf("x", [P, TILES, D], F32),
            "wproj": sbuf("wproj", [P, KD, D], F32),
            "rw": sbuf("rw", [E, D], F32),
            "rwT": sbuf("rwT", [P, KD, E], F32),
            "rbias": sbuf("rbias", [P, E], F32),
            "ident": sbuf("ident", [P, P], F32),
            "ident_b": sbuf("ident_b", [P, P], BF16),
            "ident_h": sbuf("ident_h", [P, P], F16),
            "sel": sbuf("sel", [P, 2 * VU], F32),
            "iota8": sbuf("iota8", [P, E], F32),
            "cw": sbuf("cw", [P, TILES, E], F32),
            "guard": sbuf("guard", [P, 1], F32),
            "tick": sbuf("tick", [P, 1], F32),
        }
        with ExitStack() as early:
            def esb(name, shape, dt):
                return early.enter_context(nc.sbuf_tensor(name, shape, dt))
            sb["wqkv"] = esb("wqkv", [P, KD, 3 * D], F32)
            sb["gain"] = esb("gain", [P, 2 * D], F32)
            sb["bias"] = esb("bias", [P, 2 * D], F32)
            setup(nc, dr, sb)
            project_qkv(nc, dr, sb)
        import numpy as np
        safe = int(np.float32(SAFE).view(np.int32))
        bound = nc.values_load(sb["guard"][0:1, 0:1].bitcast(I32))
        with nc.If(bound > safe):
            true_maxima(nc, dr, sb)
        sb["O"] = sbuf("O", [P, B * H * 2, 2, QC // P, VU], F32)
        attention(nc, dr, sb)
        sb["xT"] = sbuf("xT", [P, KD, T], F32)
        project_and_route(nc, dr, sb)
        experts(nc, dr, sb)


_INS = ["L0_attn_x", "L0_attn_w_qkv", "L0_attn_w_proj", "L0_attn_q_gamma", "L0_attn_q_beta", "L0_attn_k_gamma",
        "L0_attn_k_beta", "L0_ffn_router_w", "L0_ffn_experts_bias", "L0_ffn_w1", "L0_ffn_w3", "L0_ffn_w2",
        "L0_ffn_sw1", "L0_ffn_sw3", "L0_ffn_sw2"]


def kernel(**inputs):
    import numpy as np
    import concourse.bacc as bacc
    from concourse.bass_utils import run_bass_kernel_spmd

    nc = bacc.Bacc("TRN2", target_bir_lowering=False, num_devices=1)
    arrays, dr = {}, {}
    for name in _INS:
        a = np.ascontiguousarray(inputs[name])
        arrays[f"in_{name}"] = a
        short = name.replace("L0_attn_", "").replace("L0_ffn_", "")
        dr[short] = nc.dram_tensor(f"in_{name}", a.shape, mybir.dt.from_np(a.dtype), kind="ExternalInput").ap()
    dr["out"] = nc.dram_tensor("out_0", (B, S, D), F32, kind="ExternalOutput").ap()
    build(nc, dr)
    r = run_bass_kernel_spmd(nc, [arrays], core_ids=[0])
    return r.results[0]["out_0"]
```

```python
from contextlib import ExitStack

import concourse.bass as bass
from concourse import mybir

F32 = mybir.dt.float32
BF16 = mybir.dt.bfloat16
F16 = mybir.dt.float16
I32 = mybir.dt.int32
U32 = mybir.dt.uint32
ALU = mybir.AluOpType
ACT = mybir.ActivationFunctionType
AX = mybir.AxisListType
RMAX = bass.bass_isa.ReduceOp.max

P = 128
B, S, D = 2, 2048, 256
H, DH = 16, 16
E, HID = 8, 512
TOPK = 2
EPS = 1e-5
T = B * S
TILES = T // P
KD = D // P
G = 4
GT = G * P
GROUPS = TILES // G
GPB = GROUPS // B
QR = 3 * DH
KR = 2 * DH
PAIR = 6 * DH
SROWS = 3
CROWS = PAIR + SROWS
VW = 64
VU = DH + 1
VP = (0, DH + 2, 2 * DH + 2)
KSCALE = 2.0 ** 12
TOP = 15 * 0.6931471805599453
SAFE = 11.0


def wait(eng, sem, value):
    if isinstance(value, int) and value <= 0:
        return
    eng.wait_ge(sem, value)


def pipelined(eng, stop, steps, stages, peel=1, start=0, drain=True):
    def step(r, s):
        for lag, stage in stages:
            if s >= lag:
                stage(r, s - lag)
            elif not isinstance(r, int) or r > 0:
                stage(r - 1, s - lag + steps)
    if start == 0:
        for r in range(peel):
            for s in range(steps):
                step(r, s)
        start = peel
    with eng.Fori(start, stop) as r:
        for s in range(steps):
            step(r, s)
    if drain:
        for s in range(max(lag for lag, _ in stages)):
            for lag, stage in stages:
                if s < lag:
                    stage(stop - 1, s - lag + steps)


class Link:

    def __init__(self, eng, sem, per_step=0):
        self.eng, self.sem, self.per_step, self.base, self.n = eng, sem, per_step, 0, 0

    def start(self, step):
        assert self.n in (0, self.per_step), self.n
        self.base, self.n = step * self.per_step, 0

    def __call__(self, ins):
        self.n += 1
        ins.then_inc(self.sem, 1)
        self.eng.wait_ge(self.sem, self.base + self.n)


def settle(v, tick):
    v.memset(tick[:], 0.0)


def settle_pool(pool, tick):
    pool.tensor_tensor(tick[:, 0:1], tick[:, 1:2], tick[:, 1:2], ALU.add)


def rstd_newton(link, v, var, root, out, tmp, ready_sem, ready_value):
    v.wait_ge(ready_sem, ready_value)
    link(v.reciprocal(out, root))
    link(v.tensor_tensor(tmp, out, out, ALU.mult))
    link(v.tensor_tensor(tmp, tmp, var, ALU.mult))
    link(v.tensor_scalar(tmp, tmp, -0.5, 1.5, ALU.mult, ALU.add))
    link(v.tensor_tensor(out, out, tmp, ALU.mult))


def setup(nc, dr, sb):
    with ExitStack() as ctx:
        def sem(name):
            return ctx.enter_context(nc.semaphore(name))
        gb = ctx.enter_context(nc.sbuf_tensor("gb", [P, 4, DH], F32))
        wmean = ctx.enter_context(nc.sbuf_tensor("wmean", [P, KD, 2 * H], F32))
        t0 = ctx.enter_context(nc.sbuf_tensor("t0", [P, 2, DH], F32))
        a = ctx.enter_context(nc.sbuf_tensor("a", [P, 4], F32))
        x_loaded = sem("x_loaded")
        w_loaded = sem("w_loaded")
        gb_loaded = sem("gb_loaded")
        zeroed = sem("zeroed")
        ident_made = sem("ident_made")
        setup_link = sem("setup_link")
        block = ctx.enter_context(nc.Block())

        @block.sync
        def _(sp):
            sp.dma_start(sb["wqkv"][:], dr["w_qkv"].rearrange("(k p) n -> p k n", p=P)).then_inc(w_loaded, 16)
            for i, name in enumerate(("q_gamma", "q_beta", "k_gamma", "k_beta")):
                sp.dma_start(gb[:, i, :], dr[name].partition_broadcast(P)).then_inc(gb_loaded, 16)
            for b in range(B):
                sp.dma_start(sb["x"][:, b * (TILES // B):(b + 1) * (TILES // B), :],
                             dr["x"][b].rearrange("(t p) d -> p t d", p=P)).then_inc(x_loaded, 16)
            sp.dma_start(sb["wproj"][:], dr["w_proj"].rearrange("(k p) n -> p k n", p=P)).then_inc(w_loaded, 16)
            sp.dma_start(sb["rw"][:], dr["router_w"]).then_inc(w_loaded, 16)
            sp.dma_start(sb["rbias"][:], dr["experts_bias"].partition_broadcast(P)).then_inc(w_loaded, 16)
            sp.wait_ge(x_loaded, 16 * B)
            sp.wait_ge(w_loaded, 16 * 4)

        @block.gpsimd
        def _(pool):
            pool.memset(sb["ident"][:], 0.0).then_inc(zeroed, 1)
            pool.memset(sb["tick_pool"][:], 0.0)
            pool.memset(sb["sel"][:], 0.0).then_inc(zeroed, 1)
            pool.iota(sb["iota8"][:], pattern=[[1, E]], base=0, channel_multiplier=0,
                      allow_small_or_imprecise_dtypes=True).then_inc(ident_made, 1)
            pool.wait_ge(zeroed, 2)
            pool.affine_select(out=sb["ident"][:], in_=sb["ident"][:], compare_op=ALU.not_equal, fill=1.0,
                               base=0, pattern=[[-1, P]], channel_multiplier=1).then_inc(ident_made, 1)
            n = 2
            for j in range(2):
                cols = sb["sel"][:, VU * j:VU * j + DH]
                for i in range(3):
                    pool.wait_ge(ident_made, n)
                    pool.affine_select(out=cols, in_=cols, compare_op=ALU.not_equal, fill=1.0,
                                       base=-(VW * j + VP[i]), pattern=[[-1, DH]],
                                       channel_multiplier=1).then_inc(ident_made, 1)
                    n += 1
                one = sb["sel"][:, VU * j + DH:VU * j + VU]
                pool.affine_select(out=one, in_=one, compare_op=ALU.not_equal, fill=1.0,
                                   base=-(VW * j + DH), pattern=[[-1, 1]],
                                   channel_multiplier=1).then_inc(ident_made, 1)
                n += 1

        @block.vector
        def _(v):
            link = Link(v, setup_link)
            v.wait_ge(ident_made, 2)
            v.tensor_copy(sb["ident_b"][:], sb["ident"][:])
            v.tensor_copy(sb["ident_h"][:], sb["ident"][:])
            v.wait_ge(w_loaded, 64)
            w = sb["wqkv"][:, :, 0:2 * D].rearrange("p k (h d) -> p k h d", d=DH)
            link(v.tensor_reduce(wmean[:], w, AX.X, ALU.add))
            link(v.tensor_scalar(wmean[:], wmean[:], 1.0 / DH, None, ALU.mult))
            for k in range(KD):
                link(v.tensor_tensor(w[:, k], w[:, k], wmean[:, k].unsqueeze(2).to_broadcast([P, 2 * H, DH]),
                                     ALU.subtract))
            v.wait_ge(gb_loaded, 64)
            link(v.scalar_tensor_tensor(t0[:], gb[:, 2:4, :], -1.0, gb[:, 2:4, :], ALU.mult, ALU.max))
            link(v.scalar_tensor_tensor(t0[:, 0], t0[:, 0], 4.0, t0[:, 1], ALU.mult, ALU.add))
            link(v.tensor_reduce(a[:, 0:1], t0[:, 0], AX.X, ALU.max))
            link(v.tensor_scalar(a[:, 0:1], a[:, 0:1], 1e-30, None, ALU.max))
            link(v.tensor_scalar(a[:, 1:2].bitcast(I32), a[:, 0:1].bitcast(I32), 0x7F800000, None,
                                 ALU.bitwise_and))
            link(v.reciprocal(a[:, 2:3], a[:, 1:2]))
            link(v.tensor_scalar(a[:, 2:3], a[:, 2:3], KSCALE, None, ALU.mult))
            link(v.tensor_scalar(a[:, 3:4], a[:, 1:2], 1.0 / (KSCALE * DH ** 0.5), None, ALU.mult))
            for i in range(4):
                out = sb["gain" if i % 2 == 0 else "bias"][:, (i // 2) * D:(i // 2 + 1) * D]
                scale = a[:, 3:4] if i < 2 else a[:, 2:3]
                link(v.tensor_scalar(out.rearrange("p (h d) -> p h d", d=DH),
                                     gb[:, i, :].unsqueeze(1).to_broadcast([P, H, DH]), scale, None, ALU.mult))


def project_qkv(nc, dr, sb):
    with ExitStack() as ctx:
        def sem(name):
            return ctx.enter_context(nc.semaphore(name))

        def sbuf(name, shape, dt):
            return ctx.enter_context(nc.sbuf_tensor(name, shape, dt))

        bn = sbuf("bn", [P, G, 6], F32)
        mv = sbuf("mv", [P, G, 2], F32)
        ve = sbuf("ve", [P, 2, G], F32)
        root = sbuf("root", [P, 2, G], F32)
        rs = sbuf("rs", [P, G], F32)
        tm = sbuf("tm", [P, G], F32)
        xn = sbuf("xn", [P, 2, G, D], F32)
        xnT = sbuf("xnT", [P, 2, KD, GT], F32)
        C = sbuf("C", [P, 2, G, 2 * D], F32)
        sq = sbuf("sq", [P, 2, G, 2 * D], F32)
        V32 = sbuf("V32", [P, 2, H, G, VU], F32)
        NH = G * 2 * H
        hv = sbuf("hv", [P, 2, NH], F32)
        hroot = sbuf("hroot", [P, 2, NH], F32)
        hr = sbuf("hr", [P, NH], F32)
        ht = sbuf("ht", [P, NH], F32)
        hn = sbuf("hn", [P, NH], F32)
        rest = sbuf("rest", [P, G, D], F32)
        vrest = sbuf("vrest", [P, G, D], F32)
        TQ = sbuf("TQ", [P, G, H * QR], BF16)
        TK = sbuf("TK", [P, G, H * KR], F16)
        VT = sbuf("VT", [P, H, G, VW], BF16)
        NQ, NK = H * QR // P, H * KR // P
        qkT = sbuf("qkT", [P, NQ + NK, GT], BF16)
        norms = sbuf("norms", [P, GROUPS, 2], F32)
        ksum = sbuf("ksum", [P, GROUPS, NK], F32)
        stat = sbuf("stat", [P, 4], F32)
        allst = sbuf("allst", [P, 4], F32)
        fin = sbuf("fin", [P, 8], F32)
        shift = sbuf("shift", [B * H, SROWS, S], BF16)
        QP = [ctx.enter_context(nc.psum_tensor(f"QP{i}", [P, 1024], F32)) for i in range(2)]
        XP = [ctx.enter_context(nc.psum_tensor(f"XP{i}", [P, 2, KD, P], F32)) for i in range(2)]
        TP = [ctx.enter_context(nc.psum_tensor(f"TP{i}", [P, GT], BF16)) for i in range(2)]

        var_ready = sem("var_ready")
        root_ready = sem("root_ready")
        xn_ready = sem("xn_ready")
        xT_psum = sem("xT_psum")
        xT_ready = sem("xT_ready")
        qkv_psum = sem("qkv_psum")
        qkv_out = sem("qkv_out")
        head_var = sem("head_var")
        head_root = sem("head_root")
        heads_ready = sem("heads_ready")
        squares = sem("squares")
        sq_used = sem("sq_used")
        v1_ready = sem("v1_ready")
        vrest_ready = sem("vrest_ready")
        v2_ready = sem("v2_ready")
        v_ready = sem("v_ready")
        qk_ready = sem("qk_ready")
        part_psum = sem("part_psum")
        part_out = sem("part_out")
        stored = sem("stored")
        v_stored = sem("v_stored")
        v32_stored = [sem(f"v32_stored{i}") for i in range(2)]
        vt_init = sem("vt_init")
        norms_ready = sem("norms_ready")
        reduced = sem("reduced")
        roots2 = sem("roots2")
        shift_ready = sem("shift_ready")
        shift_stored = sem("shift_stored")
        dve_link = sem("dve_link")
        rs_ready = sem("rs_ready")
        ROUNDS, STEPS = GROUPS // 2, 2
        NT = NQ + NK

        qt = dr["QT"].rearrange("r (g n) -> r g n", n=GT)
        kt = dr["KT"].rearrange("r (g n) -> r g n", n=GT)
        vd = dr["VD"]
        block = ctx.enter_context(nc.Block())

        @block.tensor
        def _(pe):
            def turn_x(r, s):
                g = r * STEPS + s
                pe.wait_ge(xn_ready, g + 1)
                for h in range(2):
                    wait(pe, xT_ready, 2 * g + h - 1)
                    for t in range(2):
                        for k in range(KD):
                            ins = pe.transpose(XP[h][:, t, k, :], xn[:, s, 2 * h + t, k * P:(k + 1) * P],
                                               sb["ident"][:])
                    ins.then_inc(xT_psum, 1)

            def qkv(r, s):
                g = r * STEPS + s
                pe.wait_ge(xT_ready, 2 * g + 2)
                for j in range(G):
                    wait(pe, qkv_out, G * g + j - 1)
                    for c0, c1 in ((0, 512), (512, 768)):
                        for k in range(KD):
                            ins = pe.matmul(QP[j % 2][:, c0:c1], xnT[:, s, k, j * P:(j + 1) * P],
                                            sb["wqkv"][:, k, c0:c1], start=(k == 0), stop=(k == KD - 1))
                    ins.then_inc(qkv_psum, 1)

            def turn_parts(r, s):
                g = r * STEPS + s
                pe.wait_ge(qk_ready, g + 1)
                for m in range(NT):
                    wait(pe, part_out, NT * g + max(m - 1, 0))
                    for j in range(G):
                        if m < NQ:
                            ins = pe.transpose(TP[m % 2][:, j * P:(j + 1) * P], TQ[:, j, m * P:(m + 1) * P],
                                               sb["ident_b"][:])
                        else:
                            ins = pe.transpose(TP[m % 2][:, j * P:(j + 1) * P].bitcast(F16),
                                               TK[:, j, (m - NQ) * P:(m - NQ + 1) * P], sb["ident_h"][:])
                    ins.then_inc(part_psum, 1)

            pipelined(pe, ROUNDS, STEPS, [(0, turn_x), (1, qkv), (2, turn_parts)], peel=2)

        @block.scalar
        def _(act):
            def norm_x(r, s):
                g = r * STEPS + s
                act.wait_ge(var_ready, g + 1)
                nc.scalar.activation(root[:, s], ve[:, s], ACT.Sqrt).then_inc(root_ready, 1)
                for h in range(2):
                    act.wait_ge(xT_psum, 2 * g + h + 1)
                    wait(act, qkv_psum, G * (g - 1))
                    nc.scalar.activation(
                        xnT[:, s, :, 2 * h * P:2 * (h + 1) * P].rearrange("p k (t n) -> p t k n", n=P),
                        XP[h][:], ACT.Copy).then_inc(xT_ready, 1)

            def take_qkv(r, s):
                g = r * STEPS + s
                wait(act, qk_ready, g - 1)
                wait(act, v_ready, g - 1)
                wait(act, v32_stored[s], 16 * r)
                for j in range(G):
                    act.wait_ge(qkv_psum, G * g + j + 1)
                    nc.scalar.activation(C[:, s, j], QP[j % 2][:, 0:512], ACT.Copy)
                    nc.scalar.activation(sq[:, s, j], QP[j % 2][:, 0:512], ACT.Square)
                    nc.scalar.activation(V32[:, s, :, j, 0:DH],
                                         QP[j % 2][:, 512:768].rearrange("p (h d) -> p h d", d=DH), ACT.Copy).then_inc(qkv_out, 1)

            def head_root_of(r, s):
                g = r * STEPS + s
                act.wait_ge(head_var, g + 1)
                nc.scalar.activation(hroot[:, s], hv[:, s], ACT.Sqrt).then_inc(head_root, 1)

            def split(r, s):
                g = r * STEPS + s
                vt = VT[:].rearrange("p h g w -> p g h w")
                v4 = V32[:, s, :, :, 0:DH].rearrange("p h g d -> p g h d")
                act.wait_ge(qkv_out, G * g + G)
                act.wait_ge(vt_init, 4)
                wait(act, v_stored, 16 * g)
                for j in range(G):
                    ins = nc.scalar.activation(vt[:, j, :, 0:DH], v4[:, j], ACT.Copy)
                ins.then_inc(v1_ready, 1)
                act.wait_ge(vrest_ready, g + 1)
                r4 = vrest[:].rearrange("p g (h d) -> p g h d", d=DH)
                for j in range(G):
                    ins = nc.scalar.activation(vt[:, j, :, VP[1]:VP[1] + DH], r4[:, j], ACT.Copy)
                ins.then_inc(v2_ready, 1)
                act.wait_ge(heads_ready, g + 1)
                nc.scalar.activation(sq[:, s], C[:, s], ACT.Square).then_inc(squares, 1)

            def take_parts(r, s):
                g = r * STEPS + s
                wait(act, stored, 32 * g)
                for m in range(NT):
                    act.wait_ge(part_psum, NT * g + m + 1)
                    if m < NQ:
                        ins = nc.scalar.activation(qkT[:, m], TP[m % 2][:], ACT.Copy)
                    else:
                        ins = nc.scalar.activation(qkT[:, m].bitcast(F16), TP[m % 2][:].bitcast(F16), ACT.Copy,
                                                   accum_out=ksum[:, g, m - NQ:m - NQ + 1])
                    ins.then_inc(part_out, 1)

            pipelined(act, ROUNDS, STEPS, [(0, norm_x), (2, head_root_of), (1, take_qkv), (2, split),
                                           (2, take_parts)], peel=2)
            act.wait_ge(reduced, 1)
            nc.scalar.activation(fin[:, 0:2], allst[:, 0:2], ACT.Sqrt).then_inc(roots2, 1)

        @block.vector
        def _(v):
            link = Link(v, dve_link, 0)
            v.memset(VT[:], 0.0).then_inc(vt_init, 1)
            v.wait_ge(vt_init, 1)
            v.memset(VT[:, :, :, DH:VU], 1.0).then_inc(vt_init, 1)
            for i in range(2):
                v.memset(V32[:, i, :, :, DH:VU], 1.0).then_inc(vt_init, 1)

            xlink = Link(v, sem("x_link"), 2 + 4)
            hlink = Link(v, sem("h_link"), 16)

            def norm_x(r, s):
                g = r * STEPS + s
                xlink.start(g)
                settle(v, sb["tick"])
                x4 = sb["x"][:].rearrange("p (g t) d -> p g t d", t=G)
                for t in range(G):
                    ins = v.bn_stats(bn[:, t, :], x4[:, g, t, :])
                xlink(ins)
                settle(v, sb["tick"])
                for t in range(G):
                    ins = v.bn_aggr(mv[:, t, :], bn[:, t, :])
                xlink(ins)
                v.tensor_scalar(ve[:, s], mv[:, :, 1], EPS, None, ALU.add).then_inc(var_ready, 1)
                v.wait_ge(var_ready, g + 1)
                v.wait_ge(root_ready, g + 1)
                xlink(v.reciprocal(rs[:], root[:, s]))
                xlink(v.tensor_tensor(tm[:], rs[:], rs[:], ALU.mult))
                xlink(v.tensor_tensor(tm[:], tm[:], ve[:, s], ALU.mult))
                xlink(v.tensor_scalar(tm[:], tm[:], -0.5, 1.5, ALU.mult, ALU.add))
                v.tensor_tensor(rs[:], rs[:], tm[:], ALU.mult).then_inc(rs_ready, 1)
                v.wait_ge(rs_ready, g + 1)
                wait(v, xT_psum, 2 * (g - 1))
                for t in range(G):
                    ins = v.tensor_scalar(xn[:, s, t, :], x4[:, g, t, :], mv[:, t, 0:1], rs[:, t:t + 1],
                                          ALU.subtract, ALU.mult)
                ins.then_inc(xn_ready, 1)

            def heads(r, s):
                g = r * STEPS + s
                hlink.start(g)
                v.wait_ge(qkv_out, G * g + G)
                c3 = C[:, s].rearrange("p g (h d) -> p (g h) d", d=DH)
                s3 = sq[:, s].rearrange("p g (h d) -> p (g h) d", d=DH)
                hlink(v.tensor_reduce(hv[:, s], s3, AX.X, ALU.add))
                v.tensor_scalar(hv[:, s], hv[:, s], 1.0 / DH, EPS, ALU.mult, ALU.add).then_inc(head_var, 1)
                vt = VT[:].rearrange("p h g w -> p g h w")
                v4 = V32[:, s, :, :, 0:DH].rearrange("p h g d -> p g h d")
                r4 = vrest[:].rearrange("p g (h d) -> p g h d", d=DH)
                v.wait_ge(v1_ready, g + 1)
                for j in range(G):
                    ins = v.tensor_tensor(r4[:, j], v4[:, j], vt[:, j, :, 0:DH], ALU.subtract)
                ins.then_inc(vrest_ready, 1)
                v.wait_ge(head_var, g + 1)
                v.wait_ge(head_root, g + 1)
                hlink(v.reciprocal(hr[:], hroot[:, s]))
                hlink(v.tensor_tensor(ht[:], hr[:], hr[:], ALU.mult))
                hlink(v.tensor_tensor(ht[:], ht[:], hv[:, s], ALU.mult))
                hlink(v.tensor_scalar(ht[:], ht[:], -0.5, 1.5, ALU.mult, ALU.add))
                hlink(v.tensor_tensor(hr[:], hr[:], ht[:], ALU.mult))
                hlink(v.tensor_tensor(c3, c3, hr[:].unsqueeze(2).to_broadcast([P, NH, DH]), ALU.mult))
                gain = sb["gain"][:].unsqueeze(1).to_broadcast([P, G, 2 * D])
                bias = sb["bias"][:].unsqueeze(1).to_broadcast([P, G, 2 * D])
                hlink(v.tensor_tensor(C[:, s], C[:, s], gain, ALU.mult))
                v.tensor_tensor(C[:, s], C[:, s], bias, ALU.add).then_inc(heads_ready, 1)
                v.wait_ge(v2_ready, g + 1)
                for j in range(G):
                    ins = v.tensor_tensor(vt[:, j, :, VP[2]:VP[2] + DH], r4[:, j], vt[:, j, :, VP[1]:VP[1] + DH],
                                          ALU.subtract)
                ins.then_inc(v_ready, 1)
                v.wait_ge(heads_ready, g + 1)
                wait(v, part_psum, NT * g)
                q = C[:, s, :, 0:D].rearrange("p g (h d) -> p g h d", d=DH)
                k = C[:, s, :, D:2 * D].rearrange("p g (h d) -> p g h d", d=DH)
                tq = TQ[:].rearrange("p g (h i d) -> p g h i d", i=3, d=DH)
                tk = TK[:].rearrange("p g (h i d) -> p g h i d", i=2, d=DH)
                rr = rest[:].rearrange("p g (h d) -> p g h d", d=DH)

                def each(fn):
                    for j in range(G):
                        ins = fn(j)
                    return ins
                hlink(each(lambda j: v.tensor_copy(tq[:, j, :, 0], q[:, j])))
                hlink(each(lambda j: v.tensor_tensor(rr[:, j], q[:, j], tq[:, j, :, 0], ALU.subtract)))
                hlink(each(lambda j: v.tensor_copy(tq[:, j, :, 1], rr[:, j])))
                hlink(each(lambda j: v.tensor_tensor(tq[:, j, :, 2], rr[:, j], tq[:, j, :, 1], ALU.subtract)))
                hlink(each(lambda j: v.tensor_copy(tk[:, j, :, 0], k[:, j])))
                v.wait_ge(squares, g + 1)
                hlink(v.tensor_reduce(hn[:], s3, AX.X, ALU.add))
                hnv = hn[:].rearrange("p (g i h) -> p i g h", g=G, i=2)
                hlink(v.tensor_reduce(norms[:, g, 0:1], hnv[:, 0], AX.XY, ALU.max))
                hlink(v.tensor_reduce(norms[:, g, 1:2], hnv[:, 1], AX.XY, ALU.max))
                each(lambda j: v.tensor_tensor(tk[:, j, :, 1], k[:, j], tk[:, j, :, 0],
                                               ALU.subtract)).then_inc(qk_ready, 1)

            pipelined(v, ROUNDS, STEPS, [(0, norm_x), (2, heads)], peel=2)

            v.wait_ge(part_out, NT * GROUPS)
            v.memset(stat[:], 0.0).then_inc(norms_ready, 1)
            v.wait_ge(norms_ready, 1)
            link(v.tensor_reduce(stat[:, 0:2], norms[:].rearrange("p g i -> p i g"), AX.X, ALU.max))
            kb = ksum[:].rearrange("p (b g) m -> p b m g", b=B)
            link(v.tensor_reduce(ht[:, 0:B * NK].rearrange("p (b m) -> p b m", b=B), kb, AX.X, ALU.add))
            v.tensor_reduce(stat[:, 2:3], ht[:, 0:B * NK], AX.X, ALU.max,
                            apply_absolute_value=True).then_inc(norms_ready, 1)
            v.wait_ge(roots2, 1)
            link(v.tensor_tensor(fin[:, 2:3], fin[:, 0:1], fin[:, 1:2], ALU.mult))
            link(v.tensor_scalar(fin[:, 3:4], allst[:, 2:3], 4.01 / S, None, ALU.mult))
            link(v.tensor_tensor(fin[:, 3:4], fin[:, 3:4], fin[:, 0:1], ALU.mult))
            link(v.tensor_tensor(fin[:, 4:5], fin[:, 2:3], fin[:, 3:4], ALU.add))
            link(v.tensor_scalar(sb["guard"][:], fin[:, 4:5], 1.001, None, ALU.mult))
            link(v.tensor_scalar(fin[:, 5:6], fin[:, 2:3], -1.001, TOP, ALU.mult, ALU.add))
            link(v.memset(shift[:], 0.0))
            v.tensor_scalar(shift[:, 0, :], shift[:, 0, :], fin[0:B * H, 5:6], None,
                            ALU.add).then_inc(shift_ready, 1)

        @block.gpsimd
        def _(pool):
            pool.wait_ge(norms_ready, 2)
            pool.partition_all_reduce(allst[:], stat[:], P, RMAX).then_inc(reduced, 1)

        @block.sync
        def _(sp):
            def store(r, s):
                g = r * STEPS + s
                sp.wait_ge(qkv_out, G * g + G)
                sp.dma_start(dr["VF"][:, :, g, :], V32[:, s].rearrange("p h g w -> p h (g w)")).then_inc(
                    v32_stored[s], 16)
                sp.wait_ge(v_ready, g + 1)
                sp.dma_start(vd[:, :, g, :], VT[:].rearrange("p h g w -> p h (g w)")).then_inc(v_stored, 16)
                sp.wait_ge(part_out, NT * g + NT)
                sp.dma_start(qt[:, g, :].rearrange("(m p) n -> p m n", p=P),
                             qkT[:, 0:NQ]).then_inc(stored, 16)
                sp.dma_start(kt[:, g, :].rearrange("(m p) n -> p m n", p=P),
                             qkT[:, NQ:NT].bitcast(F16)).then_inc(stored, 16)
            sp.wait_ge(vt_init, 4)
            pipelined(sp, ROUNDS, STEPS, [(0, store)])
            for s in range(2):
                sp.wait_ge(v32_stored[s], 16 * ROUNDS)
            sp.wait_ge(shift_ready, 1)
            sp.dma_start(dr["SH"].rearrange("i b n -> b i n"), shift[:]).then_inc(shift_stored, 16)
            sp.wait_ge(shift_stored, 16)
            sp.wait_ge(v_stored, 16 * GROUPS)
            sp.wait_ge(stored, 32 * GROUPS)


def true_maxima(nc, dr, sb):
    BH = B * H
    QTILES = S // P
    with ExitStack() as ctx:
        def sem(name):
            return ctx.enter_context(nc.semaphore(name))

        def sbuf(name, shape, dt):
            return ctx.enter_context(nc.sbuf_tensor(name, shape, dt))
        Q = sbuf("mQ", [PAIR, S], BF16)
        K = sbuf("mK", [PAIR, S], F16)
        top = sbuf("top", [P, BH, QTILES], F32)
        part = sbuf("part", [P, SROWS, BH * QTILES], BF16)
        turned = sbuf("mturned", [P, P], BF16)
        scores = ctx.enter_context(nc.psum_tensor("mscores", [P, S], F32))
        TM = ctx.enter_context(nc.psum_tensor("TM", [P, P], BF16))
        m_loaded = sem("m_loaded")
        m_scores = sem("m_scores")
        m_max = sem("m_max")
        m_link = sem("m_link")
        m_parts = sem("m_parts")
        m_turned = sem("m_turned")
        m_copied = sem("m_copied")
        m_stored = sem("m_stored")
        block = ctx.enter_context(nc.Block())

        @block.sync
        def _(sp):
            def load(bh):
                wait(sp, m_scores, bh * QTILES)
                load_head(sp, dr, bh, Q, K, m_loaded)
            load(0)
            with sp.Fori(1, BH) as bh:
                load(bh)
            for i in range(SROWS):
                for c in range(BH * QTILES // P):
                    sp.wait_ge(m_copied, i * (BH * QTILES // P) + c + 1)
                    rows = dr["SH"][i].rearrange("b (q n) -> (b q) n", n=P)
                    sp.dma_start(rows[c * P:(c + 1) * P, :], turned[:]).then_inc(m_stored, 16)
                    sp.wait_ge(m_stored, 16 * (i * (BH * QTILES // P) + c + 1))

        @block.tensor
        def _(pe):
            def head(bh):
                pe.wait_ge(m_loaded, LOADS * 16 * (bh + 1))
                for q in range(QTILES):
                    wait(pe, m_max, bh * QTILES + q)
                    for c in range(S // 512):
                        ins = pe.matmul(scores[:, c * 512:(c + 1) * 512], Q[:, q * P:(q + 1) * P],
                                        K[:, c * 512:(c + 1) * 512], start=True, stop=True)
                    ins.then_inc(m_scores, 1)
            head(0)
            with pe.Fori(1, BH) as bh:
                head(bh)
            pe.wait_ge(m_parts, 1)
            n = 0
            for i in range(SROWS):
                for c in range(BH * QTILES // P):
                    wait(pe, m_copied, n)
                    pe.transpose(TM[:], part[:, i, c * P:(c + 1) * P], sb["ident_b"][:]).then_inc(m_turned, 1)
                    n += 1

        @block.scalar
        def _(act):
            act.nop()

        @block.gpsimd
        def _(pool):
            pool.nop()

        @block.vector
        def _(v):
            with v.Fori(0, BH) as bh:
                for q in range(QTILES):
                    v.wait_ge(m_scores, bh * QTILES + q + 1)
                    v.tensor_reduce(top[:, bh, q:q + 1], scores[:], AX.X, ALU.max).then_inc(m_max, 1)
            v.wait_ge(m_max, BH * QTILES)
            link = Link(v, m_link)
            t = top[:].rearrange("p b q -> p (b q)")
            link(v.tensor_scalar(t, t, -1.0, TOP, ALU.mult, ALU.add))
            link(v.tensor_copy(part[:, 0], t))
            link(v.tensor_tensor(t, t, part[:, 0], ALU.subtract))
            link(v.tensor_copy(part[:, 1], t))
            v.tensor_tensor(part[:, 2], t, part[:, 1], ALU.subtract).then_inc(m_parts, 1)
            n = 0
            for i in range(SROWS):
                for c in range(BH * QTILES // P):
                    v.wait_ge(m_turned, n + 1)
                    wait(v, m_stored, 16 * n)
                    v.tensor_copy(turned[:], TM[:]).then_inc(m_copied, 1)
                    n += 1


LOADS = 8


def load_head(sp, dr, bh, Q, K, loaded):
    b, h = bh // H, bh % H
    qv = dr["QT"].rearrange("(h r) (b n) -> h b r n", r=QR, n=S)
    kv = dr["KT"].rearrange("(h r) (b n) -> h b r n", r=KR, n=S)
    for i in range(2):
        sp.dma_start(Q[i * QR:(i + 1) * QR, :], qv[h, b]).then_inc(loaded, 16)
    for i in range(2):
        for j in range(3):
            sp.dma_start(K[i * QR + j * DH:i * QR + (j + 1) * DH, :],
                         kv[h, b, i * DH:(i + 1) * DH]).then_inc(loaded, 16)


NP = 8
NB = 5
KT = S // P
STEPS = 2 * 2 * KT
LAG = 4
QC = 512
WHOLE = [s for s in range(STEPS) if s % 8 in (1, 4, 6)]
PARTED = [s for s in range(STEPS) if s not in WHOLE]
HI_ACT = [s for s in PARTED if s % 8 == 2]
HI_DVE = [s for s in PARTED if s not in HI_ACT]
SC = [s % 3 for s in range(STEPS - 4)] + [0, 1, 0, 2]
SC_BACK = [next(d for d in range(1, STEPS) if SC[s - d] == SC[s]) for s in range(STEPS)]
PART = {s: i % NB for i, s in enumerate(PARTED)}
PART_BACK = {s: (s - PARTED[i - NB]) % STEPS for i, s in enumerate(PARTED)}


def attention(nc, dr, sb):
    with ExitStack() as ctx:
        def sem(name):
            return ctx.enter_context(nc.semaphore(name))

        def sbuf(name, shape, dt):
            return ctx.enter_context(nc.sbuf_tensor(name, shape, dt))
        Q = [sbuf(f"Q{i}", [CROWS, S], BF16) for i in range(2)]
        K = [sbuf(f"K{i}", [CROWS, S], F16) for i in range(2)]
        V = [sbuf(f"V{i}", [P, KT, VW], BF16) for i in range(2)]
        V32 = [sbuf(f"V32_{i}", [P, KT, VU], F32) for i in range(2)]
        pr = [sbuf(f"pr{i}", [P, 2 * QC], F32) for i in range(NP)]
        hi = [sbuf(f"hi{i}", [P, 2 * QC], F16) for i in range(NB)]
        lo = [sbuf(f"lo{i}", [P, 2 * QC], F16) for i in range(NB)]
        acc_sb = [sbuf(f"acc_sb{i}", [P, QC], F32) for i in range(2)]
        sc = [ctx.enter_context(nc.psum_tensor(f"sc{i}", [P, 2 * QC], F32)) for i in range(max(SC) + 1)]
        acc = [ctx.enter_context(nc.psum_tensor(f"acc{i}", [P, QC], F32)) for i in range(2)]
        turned = [a[:, 0:QC // P * 2 * VU].rearrange("p (q d) -> p q d", q=QC // P) for a in acc]
        loaded = [sem(f"loaded{i}") for i in range(2)]
        ones = sem("ones")
        scores_ready = sem("scores_ready")
        exp_done = sem("exp_done")
        hi_act = sem("hi_act")
        hi_dve = sem("hi_dve")
        lo_done = sem("lo_done")
        pv_done = sem("pv_done")
        acc_out = sem("acc_out")
        turned_ready = sem("turned_ready")
        out_done = sem("out_done")
        ROUNDS = B * H // 2
        GS = KT
        GR = STEPS // GS
        block = ctx.enter_context(nc.Block())

        def hi_ready(eng, r, s):
            mine = HI_ACT if s in HI_ACT else HI_DVE
            eng.wait_ge(hi_act if s in HI_ACT else hi_dve, r * len(mine) + mine.index(s) + 1)

        def lo_ready(eng, r, s):
            wait(eng, lo_done, r * len(PARTED) + PARTED.index(s) + 1)

        @block.sync
        def _(sp):
            def load(r, s):
                wait(sp, pv_done, r * STEPS + (s - 1) * (STEPS // 2))
                bh = 2 * r + s
                load_head(sp, dr, bh, Q[s], K[s], loaded[s])
                sp.dma_start(Q[s][PAIR:CROWS, :], dr["SH"][:, bh, :]).then_inc(loaded[s], 16)
                b, h = bh // H, bh % H
                sp.dma_start(V[s][:].rearrange("p k w -> p (k w)"),
                             dr["VD"].rearrange("p h (b g) w -> p b h (g w)", b=B)[:, b, h]).then_inc(loaded[s], 16)
                sp.dma_start(V32[s][:].rearrange("p k w -> p (k w)"),
                             dr["VF"].rearrange("p h (b g) w -> p b h (g w)", b=B)[:, b, h]).then_inc(loaded[s], 16)
            pipelined(sp, ROUNDS, 2, [(0, load)])

        @block.tensor
        def _(pe):
            pe.wait_ge(ones, 2)

            def scores(r, s):
                n = r * STEPS + s
                head, k, c = s // (STEPS // 2), s % KT, s // KT % 2
                if s % (STEPS // 2) == 0:
                    pe.wait_ge(loaded[head], 16 * (LOADS + 3) * (r + 1))
                wait(pe, exp_done, n - SC_BACK[s] + 1)
                for j in range(2):
                    ins = pe.matmul(sc[SC[s]][:, j * QC:(j + 1) * QC], K[head][:, k * P:(k + 1) * P],
                                    Q[head][:, (2 * c + j) * QC:(2 * c + j + 1) * QC], start=True, stop=True)
                ins.then_inc(scores_ready, 1)

            def values(r, s):
                n = r * STEPS + s
                head, k = s // (STEPS // 2), s % KT
                if k == 0:
                    wait(pe, out_done, r * GR + s // GS - 1)
                if s in WHOLE:
                    pe.wait_ge(exp_done, n + 1)
                    for j in range(2):
                        ins = pe.matmul(acc[s // GS % 2][j * VW:j * VW + VU, :], V32[head][:, k, :],
                                        pr[s % NP][:, j * QC:(j + 1) * QC], start=False, stop=(k == KT - 1))
                    ins.then_inc(pv_done, 1)
                    return
                hi_ready(pe, r, s)
                for part, ready in ((hi, False), (lo, True)):
                    if ready:
                        lo_ready(pe, r, s)
                    for j in range(2):
                        ins = pe.matmul(acc[s // GS % 2][j * VW:(j + 1) * VW, :], V[head][:, k, :],
                                        part[PART[s]][:, j * QC:(j + 1) * QC],
                                        start=(k == 0 and not ready), stop=(k == KT - 1 and ready))
                ins.then_inc(pv_done, 1)

            def turn(r, s):
                if s % GS != GS - 1:
                    return
                g = r * GR + s // GS
                pe.wait_ge(acc_out, g + 1)
                for q in range(QC // P):
                    ins = pe.matmul(turned[s // GS % 2][:, q, :], acc_sb[s // GS % 2][:, q * P:(q + 1) * P], sb["sel"][:],
                                    start=True, stop=True)
                ins.then_inc(turned_ready, 1)

            pipelined(pe, ROUNDS, STEPS, [(0, scores), (LAG, values), (LAG + 3, turn)])

        @block.scalar
        def _(act):
            def exponentials(r, s):
                n = r * STEPS + s
                act.wait_ge(scores_ready, n + 1)
                last, was = (r, s - NP) if s >= NP else (r - 1, s - NP + STEPS)
                if was in WHOLE:
                    wait(act, pv_done, n - NP + 1)
                elif not isinstance(last, int) or last >= 0:
                    lo_ready(act, last, was)
                nc.scalar.activation(pr[s % NP][:], sc[SC[s]][:], ACT.Exp).then_inc(exp_done, 1)

            def high(r, s):
                if s not in HI_ACT:
                    return
                n = r * STEPS + s
                act.wait_ge(exp_done, n + 1)
                wait(act, pv_done, n - PART_BACK[s] + 1)
                nc.scalar.activation(hi[PART[s]][:], pr[s % NP][:], ACT.Copy).then_inc(hi_act, 1)

            def take(r, s):
                if s % GS != GS - 1:
                    return
                g = r * GR + s // GS
                act.wait_ge(pv_done, r * STEPS + s + 1)
                wait(act, turned_ready, g - 1)
                nc.scalar.activation(acc_sb[s // GS % 2][:], acc[s // GS % 2][:], ACT.Copy).then_inc(acc_out, 1)

            pipelined(act, ROUNDS, STEPS, [(0, exponentials), (0, high), (LAG + 1, take)])

        @block.vector
        def _(v):
            for i in range(2):
                v.memset(K[i][PAIR:CROWS, :], 1.0).then_inc(ones, 1)
            out = sb["O"][:].rearrange("p (r g) j q d -> p r g j q d", r=ROUNDS)

            def low(r, s):
                if s in WHOLE:
                    return
                n = r * STEPS + s
                v.wait_ge(exp_done, n + 1)
                wait(v, pv_done, n - PART_BACK[s] + 1)
                if s in HI_DVE:
                    v.tensor_copy(hi[PART[s]][:], pr[s % NP][:]).then_inc(hi_dve, 1)
                hi_ready(v, r, s)
                v.tensor_tensor(lo[PART[s]][:], pr[s % NP][:], hi[PART[s]][:],
                                ALU.subtract).then_inc(lo_done, 1)

            def keep(r, s):
                if s % GS != GS - 1:
                    return
                g = r * GR + s // GS
                v.wait_ge(turned_ready, g + 1)
                v.tensor_copy(out[:, r, s // GS].rearrange("p j q d -> p q j d"),
                              turned[s // GS % 2].rearrange("p q (j d) -> p q j d", j=2)).then_inc(out_done, 1)

            pipelined(v, ROUNDS, STEPS, [(0, low), (LAG + 4, keep)])


def project_and_route(nc, dr, sb):
    with ExitStack() as ctx:
        def sem(name):
            return ctx.enter_context(nc.semaphore(name))

        def sbuf(name, shape, dt):
            return ctx.enter_context(nc.sbuf_tensor(name, shape, dt))
        den = sbuf("den", [P, G, H], F32)
        att = sbuf("att", [P, 2, G, D], F32)
        attT = sbuf("attT", [P, 2, KD, GT], F32)
        y = sbuf("y", [P, G, D], F32)
        bn = sbuf("bn3", [P, G, 6], F32)
        mv = sbuf("mv3", [P, G, 2], F32)
        ve = sbuf("ve3", [P, 2, 2, G], F32)
        root = sbuf("root3", [P, 2, 2, G], F32)
        rs = sbuf("rs3", [P, G], F32)
        tm = sbuf("tm3", [P, G], F32)
        xn = sbuf("xn3", [P, 2, G, D], F32)
        TPa = [ctx.enter_context(nc.psum_tensor(f"TPa{i}", [P, 2, KD, P], F32)) for i in range(2)]
        Y = ctx.enter_context(nc.psum_tensor("Y", [P, G, D], F32))
        TX = [ctx.enter_context(nc.psum_tensor(f"TX{i}", [P, 2, KD, P], F32)) for i in range(2)]
        Z = ctx.enter_context(nc.psum_tensor("Z", [P, G, E], F32))
        att_ready = sem("att_ready")
        aT_psum = sem("aT_psum")
        aT_ready = sem("aT_ready")
        y_psum = sem("y_psum")
        y_out = sem("y_out")
        var3 = sem("var3")
        root3 = sem("root3s")
        xn3 = sem("xn3s")
        xT3_psum = sem("xT3_psum")
        xT3 = sem("xT3")
        z_psum = sem("z_psum")
        z_out = sem("z_out")
        rs_done = sem("rs_done")
        x1_done = sem("x1_done")
        l3 = sem("l3")
        l3b = sem("l3b")
        xn_stored = [sem(f"xn_stored{i}") for i in range(2)]
        rw_turned = sem("rw_turned")
        rw_ready = sem("rw_ready")
        w_in = sem("w13_in")
        ROUNDS, STEPS3 = GROUPS // 2, 2
        block = ctx.enter_context(nc.Block())

        @block.tensor
        def _(pe):
            def turn_att(r, s):
                g = r * STEPS3 + s
                pe.wait_ge(att_ready, g + 1)
                for h in range(2):
                    wait(pe, aT_ready, 2 * g + h - 1)
                    for t in range(2):
                        for k in range(KD):
                            ins = pe.transpose(TPa[h][:, t, k, :], att[:, s, 2 * h + t, k * P:(k + 1) * P],
                                               sb["ident"][:])
                    ins.then_inc(aT_psum, 1)

            def project(r, s):
                g = r * STEPS3 + s
                pe.wait_ge(aT_ready, 2 * g + 2)
                wait(pe, y_out, g)
                for j in range(G):
                    for k in range(KD):
                        ins = pe.matmul(Y[:, j, :], attT[:, s, k, j * P:(j + 1) * P], sb["wproj"][:, k, :],
                                        start=(k == 0), stop=(k == KD - 1))
                ins.then_inc(y_psum, 1)

            def turn_xn(r, s):
                g = r * STEPS3 + s
                pe.wait_ge(xn3, g + 1)
                for h in range(2):
                    wait(pe, xT3, 2 * g + h - 1)
                    for t in range(2):
                        for k in range(KD):
                            ins = pe.transpose(TX[h][:, t, k, :], xn[:, s, 2 * h + t, k * P:(k + 1) * P],
                                               sb["ident"][:])
                    ins.then_inc(xT3_psum, 1)

            def route(r, s):
                g = r * STEPS3 + s
                pe.wait_ge(xT3, 2 * g + 2)
                wait(pe, z_out, g)
                for j in range(G):
                    for k in range(KD):
                        ins = pe.matmul(Z[:, j, :], attT[:, s, k, j * P:(j + 1) * P], sb["rwT"][:, k, :],
                                        start=(k == 0), stop=(k == KD - 1))
                ins.then_inc(z_psum, 1)

            for k in range(KD):
                ins = pe.transpose(Z[:, k, :], sb["rw"][:, k * P:(k + 1) * P], sb["ident"][0:E, 0:E])
            ins.then_inc(rw_turned, 1)
            pe.wait_ge(rw_ready, 1)
            pipelined(pe, ROUNDS, STEPS3, [(0, turn_att), (0, project), (1, turn_xn), (1, route)], peel=2)

        @block.scalar
        def _(act):
            def evac(r, s):
                g = r * STEPS3 + s
                wait(act, z_psum, g - 1)
                for h in range(2):
                    act.wait_ge(aT_psum, 2 * g + h + 1)
                    nc.scalar.activation(
                        attT[:, s, :, 2 * h * P:2 * (h + 1) * P].rearrange("p k (t n) -> p t k n", n=P),
                        TPa[h][:], ACT.Copy).then_inc(aT_ready, 1)

            def roots(i):
                def stage(r, s):
                    g = r * STEPS3 + s
                    act.wait_ge(var3, 2 * g + i + 1)
                    nc.scalar.activation(root[:, s, i], ve[:, s, i], ACT.Sqrt).then_inc(root3, 1)
                return stage

            def evac_xn(r, s):
                g = r * STEPS3 + s
                act.wait_ge(y_psum, g + 1)
                for h in range(2):
                    act.wait_ge(xT3_psum, 2 * g + h + 1)
                    tok = 2 * h * P
                    nc.scalar.activation(
                        attT[:, s, :, tok:tok + 2 * P].rearrange("p k (t n) -> p t k n", n=P),
                        TX[h][:], ACT.Copy).then_inc(xT3, 1)

            pipelined(act, ROUNDS, STEPS3, [(0, evac), (1, roots(0)), (1, roots(1)), (1, evac_xn)], peel=2)

        @block.sync
        def _(sp):
            for name, dst in (("w1", "W1"), ("w3", "W3")):
                for e in range(E):
                    sp.dma_start(sb[dst][:, e], dr[name][e].rearrange("(k p) n -> p k n", p=P)).then_inc(w_in, 16)
                sp.dma_start(sb[dst][:, E], dr["s" + name][0].rearrange("(k p) n -> p k n", p=P)).then_inc(w_in, 16)

            def store(r, s):
                g = r * STEPS3 + s
                sp.wait_ge(xn3, g + 1)
                sp.dma_start(dr["XN"].rearrange("(g t p) d -> g p t d", t=G, p=P)[g], xn[:, s]).then_inc(xn_stored[s], 16)
            pipelined(sp, ROUNDS, STEPS3, [(0, store)])
            for s in range(STEPS3):
                sp.wait_ge(xn_stored[s], 16 * ROUNDS)
            sp.wait_ge(w_in, 16 * 2 * (E + 1))

        @block.vector
        def _(v):
            v.wait_ge(rw_turned, 1)
            v.tensor_copy(sb["rwT"][:], Z[:, 0:KD, :]).then_inc(rw_ready, 1)
            dl = Link(v, l3, 1)
            nl = Link(v, l3b, 14)
            x4 = sb["x"][:].rearrange("p (g t) d -> p g t d", t=G)
            o4 = sb["O"][:].rearrange("p (b h c) j q d -> p b c j q h d", b=B, h=H)

            def divide(r, s):
                g = r * STEPS3 + s
                dl.start(g)
                b = r // 2
                o = o4[:, b, r % 2, s]
                wait(v, att_ready, g)
                dl(v.reciprocal(den[:], o[:, :, :, DH]))
                wait(v, aT_psum, 2 * (g - 1))
                a4 = att[:, s].rearrange("p q (h d) -> p q h d", d=DH)
                for q in range(G):
                    ins = v.tensor_tensor(a4[:, q], o[:, q, :, 0:DH], den[:, q].unsqueeze(2).to_broadcast([P, H, DH]),
                                          ALU.mult)
                ins.then_inc(att_ready, 1)

            def norm_stats(src, g, s, i):
                settle(v, sb["tick"])
                for t in range(G):
                    ins = v.bn_stats(bn[:, t, :], src(t))
                nl(ins)
                settle(v, sb["tick"])
                for t in range(G):
                    ins = v.bn_aggr(mv[:, t, :], bn[:, t, :])
                nl(ins)
                v.tensor_scalar(ve[:, s, i], mv[:, :, 1], EPS, None, ALU.add).then_inc(var3, 1)
                v.wait_ge(var3, 2 * g + i + 1)
                rstd_newton(nl, v, ve[:, s, i], root[:, s, i], rs[:], tm[:], root3, 2 * g + i + 1)

            def residual(r, s):
                g = r * STEPS3 + s
                nl.start(g)
                v.wait_ge(y_psum, g + 1)
                norm_stats(lambda t: Y[:, t, :], g, s, 0)
                for t in range(G):
                    ins = v.tensor_scalar(y[:, t, :], Y[:, t, :], mv[:, t, 0:1], rs[:, t:t + 1],
                                          ALU.subtract, ALU.mult)
                ins.then_inc(y_out, 1)
                v.wait_ge(y_out, g + 1)
                v.tensor_tensor(x4[:, g], x4[:, g], y[:], ALU.add).then_inc(x1_done, 1)
                v.wait_ge(x1_done, g + 1)
                norm_stats(lambda t: x4[:, g, t, :], g, s, 1)
                wait(v, xT3_psum, 2 * (g - 1))
                wait(v, xn_stored[s], 16 * r)
                for t in range(G):
                    ins = v.tensor_scalar(xn[:, s, t, :], x4[:, g, t, :], mv[:, t, 0:1], rs[:, t:t + 1],
                                          ALU.subtract, ALU.mult)
                ins.then_inc(xn3, 1)

            def keep_z(r, s):
                g = r * STEPS3 + s
                v.wait_ge(z_psum, g + 1)
                z4 = sb["z"][:].rearrange("p (g t) e -> p g t e", t=G)
                v.tensor_tensor(z4[:, g], Z[:], sb["rbias"][:].unsqueeze(1).to_broadcast([P, G, E]),
                                ALU.add).then_inc(z_out, 1)

            pipelined(v, ROUNDS, STEPS3, [(0, divide), (1, residual), (2, keep_z)], peel=2)


SLOT_TILES = TOPK * TILES + E
UNITS = TILES + SLOT_TILES


def dispatch(nc, dr, sb):
    with ExitStack() as ctx:
        def sem(name):
            return ctx.enter_context(nc.semaphore(name))

        def sbuf(name, shape, dt):
            return ctx.enter_context(nc.sbuf_tensor(name, shape, dt))
        best = sbuf("best", [P, TILES, 8], F32)
        bidx = sbuf("bidx", [P, TILES, 8], U32)
        bidf = sbuf("bidf", [P, TILES, TOPK], F32)
        gap = sbuf("gap", [P, TILES], F32)
        hot = sbuf("hot", [P, TOPK, TILES, E], F32)
        both = sbuf("both", [P, TILES, E], F32)
        before = sbuf("before", [P, P], F32)
        ones = sbuf("ones5", [P, P], F32)
        scan = sbuf("scan", [P, 2, TILES, E], F32)
        count_i = sbuf("count_i", [P, E], I32)
        ends = sbuf("ends", [P, E], F32)
        start = sbuf("start", [P, E], F32)
        pos = sbuf("pos", [P, TILES, E], F32)
        place = sbuf("place_f", [P, TOPK, TILES], F32)
        unit = sbuf("unit", [P, SLOT_TILES], F32)
        later = sbuf("later", [P, SLOT_TILES, E - 1], F32)
        eid = sbuf("eid_f", [P, SLOT_TILES], F32)
        zero_ids = sbuf("zero_ids", [P, SLOT_TILES], I32)
        RANK = ctx.enter_context(nc.psum_tensor("RANK", [P, TILES, E], F32))
        TOTAL = ctx.enter_context(nc.psum_tensor("TOTAL", [P, TILES, E], F32))
        link_s = sem("d_link")
        gap_ready = sem("gap_ready")
        gap_exp = sem("gap_exp")
        consts = sem("consts5")
        both_ready = sem("both_ready")
        ranked = sem("ranked")
        w_in = sem("w2_in")
        ids_zeroed = sem("ids_zeroed")
        tri = sem("tri")
        block = ctx.enter_context(nc.Block())

        @block.sync
        def _(sp):
            for e in range(E):
                sp.dma_start(sb["W2"][:, e], dr["w2"][e].rearrange("(k p) n -> p k n", p=P)).then_inc(w_in, 16)
            sp.dma_start(sb["W2"][:, E], dr["sw2"][0].rearrange("(k p) n -> p k n", p=P)).then_inc(w_in, 16)
            sp.wait_ge(consts, 1)
            sp.dma_start(dr["IDS"].rearrange("(p n) o -> p (n o)", p=P), zero_ids[:]).then_inc(ids_zeroed, 16)
            sp.wait_ge(ids_zeroed, 16)
            sp.wait_ge(w_in, 16 * (E + 1))

        @block.gpsimd
        def _(pool):
            pool.memset(zero_ids[:], 0).then_inc(consts, 1)
            pool.iota(sb["tok"][:], pattern=[[P, TILES]], base=0, channel_multiplier=1).then_inc(consts, 1)
            pool.iota(unit[:], pattern=[[1, SLOT_TILES]], base=0, channel_multiplier=0,
                      allow_small_or_imprecise_dtypes=True).then_inc(consts, 1)
            pool.memset(ones[:], 1.0).then_inc(consts, 1)
            pool.wait_ge(consts, 4)
            pool.affine_select(out=before[:], in_=ones[:], compare_op=ALU.is_gt, fill=0.0, base=0,
                               pattern=[[1, P]], channel_multiplier=-1).then_inc(tri, 1)

        @block.scalar
        def _(act):
            act.wait_ge(gap_ready, 1)
            nc.scalar.activation(gap[:], gap[:], ACT.Exp).then_inc(gap_exp, 1)

        @block.tensor
        def _(pe):
            pe.wait_ge(both_ready, 1)
            pe.wait_ge(tri, 1)
            flat = both[:].rearrange("p t e -> p (t e)")
            pe.matmul(RANK[:].rearrange("p t e -> p (t e)"), before[:], flat, start=True, stop=True)
            pe.matmul(TOTAL[:].rearrange("p t e -> p (t e)"), ones[:], flat, start=True,
                      stop=True).then_inc(ranked, 1)

        @block.vector
        def _(v):
            link = Link(v, link_s)
            z = sb["z"]
            wt = sb["wt"]
            for t in range(TILES):
                ins = v.max(best[:, t, :], z[:, t, :])
            link(ins)
            for t in range(TILES):
                ins = v.max_index(bidx[:, t, :], best[:, t, :], z[:, t, :])
            link(ins)
            v.tensor_tensor(gap[:], best[:, :, 1], best[:, :, 0], ALU.subtract).then_inc(gap_ready, 1)
            link(v.tensor_copy(bidf[:], bidx[:, :, 0:TOPK]))
            iota = sb["iota8"][:].unsqueeze(1).to_broadcast([P, TILES, E])
            for j in range(TOPK):
                link(v.tensor_tensor(hot[:, j], iota, bidf[:, :, j].unsqueeze(2).to_broadcast([P, TILES, E]),
                                     ALU.is_equal))
            v.tensor_tensor(both[:], hot[:, 0], hot[:, 1], ALU.add).then_inc(both_ready, 1)
            v.wait_ge(gap_exp, 1)
            link(v.tensor_scalar(wt[:, 0], gap[:], 1.0, None, ALU.add))
            link(v.reciprocal(wt[:, 0], wt[:, 0]))
            link(v.tensor_tensor(wt[:, 1], wt[:, 0], gap[:], ALU.mult))
            v.wait_ge(ranked, 1)
            link(v.tensor_copy(scan[:, 0], TOTAL[:]))
            i, d = 0, 1
            while d < TILES:
                link(v.tensor_copy(scan[:, 1 - i, 0:d], scan[:, i, 0:d]))
                link(v.tensor_tensor(scan[:, 1 - i, d:], scan[:, i, d:], scan[:, i, 0:TILES - d], ALU.add))
                i, d = 1 - i, 2 * d
            link(v.tensor_scalar(ends[:], scan[:, i, TILES - 1], float(P - 1), None, ALU.add))
            link(v.tensor_copy(count_i[:], ends[:]))
            link(v.tensor_scalar(count_i[:], count_i[:], P.bit_length() - 1, None, ALU.arith_shift_right))
            link(v.tensor_copy(ends[:], count_i[:]))
            link(v.memset(start[:], 0.0))
            for e in range(1, E):
                link(v.tensor_tensor(start[:, e:e + 1], start[:, e - 1:e], ends[:, e - 1:e], ALU.add))
            link(v.tensor_tensor(ends[:], start[:], ends[:], ALU.add))
            link(v.tensor_scalar(start[:], start[:], float(P), None, ALU.mult))
            link(v.tensor_tensor(pos[:], scan[:, i], TOTAL[:], ALU.subtract))
            link(v.tensor_tensor(pos[:], pos[:], RANK[:], ALU.add))
            link(v.tensor_tensor(pos[:], pos[:], start[:].unsqueeze(1).to_broadcast([P, TILES, E]), ALU.add))
            for j in range(TOPK):
                link(v.tensor_tensor(hot[:, j], hot[:, j], pos[:], ALU.mult))
                link(v.tensor_reduce(place[:, j], hot[:, j], AX.X, ALU.add))
            link(v.tensor_copy(sb["place"][:], place[:]))
            link(v.tensor_scalar(place[:], place[:], float(TILES * P), None, ALU.add))
            link(v.tensor_copy(sb["row"][:], place[:]))
            v.wait_ge(consts, 3)
            link(v.tensor_tensor(later[:], unit[:].unsqueeze(2).to_broadcast([P, SLOT_TILES, E - 1]),
                                 ends[:, 0:E - 1].unsqueeze(1).to_broadcast([P, SLOT_TILES, E - 1]), ALU.is_ge))
            link(v.tensor_reduce(eid[:], later[:], AX.X, ALU.add))
            link(v.tensor_copy(sb["eid"][:, TILES:], eid[:]))
            link(v.memset(sb["eid"][:, 0:TILES], E))


def experts(nc, dr, sb):
    with ExitStack() as ctx:
        def sem(name):
            return ctx.enter_context(nc.semaphore(name))

        def sbuf(name, shape, dt):
            return ctx.enter_context(nc.sbuf_tensor(name, shape, dt))
        KH = HID // P
        NX = 4
        W1, W3, W2 = sb["W1"], sb["W3"], sb["W2"]
        xs = [sbuf(f"xs{i}", [P, D], F32) for i in range(NX)]
        xsT = [sbuf(f"xsT{i}", [P, KD, P], F32) for i in range(2)]
        sg = [sbuf(f"sg{i}", [P, HID], F32) for i in range(2)]
        h = [sbuf(f"h{i}", [P, HID], F32) for i in range(2)]
        hT = [sbuf(f"hT{i}", [P, KH, P], F32) for i in range(2)]
        ys = [sbuf(f"ys{i}", [P, D], F32) for i in range(NX)]
        ids_row = sbuf("ids_row", [SLOT_TILES, P], I32)
        ids_f = sbuf("ids_f", [SLOT_TILES, P], F32)
        ids = sbuf("ids", [P, SLOT_TILES], U32)
        unit_ids = [sbuf(f"unit_ids{i}", [P, 1], U32) for i in range(NX)]
        XT = ctx.enter_context(nc.psum_tensor("XT", [P, KD, P], F32))
        GP = [ctx.enter_context(nc.psum_tensor(f"GP{i}", [P, HID], F32)) for i in range(2)]
        UP = [ctx.enter_context(nc.psum_tensor(f"UP{i}", [P, HID], F32)) for i in range(2)]
        HT = ctx.enter_context(nc.psum_tensor("HT", [P, KH, P], F32))
        Y = ctx.enter_context(nc.psum_tensor("Y5", [P, D], F32))
        IDT = ctx.enter_context(nc.psum_tensor("IDT", [P, SLOT_TILES], F32))
        x_in = [sem(f"x_in{i}") for i in range(NX)]
        x_gathered = [sem(f"x_gathered{i}") for i in range(NX)]
        x_turned = sem("x_turned")
        xsT_ready = sem("xsT_ready")
        g_psum = sem("g_psum")
        u_psum = sem("u_psum")
        silu_done = sem("silu_done")
        h_done = sem("h_done")
        h_turned = sem("h_turned")
        hT_ready = sem("hT_ready")
        y_psum = sem("y5_psum")
        y_out = sem("y5_out")
        y_stored = [sem(f"y_stored{i}") for i in range(NX)]
        scattered = sem("scattered")
        ids_loaded = sem("ids_loaded")
        ids_float = sem("ids_float")
        ids_turned = sem("ids_turned")
        ids_ready = sem("ids_ready")
        unit_ids_ready = sem("unit_ids_ready")
        STEPS5 = 4
        ROUNDS = UNITS // STEPS5
        IDS_ROUND = TILES // NX - 1
        block = ctx.enter_context(nc.Block())

        @block.sync
        def _(sp):
            def load(r, s):
                u = r * NX + s
                wait(sp, x_turned, u - NX + 1)
                sp.dma_start(xs[s][:], dr["XN"].rearrange("(u p) d -> u p d", p=P)[u]).then_inc(x_in[s], 16)

            def store(r, s):
                u = r * NX + s
                sp.wait_ge(y_out, u + 1)
                sp.dma_start(dr["YS"].rearrange("(u p) d -> u p d", p=P)[u], ys[s][:]).then_inc(y_stored[s], 16)
            both = [(0, load), (4, store)]
            pipelined(sp, IDS_ROUND, NX, both, peel=2, drain=False)
            sp.wait_ge(scattered, 16 * TOPK * TILES)
            sp.dma_start(ids_row[:], dr["IDS"].rearrange("(n p) o -> n (p o)", p=P)).then_inc(ids_loaded, 16)
            pipelined(sp, TILES // NX, NX, both, start=IDS_ROUND, drain=False)
            pipelined(sp, ROUNDS, NX, [(4, store)], start=TILES // NX)
            for i in range(NX):
                sp.wait_ge(y_stored[i], 16 * ROUNDS)

        @block.gpsimd
        def _(pool):
            for j in range(TOPK):
                for t in range(TILES):
                    pool.indirect_dma_start(
                        out=dr["IDS"], out_offset=bass.IndirectOffsetOnAxis(ap=sb["place"][:, j, t:t + 1], axis=0),
                        in_=sb["tok"][:, t:t + 1], in_offset=None).then_inc(scattered, 16)
            pool.wait_ge(ids_ready, 1)

            def gather(r, s):
                u = TILES + r * NX + s
                pool.wait_ge(x_turned, u - NX + 1)
                pool.tensor_copy(unit_ids[s][:], ids[:, bass.ds(r * NX + s, 1)]).then_inc(unit_ids_ready, 1)
                pool.wait_ge(unit_ids_ready, r * NX + s + 1)
                settle_pool(pool, sb["tick_pool"])
                pool.indirect_dma_start(
                    out=xs[s][:], out_offset=None, in_=dr["XN"],
                    in_offset=bass.IndirectOffsetOnAxis(ap=unit_ids[s][:], axis=0)).then_inc(x_gathered[s], 16)
            pipelined(pool, SLOT_TILES // NX, NX, [(0, gather)])

        @block.tensor
        def _(pe):
            def turn_loaded(r, s):
                pe.wait_ge(x_in[s], 16 * (r + 1))
                turn_x(r, s)

            def turn_gathered(r, s):
                pe.wait_ge(x_gathered[s], 16 * (r - TILES // NX + 1))
                turn_x(r, s)

            def turn_x(r, s):
                u = r * STEPS5 + s
                wait(pe, xsT_ready, u)
                for k in range(KD):
                    ins = pe.transpose(XT[:, k, :], xs[s][:, k * P:(k + 1) * P], sb["ident"][:])
                ins.then_inc(x_turned, 1)

            def up(r, s):
                u = r * STEPS5 + s
                e = pe.value_load(sb["eid"][0:1, bass.ds(u, 1)], min_val=0, max_val=E)
                pe.wait_ge(xsT_ready, u + 1)
                wait(pe, silu_done, u - 1)
                for k in range(KD):
                    ins = pe.matmul(GP[s % 2][:], xsT[s % 2][:, k, :], W1[:, e, k, :],
                                    start=(k == 0), stop=(k == KD - 1))
                ins.then_inc(g_psum, 1)
                wait(pe, h_done, u - 1)
                for k in range(KD):
                    ins = pe.matmul(UP[s % 2][:], xsT[s % 2][:, k, :], W3[:, e, k, :],
                                    start=(k == 0), stop=(k == KD - 1))
                ins.then_inc(u_psum, 1)

            def turn_h(r, s):
                u = r * STEPS5 + s
                pe.wait_ge(h_done, u + 1)
                wait(pe, hT_ready, u)
                for m in range(KH):
                    ins = pe.transpose(HT[:, m, :], h[s % 2][:, m * P:(m + 1) * P], sb["ident"][:])
                ins.then_inc(h_turned, 1)

            def down(r, s):
                u = r * STEPS5 + s
                e = pe.value_load(sb["eid"][0:1, bass.ds(u, 1)], min_val=0, max_val=E)
                pe.wait_ge(hT_ready, u + 1)
                wait(pe, y_out, u)
                for m in range(KH):
                    ins = pe.matmul(Y[:], hT[s % 2][:, m, :], W2[:, e, m, :], start=(m == 0), stop=(m == KH - 1))
                ins.then_inc(y_psum, 1)

            rest = [(1, up), (2, turn_h), (3, down)]
            pipelined(pe, IDS_ROUND, STEPS5, [(0, turn_loaded)] + rest, peel=2, drain=False)
            pe.wait_ge(ids_float, 1)
            pe.transpose(IDT[:], ids_f[:], sb["ident"][0:SLOT_TILES, 0:SLOT_TILES]).then_inc(ids_turned, 1)
            pipelined(pe, TILES // NX, STEPS5, [(0, turn_loaded)] + rest, start=IDS_ROUND, drain=False)
            pipelined(pe, ROUNDS, STEPS5, [(0, turn_gathered)] + rest, start=TILES // NX)

        @block.scalar
        def _(act):
            def copy_x(r, s):
                u = r * STEPS5 + s
                act.wait_ge(x_turned, u + 1)
                wait(act, u_psum, u - 1)
                nc.scalar.activation(xsT[s % 2][:], XT[:], ACT.Copy).then_inc(xsT_ready, 1)

            def silu(r, s):
                u = r * STEPS5 + s
                act.wait_ge(g_psum, u + 1)
                wait(act, h_done, u - 1)
                nc.scalar.activation(sg[s % 2][:], GP[s % 2][:], ACT.Silu).then_inc(silu_done, 1)

            def copy_h(r, s):
                u = r * STEPS5 + s
                act.wait_ge(h_turned, u + 1)
                wait(act, y_psum, u - 1)
                nc.scalar.activation(hT[s % 2][:], HT[:], ACT.Copy).then_inc(hT_ready, 1)
            pipelined(act, ROUNDS, STEPS5, [(0, copy_x), (1, silu), (2, copy_h)], peel=2)

        @block.vector
        def _(v):
            def gate(r, s):
                u = r * STEPS5 + s
                v.wait_ge(silu_done, u + 1)
                v.wait_ge(u_psum, u + 1)
                wait(v, h_turned, u - 1)
                v.tensor_tensor(h[s % 2][:], sg[s % 2][:], UP[s % 2][:], ALU.mult).then_inc(h_done, 1)

            def take_y(r, s):
                u = r * STEPS5 + s
                v.wait_ge(y_psum, u + 1)
                wait(v, y_stored[s], 16 * r)
                v.tensor_copy(ys[s][:], Y[:]).then_inc(y_out, 1)

            pipelined(v, IDS_ROUND, STEPS5, [(1, gate), (3, take_y)], peel=2, drain=False)
            v.wait_ge(ids_loaded, 16)
            v.tensor_copy(ids_f[:], ids_row[:]).then_inc(ids_float, 1)
            v.wait_ge(ids_turned, 1)
            v.tensor_copy(ids[:], IDT[:]).then_inc(ids_ready, 1)
            pipelined(v, ROUNDS, STEPS5, [(1, gate), (3, take_y)], start=IDS_ROUND)


def combine(nc, dr, sb):
    with ExitStack() as ctx:
        def sem(name):
            return ctx.enter_context(nc.semaphore(name))

        def sbuf(name, shape, dt):
            return ctx.enter_context(nc.sbuf_tensor(name, shape, dt))
        moe = sbuf("moe", [P, 2, G, D], F32)
        got = sbuf("got", [P, 2, TOPK, G, D], F32)
        bn = sbuf("bn6", [P, G, 6], F32)
        mv = sbuf("mv6", [P, 2, G, 2], F32)
        ve = sbuf("ve6", [P, 2, G], F32)
        root = sbuf("root6", [P, 2, G], F32)
        rs = sbuf("rs6", [P, G], F32)
        tm = sbuf("tm6", [P, G], F32)
        shared_in = [sem(f"shared_in{i}") for i in range(2)]
        routed_in = [sem(f"routed_in{i}") for i in range(2)]
        summed = sem("summed")
        rows_ready = sem("rows_ready")
        rows = [sbuf(f"rows{i}", [P, TOPK, G], U32) for i in range(2)]
        stats_link = sem("stats_link")
        norm_link = sem("norm_link")
        var6 = sem("var6")
        root6 = sem("root6s")
        rs_ready = sem("rs6_ready")
        scaled = sem("scaled")
        out_ready = sem("out_ready")
        out_stored = sem("out_stored")
        ROUNDS = GROUPS // 2
        block = ctx.enter_context(nc.Block())

        @block.sync
        def _(sp):
            def load(r, s):
                g = r * 2 + s
                wait(sp, out_ready, g - 1)
                sp.dma_start(moe[:, s], dr["YS"][0:T].rearrange("(g t p) d -> g p t d", t=G, p=P)[g]).then_inc(
                    shared_in[s], 16)

            def store(r, s):
                g = r * 2 + s
                sp.wait_ge(out_ready, g + 1)
                sp.dma_start(dr["out"].rearrange("b (g t p) d -> (b g) p t d", t=G, p=P)[g],
                             sb["x"][:].rearrange("p (g t) d -> p g t d", t=G)[:, g]).then_inc(out_stored, 16)
            pipelined(sp, ROUNDS, 2, [(0, load), (2, store)], peel=2)
            sp.wait_ge(out_stored, 16 * GROUPS)

        @block.gpsimd
        def _(pool):
            def gather(r, s):
                g = r * 2 + s
                wait(pool, summed, g - 1)
                pool.tensor_copy(rows[s][:], sb["row"][:, :, bass.ds(g * G, G)]).then_inc(rows_ready, 1)
                pool.wait_ge(rows_ready, g + 1)
                settle_pool(pool, sb["tick_pool"])
                for j in range(TOPK):
                    for t in range(G):
                        pool.indirect_dma_start(
                            out=got[:, s, j, t, :], out_offset=None, in_=dr["YS"],
                            in_offset=bass.IndirectOffsetOnAxis(ap=rows[s][:, j, t:t + 1], axis=0)
                        ).then_inc(routed_in[s], 16)
            pipelined(pool, ROUNDS, 2, [(0, gather)], peel=2)

        @block.scalar
        def _(act):
            def roots(r, s):
                act.wait_ge(var6, r * 2 + s + 1)
                nc.scalar.activation(root[:, s], ve[:, s], ACT.Sqrt).then_inc(root6, 1)
            pipelined(act, ROUNDS, 2, [(0, roots)], peel=2)

        @block.vector
        def _(v):
            sl = Link(v, stats_link, 3)
            nl = Link(v, norm_link, 4)
            x4 = sb["x"][:].rearrange("p (g t) d -> p g t d", t=G)

            def sums(r, s):
                g = r * 2 + s
                sl.start(g)
                v.wait_ge(shared_in[s], 16 * (r + 1))
                v.wait_ge(routed_in[s], 16 * TOPK * G * (r + 1))
                for j in range(TOPK):
                    for t in range(G):
                        ins = v.scalar_tensor_tensor(moe[:, s, t, :], got[:, s, j, t, :],
                                                     sb["wt"][:, j, bass.ds(g * G + t, 1)], moe[:, s, t, :],
                                                     ALU.mult, ALU.add)
                    if j == 0:
                        sl(ins)
                ins.then_inc(summed, 1)
                v.wait_ge(summed, g + 1)
                settle(v, sb["tick"])
                for t in range(G):
                    ins = v.bn_stats(bn[:, t, :], moe[:, s, t, :])
                sl(ins)
                settle(v, sb["tick"])
                for t in range(G):
                    ins = v.bn_aggr(mv[:, s, t, :], bn[:, t, :])
                sl(ins)
                v.tensor_scalar(ve[:, s], mv[:, s, :, 1], EPS, None, ALU.add).then_inc(var6, 1)

            def norm(r, s):
                g = r * 2 + s
                nl.start(g)
                v.wait_ge(root6, g + 1)
                nl(v.reciprocal(rs[:], root[:, s]))
                nl(v.tensor_tensor(tm[:], rs[:], rs[:], ALU.mult))
                nl(v.tensor_tensor(tm[:], tm[:], ve[:, s], ALU.mult))
                nl(v.tensor_scalar(tm[:], tm[:], -0.5, 1.5, ALU.mult, ALU.add))
                v.tensor_tensor(rs[:], rs[:], tm[:], ALU.mult).then_inc(rs_ready, 1)
                v.wait_ge(rs_ready, g + 1)
                for t in range(G):
                    ins = v.tensor_scalar(moe[:, s, t, :], moe[:, s, t, :], mv[:, s, t, 0:1], rs[:, t:t + 1],
                                          ALU.subtract, ALU.mult)
                ins.then_inc(scaled, 1)
                v.wait_ge(scaled, g + 1)
                v.tensor_tensor(x4[:, g], x4[:, g], moe[:, s], ALU.add).then_inc(out_ready, 1)

            pipelined(v, ROUNDS, 2, [(0, sums), (1, norm)], peel=2)


def build(nc, dr):
    with ExitStack() as ctx:
        def sbuf(name, shape, dt):
            return ctx.enter_context(nc.sbuf_tensor(name, shape, dt))
        dr["QT"] = nc.dram_tensor("QT", (H * QR, T), BF16, kind="Internal").ap()
        dr["KT"] = nc.dram_tensor("KT", (H * KR, T), F16, kind="Internal").ap()
        dr["VD"] = nc.dram_tensor("VD", (P, H, GROUPS, G * VW), BF16, kind="Internal").ap()
        dr["VF"] = nc.dram_tensor("VF", (P, H, GROUPS, G * VU), F32, kind="Internal").ap()
        dr["XN"] = nc.dram_tensor("XN", (T, D), F32, kind="Internal").ap()
        dr["IDS"] = nc.dram_tensor("IDS", (SLOT_TILES * P, 1), I32, kind="Internal").ap()
        dr["YS"] = nc.dram_tensor("YS", (UNITS * P, D), F32, kind="Internal").ap()
        dr["SH"] = nc.dram_tensor("SH", (SROWS, B * H, S), BF16, kind="Internal").ap()
        sb = {
            "x": sbuf("x", [P, TILES, D], F32),
            "wproj": sbuf("wproj", [P, KD, D], F32),
            "rw": sbuf("rw", [E, D], F32),
            "rwT": sbuf("rwT", [P, KD, E], F32),
            "rbias": sbuf("rbias", [P, E], F32),
            "ident": sbuf("ident", [P, P], F32),
            "ident_b": sbuf("ident_b", [P, P], BF16),
            "ident_h": sbuf("ident_h", [P, P], F16),
            "sel": sbuf("sel", [P, 2 * VU], F32),
            "iota8": sbuf("iota8", [P, E], F32),
            "z": sbuf("z", [P, TILES, E], F32),
            "wt": sbuf("wt", [P, TOPK, TILES], F32),
            "place": sbuf("place", [P, TOPK, TILES], U32),
            "row": sbuf("row", [P, TOPK, TILES], U32),
            "tok": sbuf("tok", [P, TILES], I32),
            "eid": sbuf("eid", [P, UNITS], I32),
            "guard": sbuf("guard", [P, 1], F32),
            "tick": sbuf("tick", [P, 1], F32),
            "tick_pool": sbuf("tick_pool", [P, 2], F32),
        }
        with ExitStack() as early:
            def esb(name, shape, dt):
                return early.enter_context(nc.sbuf_tensor(name, shape, dt))
            sb["wqkv"] = esb("wqkv", [P, KD, 3 * D], F32)
            sb["gain"] = esb("gain", [P, 2 * D], F32)
            sb["bias"] = esb("bias", [P, 2 * D], F32)
            setup(nc, dr, sb)
            project_qkv(nc, dr, sb)
        import numpy as np
        safe = int(np.float32(SAFE).view(np.int32))
        bound = nc.values_load(sb["guard"][0:1, 0:1].bitcast(I32))
        with nc.If(bound > safe):
            true_maxima(nc, dr, sb)
        sb["O"] = sbuf("O", [P, B * H * 2, 2, QC // P, VU], F32)
        attention(nc, dr, sb)
        sb["W1"] = sbuf("W1", [P, E + 1, KD, HID], F32)
        sb["W3"] = sbuf("W3", [P, E + 1, KD, HID], F32)
        project_and_route(nc, dr, sb)
        sb["W2"] = sbuf("W2", [P, E + 1, HID // P, D], F32)
        dispatch(nc, dr, sb)
        experts(nc, dr, sb)
        combine(nc, dr, sb)


_INS = ["L0_attn_x", "L0_attn_w_qkv", "L0_attn_w_proj", "L0_attn_q_gamma", "L0_attn_q_beta", "L0_attn_k_gamma",
        "L0_attn_k_beta", "L0_ffn_router_w", "L0_ffn_experts_bias", "L0_ffn_w1", "L0_ffn_w3", "L0_ffn_w2",
        "L0_ffn_sw1", "L0_ffn_sw3", "L0_ffn_sw2"]


def kernel(**inputs):
    import numpy as np
    import concourse.bacc as bacc
    from concourse.bass_utils import run_bass_kernel_spmd

    nc = bacc.Bacc("TRN2", target_bir_lowering=False, num_devices=1)
    arrays, dr = {}, {}
    for name in _INS:
        a = np.ascontiguousarray(inputs[name])
        arrays[f"in_{name}"] = a
        short = name.replace("L0_attn_", "").replace("L0_ffn_", "")
        dr[short] = nc.dram_tensor(f"in_{name}", a.shape, mybir.dt.from_np(a.dtype), kind="ExternalInput").ap()
    dr["out"] = nc.dram_tensor("out_0", (B, S, D), F32, kind="ExternalOutput").ap()
    build(nc, dr)
    r = run_bass_kernel_spmd(nc, [arrays], core_ids=[0])
    return r.results[0]["out_0"]
```

```python
from contextlib import ExitStack

import concourse.bass as bass
import numpy as np
from concourse import mybir

F32 = mybir.dt.float32
BF16 = mybir.dt.bfloat16
F16 = mybir.dt.float16
I32 = mybir.dt.int32
U32 = mybir.dt.uint32
ALU = mybir.AluOpType
ACT = mybir.ActivationFunctionType
AX = mybir.AxisListType
RMAX = bass.bass_isa.ReduceOp.max

P = 128
B, S, D = 2, 2048, 256
H, DH = 16, 16
E, HID = 8, 512
TOPK = 2
EPS = 1e-5
T = B * S
TILES = T // P
KD = D // P
G = 4
GT = G * P
GROUPS = TILES // G
G1 = 2
GT1 = G1 * P
GROUPS1 = TILES // G1
QR = 3 * DH
KR = 2 * DH
PAIR = 6 * DH
SROWS = 3
CROWS = PAIR + SROWS
VW = 64
VU = DH + 1
VP = (0, DH + 2, 2 * DH + 2)
KSCALE = 2.0 ** 12
TOP = 15 * 0.6931471805599453
SAFE = 11.0


def wait(eng, sem, value):
    if isinstance(value, int) and value <= 0:
        return
    eng.wait_ge(sem, value)


def pipelined(eng, stop, steps, stages, peel=0, start=0, drain=True):
    def step(r, s):
        for lag, stage in stages:
            back = (lag - s + steps - 1) // steps if lag > s else 0
            if not isinstance(r, int) or r >= back:
                stage(r - back if back else r, s - lag + back * steps)
    for r in range(start, start + peel):
        for s in range(steps):
            step(r, s)
    start += peel
    if start < stop:
        with eng.Fori(start, stop) as r:
            for s in range(steps):
                step(r, s)
    if drain:
        for s in range(max(lag for lag, _ in stages)):
            for lag, stage in stages:
                if s < lag:
                    stage(stop + (s - lag) // steps, (s - lag) % steps)


class Link:

    def __init__(self, eng, sem, per_step=0):
        self.eng, self.sem, self.per_step, self.base, self.n = eng, sem, per_step, 0, 0

    def start(self, step):
        assert self.n in (0, self.per_step), self.n
        self.base, self.n = step * self.per_step, 0

    def __call__(self, ins):
        self.n += 1
        ins.then_inc(self.sem, 1)
        self.eng.wait_ge(self.sem, self.base + self.n)


def settle(v, tick):
    v.memset(tick[:], 0.0)


def settle_pool(pool, tick):
    pool.tensor_tensor(tick[:, 0:1], tick[:, 1:2], tick[:, 1:2], ALU.add)


def rstd_newton(link, v, var, root, out, tmp, ready_sem, ready_value):
    v.wait_ge(ready_sem, ready_value)
    link(v.reciprocal(out, root))
    link(v.tensor_tensor(tmp, out, out, ALU.mult))
    link(v.tensor_tensor(tmp, tmp, var, ALU.mult))
    link(v.tensor_scalar(tmp, tmp, -0.5, 1.5, ALU.mult, ALU.add))
    link(v.tensor_tensor(out, out, tmp, ALU.mult))


def setup(nc, dr, sb):
    with ExitStack() as ctx:
        def sem(name):
            return ctx.enter_context(nc.semaphore(name))
        wmean = ctx.enter_context(nc.sbuf_tensor("wmean", [P, KD, 2 * H], F32))
        t0 = ctx.enter_context(nc.sbuf_tensor("t0", [P, 2, DH], F32))
        a = ctx.enter_context(nc.sbuf_tensor("a", [P, 4], F32))
        bn = ctx.enter_context(nc.sbuf_tensor("bn", [P, TILES, 6], F32))
        ve = ctx.enter_context(nc.sbuf_tensor("ve", [P, TILES], F32))
        root = ctx.enter_context(nc.sbuf_tensor("root", [P, TILES], F32))
        tm = ctx.enter_context(nc.sbuf_tensor("tm", [P, TILES], F32))
        CHUNKS = 4
        CT = TILES // CHUNKS
        x_loaded = [sem(f"x_loaded{i}") for i in range(CHUNKS)]
        w_loaded = sem("w_loaded")
        gb_loaded = sem("gb_loaded")
        rest_loaded = sem("rest_loaded")
        zeroed = sem("zeroed")
        ident_made = sem("ident_made")
        setup_link = sem("setup_link")
        x_var = sem("x_var")
        x_root = sem("x_root")
        block = ctx.enter_context(nc.Block())

        @block.sync
        def _(sp):
            for i, name in enumerate(("q_gamma", "q_beta", "k_gamma", "k_beta")):
                sp.dma_start(sb["gb"][:, i, :], dr[name].partition_broadcast(P)).then_inc(gb_loaded, 16)
            xb = dr["x"].rearrange("b (c t p) d -> (b c) p t d", t=CT, p=P)
            for c in range(CHUNKS):
                sp.dma_start(sb["x"][:, c * CT:(c + 1) * CT, :], xb[c]).then_inc(x_loaded[c], 16)
                if c == 0:
                    sp.dma_start(sb["wqkv"][:], dr["w_qkv"].rearrange("(k p) n -> p k n", p=P)).then_inc(w_loaded, 16)
            sp.dma_start(sb["wproj"][:], dr["w_proj"].rearrange("(k p) n -> p k n", p=P)).then_inc(rest_loaded, 16)
            sp.dma_start(sb["rw"][:], dr["router_w"]).then_inc(rest_loaded, 16)
            sp.dma_start(sb["rbias"][:], dr["experts_bias"].partition_broadcast(P)).then_inc(rest_loaded, 16)
            sp.wait_ge(rest_loaded, 16 * 3)

        @block.gpsimd
        def _(pool):
            pool.memset(sb["ident"][:], 0.0).then_inc(zeroed, 1)
            pool.memset(sb["spread"][:], 0.0).then_inc(zeroed, 1)
            pool.memset(sb["sums"][:], 1.0 / DH).then_inc(zeroed, 1)
            pool.memset(sb["sel"][:], 0.0).then_inc(zeroed, 1)
            pool.memset(sb["tick_pool"][:], 0.0)
            pool.iota(sb["iota8"][:], pattern=[[1, E]], base=0, channel_multiplier=0,
                      allow_small_or_imprecise_dtypes=True).then_inc(ident_made, 1)
            pool.wait_ge(zeroed, 4)
            pool.affine_select(out=sb["ident"][:], in_=sb["ident"][:], compare_op=ALU.not_equal, fill=1.0,
                               base=0, pattern=[[-1, P]], channel_multiplier=1).then_inc(ident_made, 1)
            spread = sb["spread"][:].rearrange("p m (h d) -> p m h d", d=DH)
            pool.affine_select(out=spread, in_=spread, compare_op=ALU.not_equal, fill=1.0, base=0,
                               pattern=[[-32, 2 * KD], [-1, P // DH], [0, DH]],
                               channel_multiplier=1).then_inc(ident_made, 1)
            pool.affine_select(out=sb["sums"][:], in_=sb["sums"][:], compare_op=ALU.is_ge, fill=0.0, base=0,
                               pattern=[[-DH, 32]], channel_multiplier=1).then_inc(ident_made, 1)
            pool.wait_ge(ident_made, 4)
            pool.affine_select(out=sb["sums"][:], in_=sb["sums"][:], compare_op=ALU.is_ge, fill=0.0,
                               base=DH - 1, pattern=[[DH, 32]], channel_multiplier=-1).then_inc(ident_made, 1)
            n = 5
            for j in range(2):
                cols = sb["sel"][:, VU * j:VU * j + DH]
                for i in range(3):
                    pool.wait_ge(ident_made, n)
                    pool.affine_select(out=cols, in_=cols, compare_op=ALU.not_equal, fill=1.0,
                                       base=-(VW * j + VP[i]), pattern=[[-1, DH]],
                                       channel_multiplier=1).then_inc(ident_made, 1)
                    n += 1
                one = sb["sel"][:, VU * j + DH:VU * j + VU]
                pool.affine_select(out=one, in_=one, compare_op=ALU.not_equal, fill=1.0,
                                   base=-(VW * j + DH), pattern=[[-1, 1]],
                                   channel_multiplier=1).then_inc(ident_made, 1)
                n += 1

        @block.scalar
        def _(act):
            act.wait_ge(x_var, 1)
            nc.scalar.activation(root[:], ve[:], ACT.Sqrt).then_inc(x_root, 1)

        @block.vector
        def _(v):
            link = Link(v, setup_link)
            gb = sb["gb"]
            v.wait_ge(gb_loaded, 64)
            link(v.scalar_tensor_tensor(t0[:], gb[:, 2:4, :], -1.0, gb[:, 2:4, :], ALU.mult, ALU.max))
            link(v.scalar_tensor_tensor(t0[:, 0], t0[:, 0], 4.0, t0[:, 1], ALU.mult, ALU.add))
            link(v.tensor_reduce(a[:, 0:1], t0[:, 0], AX.X, ALU.max))
            link(v.tensor_scalar(a[:, 0:1], a[:, 0:1], 1e-30, None, ALU.max))
            link(v.tensor_scalar(a[:, 1:2].bitcast(I32), a[:, 0:1].bitcast(I32), 0x7F800000, None,
                                 ALU.bitwise_and))
            link(v.reciprocal(a[:, 2:3], a[:, 1:2]))
            link(v.tensor_scalar(a[:, 2:3], a[:, 2:3], KSCALE, None, ALU.mult))
            link(v.tensor_scalar(a[:, 3:4], a[:, 1:2], 1.0 / (KSCALE * DH ** 0.5), None, ALU.mult))
            for i in range(4):
                link(v.tensor_scalar(gb[:, i, :], gb[:, i, :], a[:, 3:4] if i < 2 else a[:, 2:3], None, ALU.mult))
            v.wait_ge(ident_made, 3)
            v.tensor_copy(sb["ident_b"][:], sb["ident"][:])
            for m in range(2 * KD):
                spread = sb["spread"][:, m].rearrange("p (h d) -> p h d", d=DH)
                gain = gb[:, m // KD * 2, :].unsqueeze(1).to_broadcast([P, P // DH, DH])
                link(v.tensor_tensor(spread, spread, gain, ALU.mult))
            v.wait_ge(w_loaded, 16)
            w = sb["wqkv"][:, :, 0:2 * D].rearrange("p k (h d) -> p k h d", d=DH)
            link(v.tensor_reduce(wmean[:], w, AX.X, ALU.add))
            link(v.tensor_scalar(wmean[:], wmean[:], 1.0 / DH, None, ALU.mult))
            for k in range(KD):
                link(v.tensor_tensor(w[:, k], w[:, k], wmean[:, k].unsqueeze(2).to_broadcast([P, 2 * H, DH]),
                                     ALU.subtract))
            for c in range(CHUNKS):
                v.wait_ge(x_loaded[c], 16)
                for t in range(c * CT, (c + 1) * CT):
                    ins = v.bn_stats(bn[:, t, :], sb["x"][:, t, :])
            link(ins)
            for t in range(TILES):
                ins = v.bn_aggr(sb["mv"][:, t, :], bn[:, t, :])
            link(ins)
            v.tensor_scalar(ve[:], sb["mv"][:, :, 1], EPS, None, ALU.add).then_inc(x_var, 1)
            v.wait_ge(x_var, 1)
            rstd_newton(link, v, ve[:], root[:], sb["rs"][:], tm[:], x_root, 1)


def project_qkv(nc, dr, sb):
    with ExitStack() as ctx:
        def sem(name):
            return ctx.enter_context(nc.semaphore(name))

        def sbuf(name, shape, dt):
            return ctx.enter_context(nc.sbuf_tensor(name, shape, dt))

        xn = sbuf("xn", [P, 2, G1, D], F32)
        xnT = sbuf("xnT", [P, 2, KD, GT1], F32)
        C = [[sbuf(f"C{i}{h}", [P, KD, GT1], F32) for h in range(2)] for i in range(2)]
        sq = [[sbuf(f"sq{i}{h}", [P, KD, GT1], F32) for h in range(2)] for i in range(2)]
        Y = [sbuf(f"Y1{h}", [P, KD, GT1], F32) for h in range(2)]
        V32 = [sbuf(f"V32_1{i}", [P, H, G1, VU], F32) for i in range(2)]
        VT = [sbuf(f"VT{i}", [P, H, G1, VW], BF16) for i in range(2)]
        hv = sbuf("hv", [P, GT1], F32)
        root = sbuf("hroot", [P, 2, GT1], F32)
        hy = sbuf("hy", [P, GT1], F32)
        ht = sbuf("ht", [P, GT1], F32)
        hr = sbuf("hr", [P, 2, GT1], F32)
        rest = sbuf("rest", [P, KD, GT1], F32)
        vrest = sbuf("vrest", [P, H, G1, DH], F32)
        QP = [sbuf(f"QP{i}", [P, 3, KD, GT1], BF16) for i in range(2)]
        KP = [sbuf(f"KP{i}", [P, 2, KD, GT1], F16) for i in range(2)]
        brow = sbuf("brow", [P, 2, P], F32)
        bcol = sbuf("bcol", [P, 2], F32)
        ksum = sbuf("ksum", [P, KD, GROUPS1], F32)
        stat = sbuf("stat", [P, 1], F32)
        kmean = sbuf("kmean", [P, 1], F32)
        gs = sbuf("gs", [P, 4, DH], F32)
        fin = sbuf("fin", [P, 16], F32)
        ks2 = sbuf("ks2", [P, KD * B], F32)
        shift = sbuf("shift", [B * H, SROWS, S], BF16)
        XP = [ctx.enter_context(nc.psum_tensor(f"XP{i}", [P, KD, GT1], F32)) for i in range(2)]
        QK = [ctx.enter_context(nc.psum_tensor(f"QK{i}", [P, KD, GT1], F32)) for i in range(2)]
        RS = [ctx.enter_context(nc.psum_tensor(f"RS{i}", [P, KD, GT1], F32)) for i in range(2)]
        VPS = ctx.enter_context(nc.psum_tensor("VPS", [P, G1, D], F32))
        VAR = ctx.enter_context(nc.psum_tensor("VAR", [P, GT1], F32))

        biases = sem("biases")
        bias_turned = sem("bias_turned")
        xn_ready = sem("xn_ready")
        xT_psum = sem("xT_psum")
        xT_ready = sem("xT_ready")
        qk_psum = sem("qk_psum")
        qk_taken = sem("qk_taken")
        v_psum = sem("v_psum")
        v_taken = sem("v_taken")
        var_psum = sem("var_psum")
        hv_done = sem("hv_done")
        root_done = sem("root_done")
        hr_ready = sem("hr_ready")
        rs_psum = sem("rs_psum")
        mult_done = sem("mult_done")
        q_hi = sem("q_hi")
        k_hi = sem("k_hi")
        rest_done = sem("rest_done")
        k_lo = sem("k_lo")
        q_mid = sem("q_mid")
        q_lo = sem("q_lo")
        v_hi = sem("v_hi")
        vrest_ready = sem("vrest_ready")
        v_mid = sem("v_mid")
        v_lo = sem("v_lo")
        v32_stored = [sem(f"v32_stored{i}") for i in range(2)]
        v_stored = [sem(f"v_stored{i}") for i in range(2)]
        qk_stored = [sem(f"qk_stored{i}") for i in range(2)]
        ones_set = sem("ones_set")
        stat_ready = sem("stat_ready")
        reduced = sem("reduced")
        squared = sem("squared")
        rooted = sem("rooted")
        shift_ready = sem("shift_ready")
        shift_stored = sem("shift_stored")
        fin_link = sem("fin_link")
        newton = sem("newton")
        ROUNDS, STEPS = GROUPS1 // 2, 2
        block = ctx.enter_context(nc.Block())

        @block.tensor
        def _(pe):
            pe.wait_ge(biases, 2)
            for i in range(2):
                ins = pe.transpose(RS[0][:, i, 0:P], brow[:, i, :], sb["ident"][:])
            ins.then_inc(bias_turned, 1)
            pe.wait_ge(biases, 3)

            def turn_x(r, s):
                g = r * STEPS + s
                pe.wait_ge(xn_ready, g + 1)
                wait(pe, xT_ready, g - 1)
                for t in range(G1):
                    for k in range(KD):
                        ins = pe.transpose(XP[s][:, k, t * P:(t + 1) * P], xn[:, s, t, k * P:(k + 1) * P],
                                           sb["ident"][:])
                ins.then_inc(xT_psum, 1)

            def spread(r, s):
                g = r * STEPS + s
                pe.wait_ge(hr_ready, g + 1)
                for h in range(2):
                    wait(pe, mult_done, 2 * g + h - 1)
                    for m in range(KD):
                        ins = pe.matmul(RS[h][:, m, :], sb["spread"][:, h * KD + m, :], hr[:, s, :],
                                        start=True, stop=True)
                    ins.then_inc(rs_psum, 1)

            def qk(r, s):
                g = r * STEPS + s
                pe.wait_ge(xT_ready, g + 1)
                for h in range(2):
                    wait(pe, qk_taken, 2 * g + h - 1)
                    for m in range(KD):
                        col = h * D + m * P
                        for k in range(KD):
                            ins = pe.matmul(QK[h][:, m, :], sb["wqkv"][:, k, col:col + P], xnT[:, s, k, :],
                                            start=(k == 0), stop=(k == KD - 1))
                    ins.then_inc(qk_psum, 1)

            def values(r, s):
                g = r * STEPS + s
                wait(pe, v_taken, g)
                for t in range(G1):
                    for k in range(KD):
                        ins = pe.matmul(VPS[:, t, :], xnT[:, s, k, t * P:(t + 1) * P],
                                        sb["wqkv"][:, k, 2 * D:3 * D], start=(k == 0), stop=(k == KD - 1))
                ins.then_inc(v_psum, 1)

            def variances(r, s):
                g = r * STEPS + s
                pe.wait_ge(qk_taken, 2 * g + 2)
                wait(pe, hv_done, g)
                for m in range(2 * KD):
                    ins = pe.matmul(VAR[32 * m:32 * (m + 1), :], sb["sums"][:], sq[s][m // KD][:, m % KD, :],
                                    start=True, stop=True)
                ins.then_inc(var_psum, 1)

            pipelined(pe, ROUNDS, STEPS, [(4, spread), (1, turn_x), (2, qk), (2, values), (2, variances)], peel=3)

        @block.scalar
        def _(act):
            def roots(r, s):
                g = r * STEPS + s
                act.wait_ge(hv_done, g + 1)
                wait(act, hr_ready, g - 1)
                nc.scalar.activation(root[:, s], hv[:], ACT.Sqrt).then_inc(root_done, 1)

            def take_x(r, s):
                g = r * STEPS + s
                act.wait_ge(xT_psum, g + 1)
                wait(act, v_psum, g - 1)
                nc.scalar.activation(xnT[:, s], XP[s][:], ACT.Copy).then_inc(xT_ready, 1)

            def take_qk(r, s):
                g = r * STEPS + s
                wait(act, var_psum, g - 1)
                for h in range(2):
                    act.wait_ge(qk_psum, 2 * g + h + 1)
                    wait(act, mult_done, 2 * g + h - 3)
                    nc.scalar.activation(sq[s][h][:], QK[h][:], ACT.Square)
                    nc.scalar.activation(C[s][h][:], QK[h][:], ACT.Copy).then_inc(qk_taken, 1)

            def take_v(r, s):
                g = r * STEPS + s
                act.wait_ge(v_psum, g + 1)
                wait(act, vrest_ready, g - 1)
                wait(act, v32_stored[s], 16 * r)
                nc.scalar.activation(V32[s][:, :, :, 0:DH].rearrange("p h t d -> p t h d"),
                                     VPS[:].rearrange("p t (h d) -> p t h d", d=DH), ACT.Copy).then_inc(v_taken, 1)

            def v_high(r, s):
                g = r * STEPS + s
                act.wait_ge(v_taken, g + 1)
                wait(act, v_stored[s], 16 * r)
                nc.scalar.activation(VT[s][:, :, :, 0:DH], V32[s][:, :, :, 0:DH], ACT.Copy).then_inc(v_hi, 1)

            def v_middle(r, s):
                g = r * STEPS + s
                act.wait_ge(vrest_ready, g + 1)
                nc.scalar.activation(VT[s][:, :, :, VP[1]:VP[1] + DH], vrest[:], ACT.Copy).then_inc(v_mid, 1)

            def high(r, s):
                g = r * STEPS + s
                wait(act, qk_stored[s], 32 * r)
                act.wait_ge(mult_done, 2 * g + 1)
                nc.scalar.activation(QP[s][:, 0], Y[0][:], ACT.Identity, bias=bcol[:, 0:1]).then_inc(q_hi, 1)
                act.wait_ge(mult_done, 2 * g + 2)
                for m in range(KD):
                    ins = nc.scalar.activation(KP[s][:, 0, m], Y[1][:, m], ACT.Identity, bias=bcol[:, 1:2],
                                               accum_out=ksum[:, m, bass.ds(g, 1)])
                ins.then_inc(k_hi, 1)

            act.wait_ge(ones_set, 4)
            pipelined(act, ROUNDS, STEPS, [(3, roots), (1, take_x), (3, v_high), (4, high), (3, v_middle),
                                           (2, take_qk), (2, take_v)], peel=3)
            act.wait_ge(squared, 1)
            nc.scalar.activation(fin[:, 4:8], fin[:, 0:4], ACT.Sqrt).then_inc(rooted, 1)

        @block.vector
        def _(v):
            link = Link(v, fin_link)
            for i in range(2):
                v.tensor_copy(brow[:, i].rearrange("p (h d) -> p h d", d=DH),
                              sb["gb"][:, 2 * i + 1, :].unsqueeze(1).to_broadcast([P, P // DH, DH])
                              ).then_inc(biases, 1)
            for i in range(2):
                v.memset(VT[i][:], 0.0).then_inc(ones_set, 1)
            v.wait_ge(ones_set, 2)
            for i in range(2):
                v.memset(VT[i][:, :, :, DH:VU], 1.0)
                v.memset(V32[i][:, :, :, DH:VU], 1.0).then_inc(ones_set, 1)
            v.wait_ge(bias_turned, 1)
            v.tensor_copy(bcol[:], RS[0][:, :, 0]).then_inc(biases, 1)
            nl = Link(v, newton, 4)

            def norm_x(r, s):
                g = r * STEPS + s
                wait(v, xT_psum, g - 1)
                for t in range(G1):
                    tile = bass.ds(g * G1 + t, 1)
                    ins = v.tensor_scalar(xn[:, s, t, :], sb["x"][:, g * G1 + t, :], sb["mv"][:, tile, 0],
                                          sb["rs"][:, tile], ALU.subtract, ALU.mult)
                ins.then_inc(xn_ready, 1)

            def variances(r, s):
                g = r * STEPS + s
                v.wait_ge(var_psum, g + 1)
                wait(v, hr_ready, g)
                v.tensor_scalar(hv[:], VAR[:], EPS, None, ALU.add).then_inc(hv_done, 1)

            def deviations(r, s):
                g = r * STEPS + s
                nl.start(g)
                v.wait_ge(hv_done, g + 1)
                v.wait_ge(root_done, g + 1)
                nl(v.reciprocal(hy[:], root[:, s]))
                nl(v.tensor_tensor(ht[:], hy[:], hy[:], ALU.mult))
                nl(v.tensor_tensor(ht[:], ht[:], hv[:], ALU.mult))
                nl(v.tensor_scalar(ht[:], ht[:], -0.5, 1.5, ALU.mult, ALU.add))
                wait(v, rs_psum, 2 * (g - 1))
                v.tensor_tensor(hr[:, s], hy[:], ht[:], ALU.mult).then_inc(hr_ready, 1)
                v.wait_ge(hr_ready, g + 1)

            def multiply(r, s):
                g = r * STEPS + s
                for h, used in ((0, rest_done), (1, k_lo)):
                    v.wait_ge(rs_psum, 2 * g + h + 1)
                    wait(v, used, g)
                    v.tensor_tensor(Y[h][:], C[s][h][:], RS[h][:], ALU.mult).then_inc(mult_done, 1)

            def q_rest_k_low(r, s):
                g = r * STEPS + s
                v.wait_ge(q_hi, g + 1)
                wait(v, q_lo, g)
                v.scalar_tensor_tensor(rest[:], Y[0][:], bcol[:, 0:1], QP[s][:, 0], ALU.add,
                                       ALU.subtract).then_inc(rest_done, 1)
                v.wait_ge(k_hi, g + 1)
                v.scalar_tensor_tensor(KP[s][:, 1], Y[1][:], bcol[:, 1:2], KP[s][:, 0], ALU.add,
                                       ALU.subtract).then_inc(k_lo, 1)

            def q_middle(r, s):
                g = r * STEPS + s
                v.wait_ge(rest_done, g + 1)
                v.tensor_copy(QP[s][:, 1], rest[:]).then_inc(q_mid, 1)

            def q_low(r, s):
                g = r * STEPS + s
                v.wait_ge(q_mid, g + 1)
                v.tensor_tensor(QP[s][:, 2], rest[:], QP[s][:, 1], ALU.subtract).then_inc(q_lo, 1)

            pipelined(v, ROUNDS, STEPS, [(3, variances), (0, norm_x), (4, multiply), (3, deviations),
                                         (4, q_rest_k_low), (4, q_middle), (4, q_low)], peel=3)

            gq, bq, gk, bk = (sb["gb"][:, i, :] for i in range(4))
            for i, (u, w) in enumerate(((gq, bk), (bq, gk), (bq, bq), (bk, bk))):
                link(v.tensor_tensor(gs[:, i, :], u, w, ALU.mult))
            link(v.tensor_tensor(gs[:, 0:2, :], gs[:, 0:2, :], gs[:, 0:2, :], ALU.mult))
            v.tensor_reduce(fin[:, 0:4], gs[:], AX.X, ALU.add).then_inc(squared, 1)
            v.wait_ge(squared, 1)
            link(v.tensor_tensor(gs[:, 0, :], gq, gk, ALU.mult))
            link(v.tensor_reduce(fin[:, 8:9], gs[:, 0, :], AX.X, ALU.max, apply_absolute_value=True))
            link(v.tensor_reduce(fin[:, 9:10], gq, AX.X, ALU.max, apply_absolute_value=True))
            v.wait_ge(k_hi, GROUPS1)
            link(v.tensor_reduce(ks2[:].rearrange("p (m b) -> p m b", b=B),
                                 ksum[:].rearrange("p m (b g) -> p m b g", b=B), AX.X, ALU.add))
            v.tensor_reduce(stat[:], ks2[:], AX.X, ALU.max, apply_absolute_value=True).then_inc(stat_ready, 1)
            v.wait_ge(rooted, 1)
            link(v.tensor_tensor(fin[:, 10:11], fin[:, 6:7], fin[:, 7:8], ALU.mult))
            link(v.scalar_tensor_tensor(fin[:, 10:11], fin[:, 8:9], 16.0, fin[:, 10:11], ALU.mult, ALU.add))
            link(v.scalar_tensor_tensor(fin[:, 10:11], fin[:, 4:5], 4.0, fin[:, 10:11], ALU.mult, ALU.add))
            link(v.scalar_tensor_tensor(fin[:, 10:11], fin[:, 5:6], 4.0, fin[:, 10:11], ALU.mult, ALU.add))
            link(v.scalar_tensor_tensor(fin[:, 9:10], fin[:, 9:10], 4.0, fin[:, 6:7], ALU.mult, ALU.add))
            v.wait_ge(reduced, 1)
            link(v.tensor_scalar(fin[:, 11:12], kmean[:], 4.01 / S, None, ALU.mult))
            link(v.tensor_tensor(fin[:, 11:12], fin[:, 11:12], fin[:, 9:10], ALU.mult))
            link(v.tensor_tensor(fin[:, 11:12], fin[:, 11:12], fin[:, 10:11], ALU.add))
            link(v.tensor_scalar(sb["guard"][:], fin[:, 11:12], 1.001, None, ALU.mult))
            link(v.tensor_scalar(fin[:, 12:13], fin[:, 10:11], -1.001, TOP, ALU.mult, ALU.add))
            link(v.memset(shift[:], 0.0))
            v.tensor_scalar(shift[:, 0, :], shift[:, 0, :], fin[0:B * H, 12:13], None,
                            ALU.add).then_inc(shift_ready, 1)

        @block.gpsimd
        def _(pool):
            def v_remainder(r, s):
                g = r * STEPS + s
                pool.wait_ge(v_hi, g + 1)
                wait(pool, v_lo, g)
                pool.tensor_tensor(vrest[:], V32[s][:, :, :, 0:DH], VT[s][:, :, :, 0:DH],
                                ALU.subtract).then_inc(vrest_ready, 1)

            def v_low(r, s):
                g = r * STEPS + s
                pool.wait_ge(v_mid, g + 1)
                pool.tensor_tensor(VT[s][:, :, :, VP[2]:VP[2] + DH], vrest[:], VT[s][:, :, :, VP[1]:VP[1] + DH],
                                ALU.subtract).then_inc(v_lo, 1)

            pool.wait_ge(ones_set, 4)
            pipelined(pool, ROUNDS, STEPS, [(0, v_remainder), (0, v_low)], peel=1)
            pool.wait_ge(stat_ready, 1)
            pool.partition_all_reduce(kmean[:], stat[:], P, RMAX).then_inc(reduced, 1)

        @block.sync
        def _(sp):
            def store_v32(r, s):
                g = r * STEPS + s
                sp.wait_ge(v_taken, g + 1)
                sp.dma_start(dr["VF"][:, g], V32[s][:].rearrange("p h t w -> p h (t w)")).then_inc(v32_stored[s], 16)

            def store_v(r, s):
                g = r * STEPS + s
                sp.wait_ge(v_lo, g + 1)
                sp.dma_start(dr["VD"][:, g], VT[s][:].rearrange("p h t w -> p h (t w)")).then_inc(v_stored[s], 16)

            def store_qk(r, s):
                g = r * STEPS + s
                sp.wait_ge(k_lo, g + 1)
                sp.dma_start(dr["KT"].rearrange("(m p) (g n) -> g p m n", p=P, n=GT1)[g],
                             KP[s][:].rearrange("p i m n -> p (i m) n")).then_inc(qk_stored[s], 16)
                sp.wait_ge(q_lo, g + 1)
                sp.dma_start(dr["QT"].rearrange("(m p) (g n) -> g p m n", p=P, n=GT1)[g],
                             QP[s][:].rearrange("p i m n -> p (i m) n")).then_inc(qk_stored[s], 16)
            sp.wait_ge(ones_set, 4)
            pipelined(sp, ROUNDS, STEPS, [(4, store_qk), (2, store_v32), (3, store_v)], peel=3)
            sp.wait_ge(shift_ready, 1)
            sp.dma_start(dr["SH"].rearrange("i b n -> b i n"), shift[:]).then_inc(shift_stored, 16)
            sp.wait_ge(shift_stored, 16)
            for s in range(STEPS):
                sp.wait_ge(v32_stored[s], 16 * ROUNDS)
                sp.wait_ge(v_stored[s], 16 * ROUNDS)
                sp.wait_ge(qk_stored[s], 32 * ROUNDS)


MAXIMA_SEMS = ("m_loaded", "m_scores", "m_max", "m_link", "m_parts", "m_turned", "m_copied", "m_stored")


def true_maxima(nc, dr, sb, sems):
    BH = B * H
    QTILES = S // P
    with ExitStack() as ctx:
        def sbuf(name, shape, dt):
            return ctx.enter_context(nc.sbuf_tensor(name, shape, dt))
        Q = sbuf("mQ", [PAIR, S], BF16)
        K = sbuf("mK", [PAIR, S], F16)
        top = sbuf("top", [P, BH, QTILES], F32)
        part = sbuf("part", [P, SROWS, BH * QTILES], BF16)
        turned = sbuf("mturned", [P, P], BF16)
        scores = ctx.enter_context(nc.psum_tensor("mscores", [P, S], F32))
        TM = ctx.enter_context(nc.psum_tensor("TM", [P, P], BF16))
        m_loaded, m_scores, m_max, m_link, m_parts, m_turned, m_copied, m_stored = sems
        block = ctx.enter_context(nc.Block())

        @block.sync
        def _(sp):
            def load(bh):
                wait(sp, m_scores, bh * QTILES)
                load_head(sp, dr, bh, Q, K, m_loaded)
            load(0)
            with sp.Fori(1, BH) as bh:
                load(bh)
            for i in range(SROWS):
                for c in range(BH * QTILES // P):
                    sp.wait_ge(m_copied, i * (BH * QTILES // P) + c + 1)
                    rows = dr["SH"][i].rearrange("b (q n) -> (b q) n", n=P)
                    sp.dma_start(rows[c * P:(c + 1) * P, :], turned[:]).then_inc(m_stored, 16)
                    sp.wait_ge(m_stored, 16 * (i * (BH * QTILES // P) + c + 1))

        @block.tensor
        def _(pe):
            def head(bh):
                pe.wait_ge(m_loaded, LOADS * 16 * (bh + 1))
                for q in range(QTILES):
                    wait(pe, m_max, bh * QTILES + q)
                    for c in range(S // 512):
                        ins = pe.matmul(scores[:, c * 512:(c + 1) * 512], Q[:, q * P:(q + 1) * P],
                                        K[:, c * 512:(c + 1) * 512], start=True, stop=True)
                    ins.then_inc(m_scores, 1)
            head(0)
            with pe.Fori(1, BH) as bh:
                head(bh)
            pe.wait_ge(m_parts, 1)
            n = 0
            for i in range(SROWS):
                for c in range(BH * QTILES // P):
                    wait(pe, m_copied, n)
                    pe.transpose(TM[:], part[:, i, c * P:(c + 1) * P], sb["ident_b"][:]).then_inc(m_turned, 1)
                    n += 1

        @block.scalar
        def _(act):
            act.nop()

        @block.gpsimd
        def _(pool):
            pool.nop()

        @block.vector
        def _(v):
            with v.Fori(0, BH) as bh:
                for q in range(QTILES):
                    v.wait_ge(m_scores, bh * QTILES + q + 1)
                    v.tensor_reduce(top[:, bh, q:q + 1], scores[:], AX.X, ALU.max).then_inc(m_max, 1)
            v.wait_ge(m_max, BH * QTILES)
            link = Link(v, m_link)
            t = top[:].rearrange("p b q -> p (b q)")
            link(v.tensor_scalar(t, t, -1.0, TOP, ALU.mult, ALU.add))
            link(v.tensor_copy(part[:, 0], t))
            link(v.tensor_tensor(t, t, part[:, 0], ALU.subtract))
            link(v.tensor_copy(part[:, 1], t))
            v.tensor_tensor(part[:, 2], t, part[:, 1], ALU.subtract).then_inc(m_parts, 1)
            n = 0
            for i in range(SROWS):
                for c in range(BH * QTILES // P):
                    v.wait_ge(m_turned, n + 1)
                    wait(v, m_stored, 16 * n)
                    v.tensor_copy(turned[:], TM[:]).then_inc(m_copied, 1)
                    n += 1


LOADS = 12


def load_head(sp, dr, bh, Q, K, loaded):
    b, h = bh // H, bh % H
    qv = dr["QT"].rearrange("(i h d) (b n) -> h b i d n", h=H, d=DH, n=S)
    kv = dr["KT"].rearrange("(i h d) (b n) -> h b i d n", h=H, d=DH, n=S)
    for i in range(2):
        for j in range(3):
            sp.dma_start(Q[i * QR + j * DH:i * QR + (j + 1) * DH, :], qv[h, b, j]).then_inc(loaded, 16)
    for i in range(2):
        for j in range(3):
            sp.dma_start(K[i * QR + j * DH:i * QR + (j + 1) * DH, :],
                         kv[h, b, i]).then_inc(loaded, 16)


NP = 8
NB = 5
KT = S // P
STEPS = 2 * 2 * KT
LAG = 5
QC = 512
WHOLE = [s for s in range(STEPS) if s % 8 in (1, 4, 6)]
PARTED = [s for s in range(STEPS) if s not in WHOLE]
HI_ACT = [s for s in PARTED if s % 8 == 5]
HI_DVE = [s for s in PARTED if s not in HI_ACT]
SC = [s % 3 for s in range(STEPS - 4)] + [0, 1, 0, 2]
SC_BACK = [next(d for d in range(1, STEPS) if SC[s - d] == SC[s]) for s in range(STEPS)]
PART = {s: i % NB for i, s in enumerate(PARTED)}
PART_BACK = {s: (s - PARTED[i - NB]) % STEPS for i, s in enumerate(PARTED)}


def attention(nc, dr, sb):
    with ExitStack() as ctx:
        def sem(name):
            return ctx.enter_context(nc.semaphore(name))

        def sbuf(name, shape, dt):
            return ctx.enter_context(nc.sbuf_tensor(name, shape, dt))
        Q = [sbuf(f"Q{i}", [CROWS, S], BF16) for i in range(2)]
        K = [sbuf(f"K{i}", [CROWS, S], F16) for i in range(2)]
        V = [sbuf(f"V{i}", [P, KT, VW], BF16) for i in range(2)]
        V32 = [sbuf(f"V32_{i}", [P, KT, VU], F32) for i in range(2)]
        pr = [sbuf(f"pr{i}", [P, 2 * QC], F32) for i in range(NP)]
        hi = [sbuf(f"hi{i}", [P, 2 * QC], F16) for i in range(NB)]
        lo = [sbuf(f"lo{i}", [P, 2 * QC], F16) for i in range(NB)]
        acc_sb = [sbuf(f"acc_sb{i}", [P, QC], F32) for i in range(2)]
        sc = [ctx.enter_context(nc.psum_tensor(f"sc{i}", [P, 2 * QC], F32)) for i in range(max(SC) + 1)]
        acc = [ctx.enter_context(nc.psum_tensor(f"acc{i}", [P, QC], F32)) for i in range(2)]
        turned = [a[:, 0:QC // P * 2 * VU].rearrange("p (q d) -> p q d", q=QC // P) for a in acc]
        loaded = [sem(f"loaded{i}") for i in range(2)]
        ones = sem("ones")
        scores_ready = sem("scores_ready")
        exp_done = sem("exp_done")
        hi_act = sem("hi_act")
        hi_dve = sem("hi_dve")
        lo_done = sem("lo_done")
        pv_done = sem("pv_done")
        acc_out = sem("acc_out")
        turned_ready = sem("turned_ready")
        out_done = sem("out_done")
        ROUNDS = B * H // 2
        GS = KT
        GR = STEPS // GS
        block = ctx.enter_context(nc.Block())

        def hi_ready(eng, r, s):
            mine = HI_ACT if s in HI_ACT else HI_DVE
            eng.wait_ge(hi_act if s in HI_ACT else hi_dve, r * len(mine) + mine.index(s) + 1)

        def lo_ready(eng, r, s):
            wait(eng, lo_done, r * len(PARTED) + PARTED.index(s) + 1)

        @block.sync
        def _(sp):
            def load(r, s):
                wait(sp, pv_done, r * STEPS + (s - 1) * (STEPS // 2))
                bh = 2 * r + s
                load_head(sp, dr, bh, Q[s], K[s], loaded[s])
                sp.dma_start(Q[s][PAIR:CROWS, :], dr["SH"][:, bh, :]).then_inc(loaded[s], 16)
                b, h = bh // H, bh % H
                for name, dst in (("VD", V[s]), ("VF", V32[s])):
                    sp.dma_start(dst[:].rearrange("p (g t) w -> p g (t w)", t=G1),
                                 dr[name].rearrange("p (b g) h w -> p b h g w", b=B)[:, b, h]).then_inc(loaded[s], 16)
            pipelined(sp, ROUNDS, 2, [(0, load)], peel=1)

        @block.tensor
        def _(pe):
            pe.wait_ge(ones, 2)

            def scores(r, s):
                n = r * STEPS + s
                head, k, c = s // (STEPS // 2), s % KT, s // KT % 2
                if s % (STEPS // 2) == 0:
                    pe.wait_ge(loaded[head], 16 * (LOADS + 3) * (r + 1))
                wait(pe, exp_done, n - SC_BACK[s] + 1)
                for j in range(2):
                    ins = pe.matmul(sc[SC[s]][:, j * QC:(j + 1) * QC], K[head][:, k * P:(k + 1) * P],
                                    Q[head][:, (2 * c + j) * QC:(2 * c + j + 1) * QC], start=True, stop=True)
                ins.then_inc(scores_ready, 1)

            def values(r, s):
                n = r * STEPS + s
                head, k = s // (STEPS // 2), s % KT
                if k == 0:
                    wait(pe, out_done, r * GR + s // GS - 1)
                if s in WHOLE:
                    pe.wait_ge(exp_done, n + 1)
                    for j in range(2):
                        ins = pe.matmul(acc[s // GS % 2][j * VW:j * VW + VU, :], V32[head][:, k, :],
                                        pr[s % NP][:, j * QC:(j + 1) * QC], start=False, stop=(k == KT - 1))
                    ins.then_inc(pv_done, 1)
                    return
                hi_ready(pe, r, s)
                for part, ready in ((hi, False), (lo, True)):
                    if ready:
                        lo_ready(pe, r, s)
                    for j in range(2):
                        ins = pe.matmul(acc[s // GS % 2][j * VW:(j + 1) * VW, :], V[head][:, k, :],
                                        part[PART[s]][:, j * QC:(j + 1) * QC],
                                        start=(k == 0 and not ready), stop=(k == KT - 1 and ready))
                ins.then_inc(pv_done, 1)

            def turn(r, s):
                if s % GS != GS - 1:
                    return
                g = r * GR + s // GS
                pe.wait_ge(acc_out, g + 1)
                for q in range(QC // P):
                    ins = pe.matmul(turned[s // GS % 2][:, q, :], acc_sb[s // GS % 2][:, q * P:(q + 1) * P], sb["sel"][:],
                                    start=True, stop=True)
                ins.then_inc(turned_ready, 1)

            pipelined(pe, ROUNDS, STEPS, [(0, scores), (LAG, values), (LAG + 3, turn)], peel=1)

        @block.scalar
        def _(act):
            def exponentials(r, s):
                n = r * STEPS + s
                act.wait_ge(scores_ready, n + 1)
                last, was = (r, s - NP) if s >= NP else (r - 1, s - NP + STEPS)
                if was in WHOLE:
                    wait(act, pv_done, n - NP + 1)
                elif not isinstance(last, int) or last >= 0:
                    lo_ready(act, last, was)
                nc.scalar.activation(pr[s % NP][:], sc[SC[s]][:], ACT.Exp).then_inc(exp_done, 1)

            def high(r, s):
                if s not in HI_ACT:
                    return
                n = r * STEPS + s
                act.wait_ge(exp_done, n + 1)
                wait(act, pv_done, n - PART_BACK[s] + 1)
                nc.scalar.activation(hi[PART[s]][:], pr[s % NP][:], ACT.Copy).then_inc(hi_act, 1)

            def take(r, s):
                if s % GS != GS - 1:
                    return
                g = r * GR + s // GS
                act.wait_ge(pv_done, r * STEPS + s + 1)
                wait(act, turned_ready, g - 1)
                nc.scalar.activation(acc_sb[s // GS % 2][:], acc[s // GS % 2][:], ACT.Copy).then_inc(acc_out, 1)

            pipelined(act, ROUNDS, STEPS, [(0, exponentials), (1, high), (LAG + 1, take)], peel=1)

        @block.vector
        def _(v):
            for i in range(2):
                v.memset(K[i][PAIR:CROWS, :], 1.0).then_inc(ones, 1)
            out = sb["O"][:].rearrange("p (r g) j q d -> p r g j q d", r=ROUNDS)

            def low(r, s):
                if s in WHOLE:
                    return
                n = r * STEPS + s
                v.wait_ge(exp_done, n + 1)
                wait(v, pv_done, n - PART_BACK[s] + 1)
                if s in HI_DVE:
                    v.tensor_copy(hi[PART[s]][:], pr[s % NP][:]).then_inc(hi_dve, 1)
                hi_ready(v, r, s)
                v.tensor_tensor(lo[PART[s]][:], pr[s % NP][:], hi[PART[s]][:],
                                ALU.subtract).then_inc(lo_done, 1)

            def keep(r, s):
                if s % GS != GS - 1:
                    return
                g = r * GR + s // GS
                v.wait_ge(turned_ready, g + 1)
                v.tensor_copy(out[:, r, s // GS].rearrange("p j q d -> p q j d"),
                              turned[s // GS % 2].rearrange("p q (j d) -> p q j d", j=2)).then_inc(out_done, 1)

            pipelined(v, ROUNDS, STEPS, [(0, low), (LAG + 4, keep)], peel=1)


def project_and_route(nc, dr, sb):
    with ExitStack() as ctx:
        def sem(name):
            return ctx.enter_context(nc.semaphore(name))

        def sbuf(name, shape, dt):
            return ctx.enter_context(nc.sbuf_tensor(name, shape, dt))
        den = sbuf("den", [P, G, H], F32)
        att = sbuf("att", [P, 2, G, D], F32)
        attT = sbuf("attT", [P, 2, KD, GT], F32)
        y = sbuf("y", [P, 2, G, D], F32)
        xn = sbuf("xn3", [P, 2, G, D], F32)
        xnT = sbuf("xnT3", [P, 2, KD, GT], F32)
        bn = [sbuf(f"bn3{i}", [P, G, 6], F32) for i in range(2)]
        mv = [sbuf(f"mv3{i}", [P, G, 2], F32) for i in range(2)]
        ve = [sbuf(f"ve3{i}", [P, G], F32) for i in range(2)]
        root = [sbuf(f"root3{i}", [P, G], F32) for i in range(2)]
        rs = [sbuf(f"rs3{i}", [P, 2, G], F32) for i in range(2)]
        tm = [sbuf(f"tm3{i}", [P, G], F32) for i in range(2)]
        away = sbuf("away", [P, 2, G], F32)
        TA = [ctx.enter_context(nc.psum_tensor(f"TA{i}", [P, 2, KD, P], F32)) for i in range(2)]
        Y = [ctx.enter_context(nc.psum_tensor(f"Y{i}", [P, G, D], F32)) for i in range(2)]
        TX = ctx.enter_context(nc.psum_tensor("TX", [P, 2, KD, P], F32))
        Z = ctx.enter_context(nc.psum_tensor("Z", [P, G, E], F32))
        att_ready = sem("att_ready")
        aT_psum = sem("aT_psum")
        aT_ready = sem("aT_ready")
        y_psum = sem("y_psum")
        var3 = [sem(f"var3{i}") for i in range(2)]
        root3 = [sem(f"root3s{i}") for i in range(2)]
        away_ready = sem("away_ready")
        y_done = sem("y_done")
        x1_done = sem("x1_done")
        xn_ready = sem("xn3s")
        xT_psum = sem("xT3_psum")
        xT_ready = sem("xT3")
        z_psum = sem("z_psum")
        z_out = sem("z_out")
        xn_stored = [sem(f"xn_stored{i}") for i in range(2)]
        rw_turned = sem("rw_turned")
        rw_ready = sem("rw_ready")
        w_in = sem("w13_in")
        divide_link = sem("divide_link")
        stats_link = [sem(f"stats_link3{i}") for i in range(2)]
        newton_link = [sem(f"newton_link3{i}") for i in range(2)]
        ROUNDS, STEPS3 = GROUPS // 2, 2
        block = ctx.enter_context(nc.Block())

        @block.tensor
        def _(pe):
            def turn_att(r, s):
                g = r * STEPS3 + s
                pe.wait_ge(att_ready, g + 1)
                for h in range(2):
                    wait(pe, aT_ready, 2 * g + h - 1)
                    for t in range(2):
                        for k in range(KD):
                            ins = pe.transpose(TA[h][:, t, k, :], att[:, s, 2 * h + t, k * P:(k + 1) * P],
                                               sb["ident"][:])
                    ins.then_inc(aT_psum, 1)

            def project(r, s):
                g = r * STEPS3 + s
                pe.wait_ge(aT_ready, 2 * g + 2)
                wait(pe, y_done, g - 1)
                for j in range(G):
                    for k in range(KD):
                        ins = pe.matmul(Y[s][:, j, :], attT[:, s, k, j * P:(j + 1) * P], sb["wproj"][:, k, :],
                                        start=(k == 0), stop=(k == KD - 1))
                ins.then_inc(y_psum, 1)

            def turn_xn(h):
                def stage(r, s):
                    g = r * STEPS3 + s
                    pe.wait_ge(xn_ready, g + 1)
                    wait(pe, xT_ready, 2 * g + h)
                    for t in range(2):
                        for k in range(KD):
                            ins = pe.transpose(TX[:, t, k, :], xn[:, s, 2 * h + t, k * P:(k + 1) * P],
                                               sb["ident"][:])
                    ins.then_inc(xT_psum, 1)
                return stage

            def route(r, s):
                g = r * STEPS3 + s
                pe.wait_ge(xT_ready, 2 * g + 2)
                wait(pe, z_out, g)
                for j in range(G):
                    for k in range(KD):
                        ins = pe.matmul(Z[:, j, :], xnT[:, s, k, j * P:(j + 1) * P], sb["rwT"][:, k, :],
                                        start=(k == 0), stop=(k == KD - 1))
                ins.then_inc(z_psum, 1)

            for k in range(KD):
                ins = pe.transpose(Z[:, k, :], sb["rw"][:, k * P:(k + 1) * P], sb["ident"][0:E, 0:E])
            ins.then_inc(rw_turned, 1)
            pe.wait_ge(rw_ready, 1)
            pipelined(pe, ROUNDS, STEPS3, [(3, turn_xn(0)), (0, turn_att), (3, turn_xn(1)), (0, project),
                                           (3, route)], peel=3)

        @block.scalar
        def _(act):
            def take_att(r, s):
                g = r * STEPS3 + s
                wait(act, y_psum, g - 1)
                for h in range(2):
                    act.wait_ge(aT_psum, 2 * g + h + 1)
                    nc.scalar.activation(
                        attT[:, s, :, 2 * h * P:2 * (h + 1) * P].rearrange("p k (t n) -> p t k n", n=P),
                        TA[h][:], ACT.Copy).then_inc(aT_ready, 1)

            def roots(i):
                def stage(r, s):
                    act.wait_ge(var3[i], r * STEPS3 + s + 1)
                    nc.scalar.activation(root[i][:], ve[i][:], ACT.Sqrt).then_inc(root3[i], 1)
                return stage

            def norm_y(r, s):
                g = r * STEPS3 + s
                act.wait_ge(away_ready, g + 1)
                wait(act, x1_done, g - 1)
                for t in range(G):
                    ins = nc.scalar.activation(y[:, s, t, :], Y[s][:, t, :], ACT.Identity,
                                               bias=away[:, s, t:t + 1], scale=rs[0][:, s, t:t + 1])
                ins.then_inc(y_done, 1)

            def take_xn(r, s):
                g = r * STEPS3 + s
                wait(act, z_psum, g - 1)
                for h in range(2):
                    act.wait_ge(xT_psum, 2 * g + h + 1)
                    nc.scalar.activation(
                        xnT[:, s, :, 2 * h * P:2 * (h + 1) * P].rearrange("p k (t n) -> p t k n", n=P),
                        TX[:], ACT.Copy).then_inc(xT_ready, 1)

            pipelined(act, ROUNDS, STEPS3, [(0, take_att), (3, take_xn), (1, roots(0)), (2, roots(1)),
                                            (1, norm_y)], peel=3)

        @block.gpsimd
        def _(pool):
            def residual(r, s):
                g = r * STEPS3 + s
                pool.wait_ge(y_done, g + 1)
                x4 = sb["x"][:].rearrange("p (g t) d -> p g t d", t=G)
                pool.tensor_tensor(x4[:, g], x4[:, g], y[:, s], ALU.add).then_inc(x1_done, 1)
            pipelined(pool, ROUNDS, STEPS3, [(0, residual)])

        @block.sync
        def _(sp):
            for e in (E, *range(E)):
                for name, dst in (("w1", "W1"), ("w3", "W3")):
                    src = dr["s" + name][0] if e == E else dr[name][e]
                    sp.dma_start(sb[dst][:, e], src.rearrange("(k p) n -> p k n", p=P)).then_inc(w_in, 16)

            def store(r, s):
                g = r * STEPS3 + s
                sp.wait_ge(xn_ready, g + 1)
                sp.dma_start(dr["XN"].rearrange("(g t p) d -> g p t d", t=G, p=P)[g], xn[:, s]).then_inc(xn_stored[s], 16)
            pipelined(sp, ROUNDS, STEPS3, [(0, store)], peel=1)
            for s in range(STEPS3):
                sp.wait_ge(xn_stored[s], 16 * ROUNDS)
            sp.wait_ge(w_in, 16 * 2 * (E + 1))

        @block.vector
        def _(v):
            v.wait_ge(rw_turned, 1)
            v.tensor_copy(sb["rwT"][:], Z[:, 0:KD, :]).then_inc(rw_ready, 1)
            dl = Link(v, divide_link, 1)
            sl = [Link(v, stats_link[i], 2) for i in range(2)]
            nl = [Link(v, newton_link[i], 5) for i in range(2)]
            x4 = sb["x"][:].rearrange("p (g t) d -> p g t d", t=G)
            o4 = sb["O"][:].rearrange("p (b h c) j q d -> p b c j q h d", b=B, h=H)

            def divide(r, s):
                g = r * STEPS3 + s
                dl.start(g)
                b = r // 2
                o = o4[:, b, r % 2, s]
                wait(v, att_ready, g)
                dl(v.reciprocal(den[:], o[:, :, :, DH]))
                wait(v, aT_psum, 2 * (g - 1))
                a4 = att[:, s].rearrange("p q (h d) -> p q h d", d=DH)
                for q in range(G):
                    ins = v.tensor_tensor(a4[:, q], o[:, q, :, 0:DH], den[:, q].unsqueeze(2).to_broadcast([P, H, DH]),
                                          ALU.mult)
                ins.then_inc(att_ready, 1)

            def stats(i, src):
                def stage(r, s):
                    g = r * STEPS3 + s
                    sl[i].start(g)
                    v.wait_ge((y_psum, x1_done)[i], g + 1)
                    settle(v, sb["tick"])
                    for t in range(G):
                        ins = v.bn_stats(bn[i][:, t, :], src(g, s, t))
                    sl[i](ins)
                    settle(v, sb["tick"])
                    for t in range(G):
                        ins = v.bn_aggr(mv[i][:, t, :], bn[i][:, t, :])
                    sl[i](ins)
                    v.tensor_scalar(ve[i][:], mv[i][:, :, 1], EPS, None, ALU.add).then_inc(var3[i], 1)
                return stage

            def deviation_y(r, s):
                g = r * STEPS3 + s
                nl[0].start(g)
                v.wait_ge(var3[0], g + 1)
                rstd_newton(nl[0], v, ve[0][:], root[0][:], rs[0][:, s], tm[0][:], root3[0], g + 1)
                v.scalar_tensor_tensor(away[:, s], mv[0][:, :, 0], -1.0, rs[0][:, s], ALU.mult,
                                       ALU.mult).then_inc(away_ready, 1)
                v.wait_ge(away_ready, g + 1)

            def norm_x(r, s):
                g = r * STEPS3 + s
                nl[1].start(g)
                v.wait_ge(var3[1], g + 1)
                rstd_newton(nl[1], v, ve[1][:], root[1][:], rs[1][:, s], tm[1][:], root3[1], g + 1)
                wait(v, xT_psum, 2 * (g - 1))
                wait(v, xn_stored[s], 16 * r)
                for t in range(G):
                    ins = v.tensor_scalar(xn[:, s, t, :], x4[:, g, t, :], mv[1][:, t, 0:1], rs[1][:, s, t:t + 1],
                                          ALU.subtract, ALU.mult)
                ins.then_inc(xn_ready, 1)
                v.wait_ge(xn_ready, g + 1)

            def keep_z(r, s):
                g = r * STEPS3 + s
                v.wait_ge(z_psum, g + 1)
                z4 = sb["z"][:].rearrange("p (g t) e -> p g t e", t=G)
                v.tensor_tensor(z4[:, g], Z[:], sb["rbias"][:].unsqueeze(1).to_broadcast([P, G, E]),
                                ALU.add).then_inc(z_out, 1)

            pipelined(v, ROUNDS, STEPS3, [(0, divide), (1, stats(0, lambda g, s, t: Y[s][:, t, :])),
                                          (2, stats(1, lambda g, s, t: x4[:, g, t, :])), (1, deviation_y),
                                          (2, norm_x), (4, keep_z)], peel=3)


SLOT_TILES = TOPK * TILES + E
SCANNED = (TILES.bit_length() - 1) % 2
FIRST = TILES // 2
UNITS = TILES + SLOT_TILES


class Carver:

    def __init__(self, area):
        self.area, self.used = area, 0

    def __call__(self, *shape, dt=F32):
        words = -(-int(np.prod(shape)) * (2 if dt == BF16 else 4) // 4)
        flat = self.area[:, self.used:self.used + words]
        self.used += words
        if dt != F32:
            flat = flat.bitcast(dt)
        names = [f"a{k}" for k in range(len(shape))]
        if len(shape) == 1:
            return flat
        return flat.rearrange(f"p ({' '.join(names)}) -> p {' '.join(names)}",
                              **dict(zip(names[1:], shape[1:])))


def experts(nc, dr, sb):
    with ExitStack() as ctx:
        def sem(name):
            return ctx.enter_context(nc.semaphore(name))

        def sbuf(name, shape, dt):
            return ctx.enter_context(nc.sbuf_tensor(name, shape, dt))
        KH = HID // P
        NX = 4
        W1, W3, W2 = sb["W1"], sb["W3"], sb["W2"]
        xs = [sbuf(f"xs{i}", [P, D], F32) for i in range(NX)]
        xsT = [sbuf(f"xsT{i}", [P, KD, P], F32) for i in range(2)]
        h = [sbuf(f"h{i}", [P, HID], F32) for i in range(2)]
        hT = [sbuf(f"hT{i}", [P, KH, P], F32) for i in range(2)]
        ys = [sbuf(f"ys{i}", [P, D], F32) for i in range(NX)]
        ids = sbuf("ids", [P, SLOT_TILES], U32)
        unit_ids = [sbuf(f"unit_ids{i}", [P, 1], U32) for i in range(NX)]
        unit = sbuf("unit", [P, SLOT_TILES], F32)
        lane = sbuf("lane", [P, P], F32)
        own = sbuf("own", [P, 1], F32)
        tile_no = sbuf("tile_no", [P, TILES], F32)
        lane_of = sbuf("lane_of", [P, TOPK, TILES], F32)
        tile_of = sbuf("tile_of", [P, TOPK, TILES], F32)
        ids_part = sbuf("ids_part", [P, SLOT_TILES], F32)
        room = sb["O"][:].rearrange("p a b c d -> p (a b c d)")
        carve = Carver(room)
        best = carve(TILES, 8)
        bidx = carve(TILES, 8, dt=U32)
        bidf = carve(TILES, TOPK)
        gap = carve(TILES)
        hot = carve(TOPK, TILES, E)
        both = carve(TILES, E)
        before = carve(P)
        ones = carve(P)
        scan = carve(2, TILES, E)
        count_i = carve(E, dt=I32)
        ends = carve(E)
        start = carve(E)
        pos = carve(TILES, E)
        place = carve(TOPK * TILES)
        place_i = carve(TOPK * TILES, dt=I32)
        part_i = carve(TOPK * TILES, dt=I32)
        later = carve(SLOT_TILES, E - 1)
        eid = carve(SLOT_TILES)
        carve = Carver(room)
        lanes = carve(TOPK * TILES, P, dt=BF16)
        tiles_own = carve(TOPK * TILES, SLOT_TILES, dt=BF16)
        tiles_no = carve(TOPK * TILES, SLOT_TILES, dt=BF16)
        GD = G * D
        got = [room[:, TOPK * GD * i:TOPK * GD * (i + 1)].rearrange("p (j t d) -> p j t d", j=TOPK, t=G)
               for i in range(2)]
        moe = [room[:, GD * (4 + i):GD * (5 + i)].rearrange("p (t d) -> p t d", t=G) for i in range(2)]
        shared = [room[:, GD * (6 + i):GD * (7 + i)].rearrange("p (t d) -> p t d", t=G) for i in range(2)]
        bn = [sbuf(f"bn6{i}", [P, G, 6], F32) for i in range(2)]
        mv = [sbuf(f"mv6{i}", [P, G, 2], F32) for i in range(2)]
        ve = [sbuf(f"ve6{i}", [P, G], F32) for i in range(2)]
        root = [sbuf(f"root6{i}", [P, G], F32) for i in range(2)]
        rs = [sbuf(f"rs6{i}", [P, G], F32) for i in range(2)]
        tm = [sbuf(f"tm6{i}", [P, G], F32) for i in range(2)]
        rows = [sbuf(f"rows{i}", [P, TOPK, G], U32) for i in range(2)]
        XT = ctx.enter_context(nc.psum_tensor("XT", [P, KD, P], F32))
        GP = [ctx.enter_context(nc.psum_tensor(f"GP{i}", [P, HID], F32)) for i in range(2)]
        UP = [ctx.enter_context(nc.psum_tensor(f"UP{i}", [P, HID], F32)) for i in range(2)]
        HT = ctx.enter_context(nc.psum_tensor("HT", [P, KH, P], F32))
        Y = ctx.enter_context(nc.psum_tensor("Y5", [P, D], F32))
        DP = ctx.enter_context(nc.psum_tensor("DP", [P, 2, TILES * E], F32))
        rank = DP[:, 0, :].rearrange("p (t e) -> p t e", e=E)
        total = DP[:, 1, :].rearrange("p (t e) -> p t e", e=E)
        out_stored = sem("out_stored")
        x_in = [sem(f"x_in{i}") for i in range(NX)]
        x_gathered = [sem(f"x_gathered{i}") for i in range(NX)]
        x_turned = sem("x_turned")
        xsT_ready = sem("xsT_ready")
        g_psum = sem("g_psum")
        u_psum = sem("u_psum")
        silu_done = sem("silu_done")
        h_done = sem("h_done")
        h_turned = sem("h_turned")
        hT_ready = sem("hT_ready")
        y_psum = sem("y5_psum")
        y_out = sem("y5_out")
        y_stored = [sem(f"y_stored{i}") for i in range(NX)]
        w2_shared = sem("w2_shared")
        w2_in = sem("w2_in")
        consts = sem("consts5")
        link_s = sem("d_link")
        gap_ready = sem("gap_ready")
        gap_exp = sem("gap_exp")
        both_ready = sem("both_ready")
        ranked = sem("ranked")
        lanes_ready = sem("lanes_ready")
        tiles_ready = sem("tiles_ready")
        own_ready = sem("own_ready")
        ids_psum = sem("ids_psum")
        ids_ready = sem("ids_ready")
        unit_ids_ready = sem("unit_ids_ready")
        shared_in = sem("shared_in")
        routed_in = [sem(f"routed_in{i}") for i in range(2)]
        summed = [sem(f"summed{i}") for i in range(2)]
        rows_ready = [sem(f"rows_ready{i}") for i in range(2)]
        stats_link = [sem(f"stats_link{i}") for i in range(2)]
        norm_link = [sem(f"norm_link{i}") for i in range(2)]
        var6 = [sem(f"var6{i}") for i in range(2)]
        root6 = [sem(f"root6s{i}") for i in range(2)]
        rs_ready = [sem(f"rs6_ready{i}") for i in range(2)]
        scaled = [sem(f"scaled{i}") for i in range(2)]
        out_ready = [sem(f"out_ready{i}") for i in range(2)]
        STEPS5 = NX
        SLOTS = FIRST // NX
        LAST = SLOTS + SLOT_TILES // NX
        ROUNDS = UNITS // NX
        IDS_ROUND = SLOTS - 1
        block = ctx.enter_context(nc.Block())

        def early(r):
            return isinstance(r, int) and r < LAST

        @block.sync
        def _(sp):
            x_tiles = dr["XN"].rearrange("(u p) d -> u p d", p=P)
            out = dr["out"].rearrange("b (g t p) d -> (b g) p t d", t=G, p=P)
            x4 = sb["x"][:].rearrange("p (g t) d -> p g t d", t=G)

            def load(r, s):
                u = r * NX + s
                wait(sp, x_turned, u - NX + 1)
                sp.dma_start(xs[s][:], x_tiles[u]).then_inc(x_in[s], 16)

            def load_second(r, s):
                u = r * NX + s
                sp.wait_ge(x_turned, u - NX + 1)
                sp.dma_start(xs[s][:], x_tiles[u - SLOT_TILES]).then_inc(x_in[s], 16)

            def store(r, s):
                u = r * NX + s
                sp.wait_ge(y_out, u + 1)
                sp.dma_start(dr["YS"].rearrange("(u p) d -> u p d", p=P)[u], ys[s][:]).then_inc(y_stored[s], 16)

            def store_last(r, s):
                if early(r):
                    store(r, s)

            def load_shared(r, s):
                if s == 0 and not early(r):
                    if isinstance(r, int) and r == LAST:
                        for i in range(NX):
                            sp.wait_ge(y_stored[i], 16 * LAST)
                    sp.wait_ge(summed[0], r - LAST + 1)
                    sp.dma_start(shared[0], dr["YS"][0:FIRST * P].rearrange(
                        "(g t p) d -> g p t d", t=G, p=P)[r - LAST]).then_inc(shared_in, 16)

            def store_out(kind, unit):
                def stage(r, s):
                    if s == unit and not early(r):
                        c = r - LAST
                        g = c + kind * (GROUPS // 2)
                        sp.wait_ge(out_ready[kind], c + 1)
                        sp.dma_start(out[g], x4[:, g]).then_inc(out_stored, 16)
                return stage
            first = [(0, load), (8, store)]
            pipelined(sp, SLOTS, NX, first, peel=2, drain=False)
            pipelined(sp, LAST, NX, [(8, store)], start=SLOTS, drain=False)
            pipelined(sp, ROUNDS, NX, [(0, load_second), (8, store_last), (8, load_shared), (12, store_out(0, 0)),
                                       (11, store_out(1, 3))], start=LAST, peel=ROUNDS - LAST)
            sp.wait_ge(out_stored, 16 * GROUPS)

        @block.gpsimd
        def _(pool):
            pool.dma_start(W2[:, E], dr["sw2"][0].rearrange("(k p) n -> p k n", p=P)).then_inc(w2_shared, 16)
            for e in range(E):
                pool.dma_start(W2[:, e], dr["w2"][e].rearrange("(k p) n -> p k n", p=P)).then_inc(w2_in, 16)
            exact = dict(base=0, allow_small_or_imprecise_dtypes=True)
            pool.memset(ones, 1.0).then_inc(consts, 1)
            pool.iota(unit[:], pattern=[[1, SLOT_TILES]], channel_multiplier=0, **exact).then_inc(consts, 1)
            pool.iota(lane[:], pattern=[[1, P]], channel_multiplier=0, **exact).then_inc(consts, 1)
            pool.iota(own[:], pattern=[[0, 1]], channel_multiplier=1, **exact).then_inc(consts, 1)
            pool.iota(tile_no[:], pattern=[[1, TILES]], channel_multiplier=0, **exact).then_inc(consts, 1)
            pool.wait_ge(consts, 5)
            pool.affine_select(out=before, in_=ones, compare_op=ALU.is_gt, fill=0.0, base=0,
                               pattern=[[1, P]], channel_multiplier=-1).then_inc(consts, 1)
            pool.wait_ge(ids_ready, 1)

            def gather(r, s):
                u = r * NX + s
                pool.wait_ge(x_turned, u - NX + 1)
                pool.tensor_copy(unit_ids[s][:], ids[:, bass.ds(u - FIRST, 1)]).then_inc(unit_ids_ready, 1)
                pool.wait_ge(unit_ids_ready, u - FIRST + 1)
                settle_pool(pool, sb["tick_pool"])
                pool.indirect_dma_start(
                    out=xs[s][:], out_offset=None, in_=dr["XN"],
                    in_offset=bass.IndirectOffsetOnAxis(ap=unit_ids[s][:], axis=0)).then_inc(x_gathered[s], 16)
            pipelined(pool, LAST, NX, [(0, gather)], start=SLOTS)
            for i in range(NX):
                pool.wait_ge(y_stored[i], 16 * LAST)

            def gather_rows(c, kind):
                g = c + kind * (GROUPS // 2)
                pool.wait_ge(summed[kind], c + 1)
                pool.tensor_copy(rows[kind][:], sb["row"][:, :, bass.ds(g * G, G)]).then_inc(rows_ready[kind], 1)
                pool.wait_ge(rows_ready[kind], c + 1)
                settle_pool(pool, sb["tick_pool"])
                for j in range(TOPK):
                    for t in range(G):
                        pool.indirect_dma_start(
                            out=got[kind][:, j, t, :], out_offset=None, in_=dr["YS"],
                            in_offset=bass.IndirectOffsetOnAxis(ap=rows[kind][:, j, t:t + 1], axis=0)
                        ).then_inc(routed_in[kind], 16)
            pipelined(pool, GROUPS // 2, 2, [(0, gather_rows)])

        @block.tensor
        def _(pe):
            def turn_loaded(r, s):
                pe.wait_ge(x_in[s], 16 * (r + 1))
                turn_x(r, s)

            def turn_gathered(r, s):
                pe.wait_ge(x_gathered[s], 16 * (r - SLOTS + 1))
                turn_x(r, s)

            def turn_second(r, s):
                pe.wait_ge(x_in[s], 16 * (r - LAST + SLOTS + 1))
                turn_x(r, s)

            def turn_x(r, s):
                u = r * STEPS5 + s
                wait(pe, xsT_ready, u)
                for k in range(KD):
                    ins = pe.transpose(XT[:, k, :], xs[s][:, k * P:(k + 1) * P], sb["ident"][:])
                ins.then_inc(x_turned, 1)

            def expert(r, u):
                if shared_rounds(r):
                    return E
                return pe.value_load(sb["eid"][0:1, bass.ds(u, 1)], min_val=0, max_val=E)

            def shared_rounds(r):
                return isinstance(r, int) and (r < SLOTS or r >= LAST)

            def up(r, s):
                u = r * STEPS5 + s
                e = expert(r, u)
                pe.wait_ge(xsT_ready, u + 1)
                wait(pe, h_done, u - 1)
                for k in range(KD):
                    ins = pe.matmul(GP[s % 2][:], xsT[s % 2][:, k, :], W1[:, e, k, :],
                                    start=(k == 0), stop=(k == KD - 1))
                ins.then_inc(g_psum, 1)
                for k in range(KD):
                    ins = pe.matmul(UP[s % 2][:], xsT[s % 2][:, k, :], W3[:, e, k, :],
                                    start=(k == 0), stop=(k == KD - 1))
                ins.then_inc(u_psum, 1)

            def turn_h(r, s):
                u = r * STEPS5 + s
                pe.wait_ge(h_done, u + 1)
                wait(pe, hT_ready, u)
                for m in range(KH):
                    ins = pe.transpose(HT[:, m, :], h[s % 2][:, m * P:(m + 1) * P], sb["ident"][:])
                ins.then_inc(h_turned, 1)

            def down(r, s):
                u = r * STEPS5 + s
                e = expert(r, u)
                pe.wait_ge(hT_ready, u + 1)
                if isinstance(u, int) and u == 0:
                    pe.wait_ge(w2_shared, 16)
                wait(pe, y_out, u)
                for m in range(KH):
                    ins = pe.matmul(Y[:], hT[s % 2][:, m, :], W2[:, e, m, :], start=(m == 0), stop=(m == KH - 1))
                ins.then_inc(y_psum, 1)

            rest = [(1, up), (2, turn_h), (3, down)]

            def rank_tokens(r, s):
                if (r, s) != (1, 0):
                    return
                pe.wait_ge(both_ready, 1)
                pe.wait_ge(consts, 6)
                flat = both.rearrange("p t e -> p (t e)")
                pe.matmul(DP[:, 0, :], before, flat, start=True, stop=True)
                pe.matmul(DP[:, 1, :], ones, flat, start=True, stop=True).then_inc(ranked, 1)

            def find_ids(r, s):
                if (r, s) != (IDS_ROUND, 1):
                    return
                pe.wait_ge(lanes_ready, 4 * TOPK)
                pe.wait_ge(tiles_ready, 4 + TOPK)
                for part, tiles in enumerate((tiles_own, tiles_no)):
                    n = TOPK * TILES
                    for i in range(n):
                        ins = pe.matmul(DP[:, part, 0:SLOT_TILES], lanes[:, i, :], tiles[:, i, :],
                                        start=(i == 0), stop=(i == n - 1))
                ins.then_inc(ids_psum, 1)
            pipelined(pe, SLOTS, STEPS5, [(0, turn_loaded)] + rest + [(0, rank_tokens), (0, find_ids)],
                      peel=SLOTS, drain=False)
            pe.wait_ge(w2_in, 16 * E)
            pe.wait_ge(ids_ready, 1)
            pipelined(pe, LAST, STEPS5, [(0, turn_gathered)] + rest, start=SLOTS, drain=False)
            pipelined(pe, ROUNDS, STEPS5, [(0, turn_second)] + rest, start=LAST)

        @block.scalar
        def _(act):
            def copy_x(r, s):
                u = r * STEPS5 + s
                act.wait_ge(x_turned, u + 1)
                wait(act, u_psum, u - 1)
                nc.scalar.activation(xsT[s % 2][:], XT[:], ACT.Copy).then_inc(xsT_ready, 1)

            def silu(r, s):
                u = r * STEPS5 + s
                act.wait_ge(g_psum, u + 1)
                wait(act, h_turned, u - 1)
                nc.scalar.activation(h[s % 2][:], GP[s % 2][:], ACT.Silu).then_inc(silu_done, 1)

            def copy_h(r, s):
                u = r * STEPS5 + s
                act.wait_ge(h_turned, u + 1)
                wait(act, y_psum, u - 1)
                nc.scalar.activation(hT[s % 2][:], HT[:], ACT.Copy).then_inc(hT_ready, 1)

            def root_of(kind, unit):
                def stage(r, s):
                    if s == unit and not early(r):
                        act.wait_ge(var6[kind], r - LAST + 1)
                        nc.scalar.activation(root[kind][:], ve[kind][:], ACT.Sqrt).then_inc(root6[kind], 1)
                return stage
            def exp_gap(r, s):
                if r == 0 and s == 3:
                    act.wait_ge(gap_ready, 1)
                    nc.scalar.activation(gap, gap, ACT.Exp).then_inc(gap_exp, 1)

            def times_own(r, s):
                if (r, s) == (2, 1):
                    act.wait_ge(tiles_ready, 4)
                    for j in range(TOPK):
                        part = slice(j * TILES, (j + 1) * TILES)
                        nc.scalar.activation(tiles_own[:, part], tiles_no[:, part], ACT.Copy,
                                             scale=own[:]).then_inc(own_ready, 1)
            units = [(0, copy_x), (1, silu), (2, copy_h)]
            pipelined(act, SLOTS, STEPS5, units + [(0, exp_gap), (0, times_own)], peel=SLOTS, drain=False)
            pipelined(act, LAST, STEPS5, units, start=SLOTS, drain=False)
            pipelined(act, ROUNDS, STEPS5, units + [(6, root_of(0, 0)), (5, root_of(1, 3))], start=LAST, peel=2)

        @block.vector
        def _(v):
            def gate(r, s):
                u = r * STEPS5 + s
                v.wait_ge(silu_done, u + 1)
                v.wait_ge(u_psum, u + 1)
                v.tensor_tensor(h[s % 2][:], h[s % 2][:], UP[s % 2][:], ALU.mult).then_inc(h_done, 1)

            def take_y(r, s):
                if not early(r) and isinstance(r, int):
                    return take_shared(r, s)
                u = r * STEPS5 + s
                v.wait_ge(y_psum, u + 1)
                wait(v, y_stored[s], 16 * r)
                v.tensor_copy(ys[s][:], Y[:]).then_inc(y_out, 1)

            def take_shared(r, s):
                if early(r):
                    return take_y(r, s)
                v.wait_ge(y_psum, r * STEPS5 + s + 1)
                v.tensor_copy(shared[1][:, s, :], Y[:]).then_inc(y_out, 1)

            link = Link(v, link_s)
            z = sb["z"]
            wt = sb["wt"]

            def best_scores():
                for t in range(TILES):
                    ins = v.max(best[:, t, :], z[:, t, :])
                link(ins)

            def best_experts():
                for t in range(TILES):
                    ins = v.max_index(bidx[:, t, :], best[:, t, :], z[:, t, :])
                link(ins)

            def chosen():
                v.tensor_tensor(gap, best[:, :, 1], best[:, :, 0], ALU.subtract).then_inc(gap_ready, 1)
                link(v.tensor_copy(bidf, bidx[:, :, 0:TOPK]))
                iota = sb["iota8"][:].unsqueeze(1).to_broadcast([P, TILES, E])
                for j in range(TOPK):
                    link(v.tensor_tensor(hot[:, j], iota, bidf[:, :, j].unsqueeze(2).to_broadcast([P, TILES, E]),
                                         ALU.is_equal))
                v.tensor_tensor(both, hot[:, 0], hot[:, 1], ALU.add).then_inc(both_ready, 1)

            def weights():
                v.wait_ge(gap_exp, 1)
                link(v.tensor_scalar(wt[:, 0], gap, 1.0, None, ALU.add))
                link(v.reciprocal(wt[:, 0], wt[:, 0]))
                link(v.tensor_tensor(wt[:, 1], wt[:, 0], gap, ALU.mult))

            def sum_tiles():
                v.wait_ge(ranked, 1)
                link(v.tensor_copy(scan[:, 0], total))
                i, d = 0, 1
                while d < TILES:
                    link(v.tensor_copy(scan[:, 1 - i, 0:d], scan[:, i, 0:d]))
                    link(v.tensor_tensor(scan[:, 1 - i, d:], scan[:, i, d:], scan[:, i, 0:TILES - d], ALU.add))
                    i, d = 1 - i, 2 * d
                return i

            def whole_tiles(i):
                link(v.tensor_scalar(ends, scan[:, i, TILES - 1], float(P - 1), None, ALU.add))
                link(v.tensor_copy(count_i, ends))
                link(v.tensor_scalar(count_i, count_i, P.bit_length() - 1, None, ALU.arith_shift_right))
                link(v.tensor_copy(ends, count_i))
                link(v.memset(start, 0.0))
                for e in range(1, E):
                    link(v.tensor_tensor(start[:, e:e + 1], start[:, e - 1:e], ends[:, e - 1:e], ALU.add))
                link(v.tensor_tensor(ends, start, ends, ALU.add))
                link(v.tensor_scalar(start, start, float(P), None, ALU.mult))

            def find_places(i):
                link(v.tensor_tensor(pos, scan[:, i], total, ALU.subtract))
                link(v.tensor_tensor(pos, pos, rank, ALU.add))
                link(v.tensor_tensor(pos, pos, start.unsqueeze(1).to_broadcast([P, TILES, E]), ALU.add))
                for j in range(TOPK):
                    link(v.tensor_tensor(hot[:, j], hot[:, j], pos, ALU.mult))
                    link(v.tensor_reduce(place[:, j * TILES:(j + 1) * TILES], hot[:, j], AX.X, ALU.add))

            def split_places():
                flat = "p j t -> p (j t)"
                link(v.tensor_copy(place_i, place))
                link(v.tensor_scalar(part_i, place_i, P - 1, None, ALU.bitwise_and))
                link(v.tensor_copy(lane_of[:].rearrange(flat), part_i))
                link(v.tensor_scalar(part_i, place_i, P.bit_length() - 1, None, ALU.arith_shift_right))
                link(v.tensor_copy(tile_of[:].rearrange(flat), part_i))
                link(v.tensor_scalar(place, place, float(FIRST * P), None, ALU.add))
                link(v.tensor_copy(sb["row"][:].rearrange(flat), place))

            def tiles_experts():
                v.wait_ge(consts, 5)
                link(v.tensor_tensor(later, unit[:].unsqueeze(2).to_broadcast([P, SLOT_TILES, E - 1]),
                                     ends[:, 0:E - 1].unsqueeze(1).to_broadcast([P, SLOT_TILES, E - 1]), ALU.is_ge))
                link(v.tensor_reduce(eid, later, AX.X, ALU.add))
                link(v.memset(sb["eid"][:], E))
                link(v.tensor_copy(sb["eid"][:, FIRST:FIRST + SLOT_TILES], eid))

            def one_hot_tiles():
                n = TOPK * TILES // 4
                for i in range(0, TOPK * TILES, n):
                    at = tile_of[:].rearrange("p j t -> p (j t)")[:, i:i + n]
                    v.tensor_tensor(tiles_no[:, i:i + n, :], unit[:].unsqueeze(1).to_broadcast([P, n, SLOT_TILES]),
                                    at.unsqueeze(2).to_broadcast([P, n, SLOT_TILES]),
                                    ALU.is_equal).then_inc(tiles_ready, 1)

            def one_hot_lanes(j):
                n = TILES // 4
                for t in range(0, TILES, n):
                    v.tensor_tensor(lanes[:, j * TILES + t:j * TILES + t + n, :],
                                    lane[:].unsqueeze(1).to_broadcast([P, n, P]),
                                    lane_of[:, j, t:t + n].unsqueeze(2).to_broadcast([P, n, P]),
                                    ALU.is_equal).then_inc(lanes_ready, 1)

            def times_tile():
                v.wait_ge(own_ready, TOPK)
                for j in range(TOPK):
                    part = tiles_no[:, j * TILES:(j + 1) * TILES, :]
                    v.tensor_tensor(part, part, tile_no[:].unsqueeze(2).to_broadcast([P, TILES, SLOT_TILES]),
                                    ALU.mult).then_inc(tiles_ready, 1)

            def dispatch(r, s):
                u = r * STEPS5 + s
                if u == 0:
                    best_scores()
                if u == 1:
                    best_experts()
                if u == 2:
                    chosen()
                if u == 4:
                    sum_tiles()
                if u == 5:
                    weights()
                    whole_tiles(SCANNED)
                if u == 6:
                    find_places(SCANNED)
                if u == 7:
                    split_places()
                    tiles_experts()
                if u == 8:
                    one_hot_tiles()
                if u in (9, 10):
                    one_hot_lanes(u - 9)
                if u == 11:
                    times_tile()
                if u == 13:
                    v.wait_ge(ids_psum, 1)
                    link(v.tensor_scalar(ids_part[:], DP[:, 1, 0:SLOT_TILES], float(P), None, ALU.mult))
                    link(v.tensor_tensor(ids_part[:], ids_part[:], DP[:, 0, 0:SLOT_TILES], ALU.add))
                    v.tensor_copy(ids[:], ids_part[:]).then_inc(ids_ready, 1)
            pipelined(v, SLOTS, STEPS5, [(1, gate), (3, take_y), (0, dispatch)], peel=SLOTS, drain=False)
            pipelined(v, LAST, STEPS5, [(1, gate), (3, take_y)], start=SLOTS, drain=False)

            x4 = sb["x"][:].rearrange("p (g t) d -> p g t d", t=G)
            sl = [Link(v, stats_link[i], 3) for i in range(2)]
            nl = [Link(v, norm_link[i], 4) for i in range(2)]
            for i in range(2):
                v.memset(tm[i][:], 0.0).then_inc(summed[i], 1)

            def sums(kind, unit):
                def stage(r, s):
                    if s != unit or early(r):
                        return
                    c = r - LAST
                    g = c + kind * (GROUPS // 2)
                    link = sl[kind]
                    link.start(c)
                    if kind == 0:
                        v.wait_ge(shared_in, 16 * (c + 1))
                    else:
                        v.wait_ge(y_out, r * STEPS5 + unit + 1)
                    v.wait_ge(routed_in[kind], 16 * TOPK * G * (c + 1))
                    for t in range(G):
                        ins = v.scalar_tensor_tensor(moe[kind][:, t, :], got[kind][:, 0, t, :],
                                                     sb["wt"][:, 0, bass.ds(g * G + t, 1)], shared[kind][:, t, :],
                                                     ALU.mult, ALU.add)
                    link(ins)
                    for t in range(G):
                        ins = v.scalar_tensor_tensor(moe[kind][:, t, :], got[kind][:, 1, t, :],
                                                     sb["wt"][:, 1, bass.ds(g * G + t, 1)], moe[kind][:, t, :],
                                                     ALU.mult, ALU.add)
                    ins.then_inc(summed[kind], 1)
                    v.wait_ge(summed[kind], c + 2)
                    settle(v, sb["tick"])
                    for t in range(G):
                        ins = v.bn_stats(bn[kind][:, t, :], moe[kind][:, t, :])
                    link(ins)
                    settle(v, sb["tick"])
                    for t in range(G):
                        ins = v.bn_aggr(mv[kind][:, t, :], bn[kind][:, t, :])
                    link(ins)
                    v.tensor_scalar(ve[kind][:], mv[kind][:, :, 1], EPS, None, ALU.add).then_inc(var6[kind], 1)
                return stage

            def norm(kind, unit):
                def stage(r, s):
                    if s != unit or early(r):
                        return
                    c = r - LAST
                    g = c + kind * (GROUPS // 2)
                    link = nl[kind]
                    link.start(c)
                    v.wait_ge(root6[kind], c + 1)
                    y, t1 = rs[kind], tm[kind]
                    link(v.reciprocal(y[:], root[kind][:]))
                    link(v.tensor_tensor(t1[:], y[:], y[:], ALU.mult))
                    link(v.tensor_tensor(t1[:], t1[:], ve[kind][:], ALU.mult))
                    link(v.tensor_scalar(t1[:], t1[:], -0.5, 1.5, ALU.mult, ALU.add))
                    v.tensor_tensor(y[:], y[:], t1[:], ALU.mult).then_inc(rs_ready[kind], 1)
                    v.wait_ge(rs_ready[kind], c + 1)
                    for t in range(G):
                        ins = v.tensor_scalar(moe[kind][:, t, :], moe[kind][:, t, :], mv[kind][:, t, 0:1],
                                              y[:, t:t + 1], ALU.subtract, ALU.mult)
                    ins.then_inc(scaled[kind], 1)
                    v.wait_ge(scaled[kind], c + 1)
                    v.tensor_tensor(x4[:, g], x4[:, g], moe[kind], ALU.add).then_inc(out_ready[kind], 1)
                return stage

            pipelined(v, ROUNDS, STEPS5, [(1, gate), (4, sums(1, 3)), (3, take_shared), (5, sums(0, 0)),
                                          (7, norm(0, 0)), (6, norm(1, 3))], start=LAST, peel=2)


def build(nc, dr):
    with ExitStack() as ctx:
        def sbuf(name, shape, dt):
            return ctx.enter_context(nc.sbuf_tensor(name, shape, dt))
        dr["QT"] = nc.dram_tensor("QT", (3 * D, T), BF16, kind="Internal").ap()
        dr["KT"] = nc.dram_tensor("KT", (2 * D, T), F16, kind="Internal").ap()
        dr["VD"] = nc.dram_tensor("VD", (P, GROUPS1, H, G1 * VW), BF16, kind="Internal").ap()
        dr["VF"] = nc.dram_tensor("VF", (P, GROUPS1, H, G1 * VU), F32, kind="Internal").ap()
        dr["XN"] = nc.dram_tensor("XN", (T, D), F32, kind="Internal").ap()
        dr["YS"] = nc.dram_tensor("YS", ((FIRST + SLOT_TILES) * P, D), F32, kind="Internal").ap()
        dr["SH"] = nc.dram_tensor("SH", (SROWS, B * H, S), BF16, kind="Internal").ap()
        sb = {
            "x": sbuf("x", [P, TILES, D], F32),
            "wproj": sbuf("wproj", [P, KD, D], F32),
            "rw": sbuf("rw", [E, D], F32),
            "rwT": sbuf("rwT", [P, KD, E], F32),
            "rbias": sbuf("rbias", [P, E], F32),
            "ident": sbuf("ident", [P, P], F32),
            "ident_b": sbuf("ident_b", [P, P], BF16),
            "sel": sbuf("sel", [P, 2 * VU], F32),
            "iota8": sbuf("iota8", [P, E], F32),
            "z": sbuf("z", [P, TILES, E], F32),
            "wt": sbuf("wt", [P, TOPK, TILES], F32),
            "row": sbuf("row", [P, TOPK, TILES], U32),
            "eid": sbuf("eid", [P, UNITS], I32),
            "guard": sbuf("guard", [P, 1], F32),
            "tick": sbuf("tick", [P, 1], F32),
            "tick_pool": sbuf("tick_pool", [P, 2], F32),
        }
        with ExitStack() as early:
            def esb(name, shape, dt):
                return early.enter_context(nc.sbuf_tensor(name, shape, dt))
            sb["wqkv"] = esb("wqkv", [P, KD, 3 * D], F32)
            sb["gb"] = esb("gb", [P, 4, DH], F32)
            sb["sums"] = esb("sums", [P, 32], F32)
            sb["spread"] = esb("spread", [P, 2 * KD, P], F32)
            sb["mv"] = esb("mv", [P, TILES, 2], F32)
            sb["rs"] = esb("rs", [P, TILES], F32)
            setup(nc, dr, sb)
            project_qkv(nc, dr, sb)
        safe = int(np.float32(SAFE).view(np.int32))
        bound = nc.values_load(sb["guard"][0:1, 0:1].bitcast(I32))
        with ExitStack() as around:
            sems = [around.enter_context(nc.semaphore(name)) for name in MAXIMA_SEMS]
            with nc.If(bound > safe):
                true_maxima(nc, dr, sb, sems)
        sb["O"] = sbuf("O", [P, B * H * 2, 2, QC // P, VU], F32)
        attention(nc, dr, sb)
        sb["W1"] = sbuf("W1", [P, E + 1, KD, HID], F32)
        sb["W3"] = sbuf("W3", [P, E + 1, KD, HID], F32)
        project_and_route(nc, dr, sb)
        sb["W2"] = sbuf("W2", [P, E + 1, HID // P, D], F32)
        experts(nc, dr, sb)


_INS = ["L0_attn_x", "L0_attn_w_qkv", "L0_attn_w_proj", "L0_attn_q_gamma", "L0_attn_q_beta", "L0_attn_k_gamma",
        "L0_attn_k_beta", "L0_ffn_router_w", "L0_ffn_experts_bias", "L0_ffn_w1", "L0_ffn_w3", "L0_ffn_w2",
        "L0_ffn_sw1", "L0_ffn_sw3", "L0_ffn_sw2"]


def kernel(**inputs):
    import numpy as np
    import concourse.bacc as bacc
    from concourse.bass_utils import run_bass_kernel_spmd

    nc = bacc.Bacc("TRN2", target_bir_lowering=False, num_devices=1)
    arrays, dr = {}, {}
    for name in _INS:
        a = np.ascontiguousarray(inputs[name])
        arrays[f"in_{name}"] = a
        short = name.replace("L0_attn_", "").replace("L0_ffn_", "")
        dr[short] = nc.dram_tensor(f"in_{name}", a.shape, mybir.dt.from_np(a.dtype), kind="ExternalInput").ap()
    dr["out"] = nc.dram_tensor("out_0", (B, S, D), F32, kind="ExternalOutput").ap()
    build(nc, dr)
    r = run_bass_kernel_spmd(nc, [arrays], core_ids=[0])
    return r.results[0]["out_0"]
```
